# Optimizing a Trainium2 kernel written in Bass

```python
import numpy as np
import jax
import jax.numpy as jnp

def _softmax(x, axis=-1):
    return jax.nn.softmax(x, axis=axis)

def _gelu(x):
    return jax.nn.gelu(x, approximate=True)

def _silu(x):
    return jax.nn.silu(x)

def _sigmoid(x):
    return jax.nn.sigmoid(x)

def _layernorm(x, axis=-1, eps=1e-05):
    m = jnp.mean(x, axis=axis, keepdims=True)
    v = jnp.var(x, axis=axis, keepdims=True)
    return (x - m) / jnp.sqrt(v + eps)

def _scatter_add(tgt, idx, src, axis=0):
    return tgt.at[idx].add(src)

def _segment_sum(src, seg, n):
    return jax.ops.segment_sum(src, seg, n)
kernel_name = 'mk_audio_tower_d1_tok_audfeat256_r4_8f0d27'

def setup_inputs(seed: int=0):
    np.random.seed(seed)
    _w = jnp.asarray

    def _rec_inputs():
        import jax
        import jax.numpy as jnp
        _rk = jax.random.key(seed)
        x = -0.00197248 + 1.00072 * jax.random.normal(jax.random.fold_in(_rk, 1), (64, 1, 10240), jnp.float32)
        return x
    x = _rec_inputs()

    def _L0_tok_setup():
        import jax, jax.numpy as jnp
        import numpy as np
        B, L = (4, 10240)
        C = 128
        DMLP = 512
        TEMP = 1e-05
        EPS = 1e-05
        FACTOR = 2

        def _conv(x, w, b, stride, pad):
            x = jnp.pad(x, ((0, 0), (0, 0), (pad, pad)), mode='reflect')
            y = jax.lax.conv_general_dilated(x, w, (stride,), 'VALID', dimension_numbers=('NCH', 'OIH', 'NCH'))
            return y + b[None, :, None]

        def _cnorm(x, g, b):
            m = jnp.mean(x, axis=1, keepdims=True)
            v = jnp.var(x, axis=1, keepdims=True, ddof=1)
            return (x - m) * jax.lax.rsqrt(v + EPS) * g[None, :, None] + b[None, :, None]

        def _forward(x, conv0_w, conv0_b, conv1_w, conv1_b, conv2_w, conv2_b, conv3_w, conv3_b, n0_w, n0_b, n1_w, n1_b, n2_w, n2_b, n3_w, n3_b, n4_w, n4_b, mlp_w1, mlp_b1, mlp_w2, mlp_b2, mlp_w3, mlp_b3):
            h = jax.nn.relu(_cnorm(_conv(x, conv0_w, conv0_b, 5, 3), n0_w, n0_b))
            h = jax.nn.relu(_cnorm(_conv(h, conv1_w, conv1_b, 4, 2), n1_w, n1_b))
            h = jax.nn.relu(_cnorm(_conv(h, conv2_w, conv2_b, 2, 1), n2_w, n2_b))
            h = jax.nn.relu(_cnorm(_conv(h, conv3_w, conv3_b, 2, 1), n3_w, n3_b))
            f = jnp.transpose(h, (0, 2, 1))
            T = f.shape[1]
            z = jax.nn.gelu(f @ mlp_w1 + mlp_b1, approximate=False)
            z = jax.nn.gelu(z @ mlp_w2 + mlp_b2, approximate=False)
            imp = jax.nn.sigmoid((z @ mlp_w3 + mlp_b3)[..., 0]) + TEMP
            imp = imp / jnp.sum(imp, axis=1, keepdims=True) * (T / FACTOR)
            Tn = T // FACTOR
            cs = jnp.cumsum(imp, axis=1)
            p = jnp.maximum(cs[:, :, None] - jnp.arange(Tn, dtype=cs.dtype)[None, None, :], 0.0)
            pc = jnp.pad(p, ((0, 0), (0, 0), (0, 1)))
            d = pc[:, :, :-1] - pc[:, :, 1:]
            wmat = d - jnp.pad(d, ((0, 0), (1, 0), (0, 0)))[:, :-1, :]
            pooled = jnp.einsum('btn,btc->bnc', wmat, f)
            out = jnp.transpose(pooled, (0, 2, 1))
            return jax.nn.relu(_cnorm(out, n4_w, n4_b))
        key = jax.random.key(seed)
        ks = jax.random.split(key, 8)

        def w(k, shape, fan_in):
            return jax.random.normal(k, shape, jnp.float32) / np.float32(np.sqrt(fan_in))
        inp = {'x': jax.random.normal(ks[0], (B, 1, L), jnp.float32), 'conv0_w': w(ks[1], (C, 1, 10), 10), 'conv0_b': jnp.zeros(C, jnp.float32), 'conv1_w': w(ks[2], (C, C, 8), C * 8), 'conv1_b': jnp.zeros(C, jnp.float32), 'conv2_w': w(ks[3], (C, C, 4), C * 4), 'conv2_b': jnp.zeros(C, jnp.float32), 'conv3_w': w(ks[4], (C, C, 4), C * 4), 'conv3_b': jnp.zeros(C, jnp.float32), 'mlp_w1': w(ks[5], (C, DMLP), C), 'mlp_b1': jnp.zeros(DMLP, jnp.float32), 'mlp_w2': w(ks[6], (DMLP, DMLP), DMLP), 'mlp_b2': jnp.zeros(DMLP, jnp.float32), 'mlp_w3': w(ks[7], (DMLP, 1), DMLP), 'mlp_b3': jnp.zeros(1, jnp.float32)}
        for i in range(5):
            inp[f'n{i}_w'] = jnp.ones(C, jnp.float32)
            inp[f'n{i}_b'] = jnp.zeros(C, jnp.float32)
        return inp
    _L0_tok_all = _L0_tok_setup()
    _L0_tok_in = {k: v for k, v in _L0_tok_all.items() if k in ('conv0_w', 'conv0_b', 'conv1_w', 'conv1_b', 'conv2_w', 'conv2_b', 'conv3_w', 'conv3_b', 'n0_w', 'n0_b', 'n1_w', 'n1_b', 'n2_w', 'n2_b', 'n3_w', 'n3_b', 'n4_w', 'n4_b', 'mlp_w1', 'mlp_b1', 'mlp_w2', 'mlp_b2', 'mlp_w3', 'mlp_b3')}
    del _L0_tok_all

    def _L0_attn_setup():
        import jax, jax.numpy as jnp
        import numpy as np
        from math import sqrt
        DIM = 64
        key = jax.random.key(seed)
        k1, k2, k3, k4 = jax.random.split(key, 4)
        B, T, D, H, R = (2, 1024, DIM, 8, 32)

        def xavier(k, shape, fan_in, fan_out):
            a = sqrt(6.0 / (fan_in + fan_out))
            return jax.random.uniform(k, shape, jnp.float32, -a, a)
        x = jax.random.normal(k1, (B, T, D), jnp.float32)
        Q = xavier(k2, (H, R, D), D, R)
        K = xavier(k3, (H, R, D), D, R)
        VO = xavier(k4, (H, D, D), D, D)
        return {'x': x, 'Q': Q, 'K': K, 'VO': VO}
    _L0_attn_all = _L0_attn_setup()
    _L0_attn_in = {k: v for k, v in _L0_attn_all.items() if k in ('Q', 'K', 'VO')}
    del _L0_attn_all

    def _L0_ffn_setup():
        import jax, jax.numpy as jnp
        import numpy as np
        B, S, H, NH, NE = (4, 256, 64, 4, 4)
        D = H // NH
        EPS = 1e-08

        def layernorm(x, g, b):
            m = jnp.mean(x, axis=-1, keepdims=True)
            v = jnp.mean((x - m) ** 2, axis=-1, keepdims=True)
            return (x - m) / jnp.sqrt(v + EPS) * g + b
        key = jax.random.key(seed)
        ks = jax.random.split(key, 18)
        sc = 0.05
        return {'x': jax.random.normal(ks[0], (B, S, H), jnp.float32), 'hl_w': jax.random.normal(ks[1], (NH, D, H), jnp.float32) * sc, 'hl_b': jax.random.normal(ks[2], (NH, D), jnp.float32) * sc, 'wq': jax.random.normal(ks[3], (NH, NE, D, D), jnp.float32) * sc, 'wk': jax.random.normal(ks[4], (NH, D, D), jnp.float32) * sc, 'wv': jax.random.normal(ks[5], (NH, D, D), jnp.float32) * sc, 'gate_w': jax.random.normal(ks[6], (NH, NE, NE * D), jnp.float32) * sc, 'gate_b': jax.random.normal(ks[7], (NH, NE), jnp.float32) * sc, 'ln_g': jnp.ones((D,), jnp.float32), 'ln_b': jnp.zeros((D,), jnp.float32), 'fc1_w': jax.random.normal(ks[8], (D, D), jnp.float32) * sc, 'fc1_b': jax.random.normal(ks[9], (D,), jnp.float32) * sc, 'fc2_w': jax.random.normal(ks[10], (D, D), jnp.float32) * sc, 'fc2_b': jax.random.normal(ks[11], (D,), jnp.float32) * sc, 'fnorm_g': jnp.ones((D,), jnp.float32), 'fnorm_b': jnp.zeros((D,), jnp.float32), 'fgate_w': jax.random.normal(ks[12], (NH, H), jnp.float32) * sc}
    _L0_ffn_all = _L0_ffn_setup()
    _L0_ffn_in = {k: v for k, v in _L0_ffn_all.items() if k in ('hl_w', 'hl_b', 'wq', 'wk', 'wv', 'gate_w', 'gate_b', 'ln_g', 'ln_b', 'fc1_w', 'fc1_b', 'fc2_w', 'fc2_b', 'fnorm_g', 'fnorm_b', 'fgate_w')}
    del _L0_ffn_all
    return {'x': x, 'L0_tok_conv0_w': _L0_tok_in['conv0_w'], 'L0_tok_conv0_b': _L0_tok_in['conv0_b'], 'L0_tok_conv1_w': _L0_tok_in['conv1_w'], 'L0_tok_conv1_b': _L0_tok_in['conv1_b'], 'L0_tok_conv2_w': _L0_tok_in['conv2_w'], 'L0_tok_conv2_b': _L0_tok_in['conv2_b'], 'L0_tok_conv3_w': _L0_tok_in['conv3_w'], 'L0_tok_conv3_b': _L0_tok_in['conv3_b'], 'L0_tok_n0_w': _L0_tok_in['n0_w'], 'L0_tok_n0_b': _L0_tok_in['n0_b'], 'L0_tok_n1_w': _L0_tok_in['n1_w'], 'L0_tok_n1_b': _L0_tok_in['n1_b'], 'L0_tok_n2_w': _L0_tok_in['n2_w'], 'L0_tok_n2_b': _L0_tok_in['n2_b'], 'L0_tok_n3_w': _L0_tok_in['n3_w'], 'L0_tok_n3_b': _L0_tok_in['n3_b'], 'L0_tok_n4_w': _L0_tok_in['n4_w'], 'L0_tok_n4_b': _L0_tok_in['n4_b'], 'L0_tok_mlp_w1': _L0_tok_in['mlp_w1'], 'L0_tok_mlp_b1': _L0_tok_in['mlp_b1'], 'L0_tok_mlp_w2': _L0_tok_in['mlp_w2'], 'L0_tok_mlp_b2': _L0_tok_in['mlp_b2'], 'L0_tok_mlp_w3': _L0_tok_in['mlp_w3'], 'L0_tok_mlp_b3': _L0_tok_in['mlp_b3'], 'L0_attn_Q': _L0_attn_in['Q'], 'L0_attn_K': _L0_attn_in['K'], 'L0_attn_VO': _L0_attn_in['VO'], 'L0_ffn_hl_w': _L0_ffn_in['hl_w'], 'L0_ffn_hl_b': _L0_ffn_in['hl_b'], 'L0_ffn_wq': _L0_ffn_in['wq'], 'L0_ffn_wk': _L0_ffn_in['wk'], 'L0_ffn_wv': _L0_ffn_in['wv'], 'L0_ffn_gate_w': _L0_ffn_in['gate_w'], 'L0_ffn_gate_b': _L0_ffn_in['gate_b'], 'L0_ffn_ln_g': _L0_ffn_in['ln_g'], 'L0_ffn_ln_b': _L0_ffn_in['ln_b'], 'L0_ffn_fc1_w': _L0_ffn_in['fc1_w'], 'L0_ffn_fc1_b': _L0_ffn_in['fc1_b'], 'L0_ffn_fc2_w': _L0_ffn_in['fc2_w'], 'L0_ffn_fc2_b': _L0_ffn_in['fc2_b'], 'L0_ffn_fnorm_g': _L0_ffn_in['fnorm_g'], 'L0_ffn_fnorm_b': _L0_ffn_in['fnorm_b'], 'L0_ffn_fgate_w': _L0_ffn_in['fgate_w']}

def reference(x, L0_tok_conv0_w, L0_tok_conv0_b, L0_tok_conv1_w, L0_tok_conv1_b, L0_tok_conv2_w, L0_tok_conv2_b, L0_tok_conv3_w, L0_tok_conv3_b, L0_tok_n0_w, L0_tok_n0_b, L0_tok_n1_w, L0_tok_n1_b, L0_tok_n2_w, L0_tok_n2_b, L0_tok_n3_w, L0_tok_n3_b, L0_tok_n4_w, L0_tok_n4_b, L0_tok_mlp_w1, L0_tok_mlp_b1, L0_tok_mlp_w2, L0_tok_mlp_b2, L0_tok_mlp_w3, L0_tok_mlp_b3, L0_attn_Q, L0_attn_K, L0_attn_VO, L0_ffn_hl_w, L0_ffn_hl_b, L0_ffn_wq, L0_ffn_wk, L0_ffn_wv, L0_ffn_gate_w, L0_ffn_gate_b, L0_ffn_ln_g, L0_ffn_ln_b, L0_ffn_fc1_w, L0_ffn_fc1_b, L0_ffn_fc2_w, L0_ffn_fc2_b, L0_ffn_fnorm_g, L0_ffn_fnorm_b, L0_ffn_fgate_w):
    import jax
    import jax.numpy as jnp

    def _L0_tok_ref(x, conv0_w, conv0_b, conv1_w, conv1_b, conv2_w, conv2_b, conv3_w, conv3_b, n0_w, n0_b, n1_w, n1_b, n2_w, n2_b, n3_w, n3_b, n4_w, n4_b, mlp_w1, mlp_b1, mlp_w2, mlp_b2, mlp_w3, mlp_b3):
        import jax, jax.numpy as jnp
        import numpy as np
        B, L = (4, 10240)
        C = 128
        DMLP = 512
        TEMP = 1e-05
        EPS = 1e-05
        FACTOR = 2

        def _conv(x, w, b, stride, pad):
            x = jnp.pad(x, ((0, 0), (0, 0), (pad, pad)), mode='reflect')
            y = jax.lax.conv_general_dilated(x, w, (stride,), 'VALID', dimension_numbers=('NCH', 'OIH', 'NCH'))
            return y + b[None, :, None]

        def _cnorm(x, g, b):
            m = jnp.mean(x, axis=1, keepdims=True)
            v = jnp.var(x, axis=1, keepdims=True, ddof=1)
            return (x - m) * jax.lax.rsqrt(v + EPS) * g[None, :, None] + b[None, :, None]

        def _forward(x, conv0_w, conv0_b, conv1_w, conv1_b, conv2_w, conv2_b, conv3_w, conv3_b, n0_w, n0_b, n1_w, n1_b, n2_w, n2_b, n3_w, n3_b, n4_w, n4_b, mlp_w1, mlp_b1, mlp_w2, mlp_b2, mlp_w3, mlp_b3):
            h = jax.nn.relu(_cnorm(_conv(x, conv0_w, conv0_b, 5, 3), n0_w, n0_b))
            h = jax.nn.relu(_cnorm(_conv(h, conv1_w, conv1_b, 4, 2), n1_w, n1_b))
            h = jax.nn.relu(_cnorm(_conv(h, conv2_w, conv2_b, 2, 1), n2_w, n2_b))
            h = jax.nn.relu(_cnorm(_conv(h, conv3_w, conv3_b, 2, 1), n3_w, n3_b))
            f = jnp.transpose(h, (0, 2, 1))
            T = f.shape[1]
            z = jax.nn.gelu(f @ mlp_w1 + mlp_b1, approximate=False)
            z = jax.nn.gelu(z @ mlp_w2 + mlp_b2, approximate=False)
            imp = jax.nn.sigmoid((z @ mlp_w3 + mlp_b3)[..., 0]) + TEMP
            imp = imp / jnp.sum(imp, axis=1, keepdims=True) * (T / FACTOR)
            Tn = T // FACTOR
            cs = jnp.cumsum(imp, axis=1)
            p = jnp.maximum(cs[:, :, None] - jnp.arange(Tn, dtype=cs.dtype)[None, None, :], 0.0)
            pc = jnp.pad(p, ((0, 0), (0, 0), (0, 1)))
            d = pc[:, :, :-1] - pc[:, :, 1:]
            wmat = d - jnp.pad(d, ((0, 0), (1, 0), (0, 0)))[:, :-1, :]
            pooled = jnp.einsum('btn,btc->bnc', wmat, f)
            out = jnp.transpose(pooled, (0, 2, 1))
            return jax.nn.relu(_cnorm(out, n4_w, n4_b))
        return _forward(x, conv0_w, conv0_b, conv1_w, conv1_b, conv2_w, conv2_b, conv3_w, conv3_b, n0_w, n0_b, n1_w, n1_b, n2_w, n2_b, n3_w, n3_b, n4_w, n4_b, mlp_w1, mlp_b1, mlp_w2, mlp_b2, mlp_w3, mlp_b3)

    def _L0_attn_ref(x, Q, K, VO):
        import jax, jax.numpy as jnp
        import numpy as np
        from math import sqrt
        DIM = 64
        d = x.shape[-1]
        q = jnp.einsum('btd,hrd->bhtr', x, Q)
        k = jnp.einsum('bud,hrd->bhur', x, K)
        scores = jnp.einsum('bhtr,bhur->bhtu', q, k) / sqrt(d)
        attn = jax.nn.softmax(scores, axis=-1)
        ctx = jnp.einsum('bhtu,bud->bhtd', attn, x)
        out = jnp.einsum('bhtd,hde->bte', ctx, VO)
        return out

    def _L0_ffn_ref(x, hl_w, hl_b, wq, wk, wv, gate_w, gate_b, ln_g, ln_b, fc1_w, fc1_b, fc2_w, fc2_b, fnorm_g, fnorm_b, fgate_w):
        import jax, jax.numpy as jnp
        import numpy as np
        B, S, H, NH, NE = (4, 256, 64, 4, 4)
        D = H // NH
        EPS = 1e-08

        def layernorm(x, g, b):
            m = jnp.mean(x, axis=-1, keepdims=True)
            v = jnp.mean((x - m) ** 2, axis=-1, keepdims=True)
            return (x - m) / jnp.sqrt(v + EPS) * g + b
        b, s, h = x.shape
        nh, d, _ = wk.shape
        ne = wq.shape[1]
        sx = jnp.einsum('bsh,ndh->bnsd', x, hl_w) + hl_b[None, :, None, :]
        pad = sx == 0
        q = jnp.einsum('bnsd,neod->bneso', sx, wq)
        k = jnp.einsum('bnsd,nod->bnso', sx, wk)
        v = jnp.einsum('bnsd,nod->bnso', sx, wv)
        causal = jnp.where(jnp.tril(jnp.ones((s, s), bool)), 0.0, -jnp.inf).astype(x.dtype)
        scores = jnp.einsum('bnesd,bntd->bnest', q, k) * d ** 0.5 + causal
        att = jax.nn.softmax(scores, axis=-1)
        qkv = jnp.einsum('bnest,bntd->bnesd', att, v)
        qkv = jnp.where(pad[:, :, None], 0.0, qkv)
        out = jnp.transpose(qkv, (0, 1, 3, 2, 4)).reshape(b, nh, s, ne * d)
        gs = jax.nn.softmax(jnp.einsum('bnsf,nef->bnse', out, gate_w) + gate_b[None, :, None, :], axis=-1)
        mixed = jnp.einsum('bnsed,bnse->bnsd', out.reshape(b, nh, s, ne, d), gs)
        resid = sx[jnp.arange(nh), jnp.arange(nh)]
        hn = layernorm(mixed + resid, ln_g, ln_b)
        f_n = jnp.transpose(hn, (0, 2, 1, 3)).reshape(b, s, h)
        fx = f_n.reshape(b, s, nh, d)
        pm = fx == 0
        hx = jnp.where(pm, 0.0, fx @ fc1_w.T + fc1_b)
        hx = jax.nn.relu(hx)
        hx = jnp.where(pm, 0.0, hx @ fc2_w.T + fc2_b)
        hx = layernorm(hx + fx, fnorm_g, fnorm_b)
        fout = hx.reshape(b, s, h)
        fg = jax.nn.softmax(fout @ fgate_w.T, axis=-1)
        return (fout.reshape(b, s, nh, d) * fg[..., None]).reshape(b, s, h)
    h = _L0_tok_ref(x, L0_tok_conv0_w, L0_tok_conv0_b, L0_tok_conv1_w, L0_tok_conv1_b, L0_tok_conv2_w, L0_tok_conv2_b, L0_tok_conv3_w, L0_tok_conv3_b, L0_tok_n0_w, L0_tok_n0_b, L0_tok_n1_w, L0_tok_n1_b, L0_tok_n2_w, L0_tok_n2_b, L0_tok_n3_w, L0_tok_n3_b, L0_tok_n4_w, L0_tok_n4_b, L0_tok_mlp_w1, L0_tok_mlp_b1, L0_tok_mlp_w2, L0_tok_mlp_b2, L0_tok_mlp_w3, L0_tok_mlp_b3)
    h = h + _L0_attn_ref(_layernorm(h, axis=-1), L0_attn_Q, L0_attn_K, L0_attn_VO)
    h = h + _L0_ffn_ref(_layernorm(h, axis=-1), L0_ffn_hl_w, L0_ffn_hl_b, L0_ffn_wq, L0_ffn_wk, L0_ffn_wv, L0_ffn_gate_w, L0_ffn_gate_b, L0_ffn_ln_g, L0_ffn_ln_b, L0_ffn_fc1_w, L0_ffn_fc1_b, L0_ffn_fc2_w, L0_ffn_fc2_b, L0_ffn_fnorm_g, L0_ffn_fnorm_b, L0_ffn_fgate_w)
    return h

_drawn_inputs = setup_inputs


def setup_inputs(seed=0):
    import zlib

    import numpy as np

    out = dict(_drawn_inputs(seed))
    spreads = {'L0_tok_conv0_b': (0.0, 0.1),
     'L0_tok_conv1_b': (0.0, 0.1),
     'L0_tok_conv2_b': (0.0, 0.1),
     'L0_tok_conv3_b': (0.0, 0.1),
     'L0_tok_n0_w': (1.0, 0.2),
     'L0_tok_n0_b': (0.0, 0.1),
     'L0_tok_n1_w': (1.0, 0.2),
     'L0_tok_n1_b': (0.0, 0.1),
     'L0_tok_n2_w': (1.0, 0.2),
     'L0_tok_n2_b': (0.0, 0.1),
     'L0_tok_n3_w': (1.0, 0.2),
     'L0_tok_n3_b': (0.0, 0.1),
     'L0_tok_n4_w': (1.0, 0.2),
     'L0_tok_n4_b': (0.0, 0.1),
     'L0_tok_mlp_b1': (0.0, 0.1),
     'L0_tok_mlp_b2': (0.0, 0.1),
     'L0_ffn_ln_g': (1.0, 0.2),
     'L0_ffn_ln_b': (0.0, 0.319),
     'L0_ffn_fnorm_g': (1.0, 0.2),
     'L0_ffn_fnorm_b': (0.0, 0.314)}
    factors = {'L0_ffn_wq': 8.0,
     'L0_ffn_wk': 8.0,
     'L0_ffn_gate_w': 64.0,
     'L0_ffn_gate_b': 55.717,
     'L0_ffn_fc1_w': 8.0,
     'L0_ffn_fc1_b': 8.0,
     'L0_ffn_fc2_w': 5.817,
     'L0_ffn_fc2_b': 2.983}
    for name, (base, spread) in spreads.items():
        noise = np.random.default_rng([zlib.crc32(name.encode()), seed]).standard_normal(out[name].shape)
        drawn = base * np.exp(spread * noise) if base else spread * noise
        out[name] = jnp.asarray(drawn.astype(out[name].dtype))
    for name, factor in factors.items():
        out[name] = (out[name] * factor).astype(out[name].dtype)
    return out
```

```python
from contextlib import ExitStack

import numpy as np

import concourse.bass as bass
from concourse import mybir

F32 = mybir.dt.float32
BF16 = mybir.dt.bfloat16
ALU = mybir.AluOpType
ACT = mybir.ActivationFunctionType
AX = mybir.AxisListType

P = 128
B = 64
C = 128
BANK = 512
EPS = 1e-5

K0, S0, PAD0, L0 = 10, 5, 3, 2048
K1, S1, PAD1, L1 = 8, 4, 2, 512
K2, S2, PAD2, L2 = 4, 2, 1, 256
K3, S3, PAD3, L3 = 4, 2, 1, 128
T = L3
TN = T // 2
G = 4
NGRP = B // G
WIN = K0 + 1
QUAD = 32
NQ = P // QUAD
JW = 2 * NQ
CH0 = L0 // JW
GX = G * CH0




def ge(eng, sem, value):
    if not isinstance(value, int) or value > 0:
        eng.wait_ge(sem, value)


def mark(eng, sem):
    eng.sem_inc(sem, 1)


def steps(eng, n, lag, per, body):
    rounds = n // per
    head = -(-(lag + 2) // per)
    if rounds - 1 - head < 2:
        head = rounds - 1
    for j in range(head * per):
        body(j // per, j % per, lambda s: j >= s)
    if head < rounds - 1:
        with eng.Fori(head, rounds - 1) as it:
            for r in range(per):
                body(it, r, lambda s: True)
    for j in range(n - per, n + lag):
        body(j // per, j % per, lambda s: 0 <= j - s < n)


def conv_phase(nc, sem, d, feat):
    with ExitStack() as ph:
        def tmp(name, shape, dt=F32):
            return ph.enter_context(nc.sbuf_tensor("cv_" + name, shape, dt))

        xw = [tmp(f"xw{i}", [P, GX]) for i in range(2)]
        prod = tmp("prod", [P, GX])
        rx = tmp("rx", [P, GX])
        w0 = tmp("w0", [P, 2, C])
        w0sum = tmp("w0sum", [P, C])
        w0T = tmp("w0T", [C, P])
        n0w = tmp("n0w", [P, C])
        wmask = tmp("wmask", [P, P])
        gram = tmp("gram", [P, P])
        vmask = tmp("vmask", [P, P])
        ones = tmp("ones", [P, P])
        onesm = tmp("onesm", [P, P])
        ident = tmp("ident", [P, P])
        epsc = tmp("epsc", [P, 1])
        w1 = tmp("w1", [P, K1, C])
        w2 = tmp("w2", [P, K2, C])
        w3 = tmp("w3", [P, K3, C])
        wmean = tmp("wmean", [P, 18])
        cols = tmp("cols", [P, 10])
        bc = tmp("bc", [P, 3])
        h0 = [tmp(f"h0_{i}", [P, G, L0 + 2 * PAD1]) for i in range(2)]
        h1 = tmp("h1", [P, G, L1 + 2 * PAD2])
        h2 = tmp("h2", [P, G, L2 + 2 * PAD3])
        sq = [tmp(f"sq{i}", [P, BANK]) for i in range(2)]
        dev = [tmp(f"dev{i}", [P, BANK]) for i in range(2)]
        yn = [tmp(f"yn{i}", [P, BANK]) for i in range(2)]
        pa = ph.enter_context(nc.psum_tensor("pa", [P, NQ, BANK], F32))
        pc = ph.enter_context(nc.psum_tensor("pc", [P, 2, BANK], F32))
        pv = ph.enter_context(nc.psum_tensor("pv", [P, 2, BANK], F32))

        s_wts, s_x = sem("s_wts"), sem("s_x")
        s_prep = sem("s_prep")
        s_pprep = sem("s_pprep")
        s_a0 = sem("s_a0")
        s_a0free = sem("s_a0free")
        s_halo0 = sem("s_halo0")
        s_z, s_zused = sem("s_z"), sem("s_zused")
        s_r, s_rdev, s_xn = sem("s_r"), sem("s_rdev"), sem("s_xn")
        s_tile = sem("s_tile")
        s_sq, s_var, s_dev = sem("s_sq"), sem("s_var"), sem("s_dev")
        s_rec, s_norm, s_relu = sem("s_rec"), sem("s_norm"), sem("s_relu")
        s_halo = sem("s_halo")
        s_rx = sem("s_rx")
        s_poolmark = sem("s_poolmark")

        TILES = [("c1", 0), ("c2", 1), ("c1", 1), ("c1", 2), ("c3", 0), ("c1", 3), ("c2", 0)]
        SETS = {0: 0, 2: 1, 3: 2, 5: 3}
        Z_AT, R_AT = 1, 4

        def slots(i0, last=False):
            if last:
                return [(0, "c2", 1), (1, "c3", 0)]
            return [(t, k, a) for t, (k, a) in enumerate(TILES)
                    if not (i0 and (k, a) in (("c2", 1), ("c3", 0)))]

        def n_of(i, t, i0, last=False):
            if last:
                return 7 * NGRP - 1 + t
            if i0:
                return {0: 1, 2: 2, 3: 3, 5: 4, 6: 5}[t]
            return i * 7 + (t - 1)

        def bank_of(u, t, i0, last=False):
            if last:
                return (7 * NGRP - 2 + t) % 2
            if i0:
                return ({0: 1, 2: 2, 3: 3, 5: 4, 6: 5}[t] - 1) % 2
            return (7 * u + t - 2) % 2

        def halo_count(i, kind, part, i0):
            if kind == "c2" and part == 0:
                return 2 if i0 else i * 6 + 2
            if kind == "c2":
                return i * 6 - 2
            return i * 6 + 1

        HALOS = {0: ("h1", 0), 1: ("h2", 1), 2: ("h1", 1), 3: ("h1", 2), 5: ("h1", 3), 6: ("h2", 0)}

        def halo_done(i, t, i0, last=False):
            if last:
                return NGRP * 6
            if i0:
                return {0: 1, 2: 2, 3: 3, 5: 4, 6: 5}[t]
            return i * 6 + {0: 0, 1: 1, 2: 2, 3: 3, 5: 4, 6: 5}[t]

        block = ph.enter_context(nc.Block())

        @block.sync
        def _(sp):
            sp.dma_start(w0[:, :, :], d["w0"]).then_inc(s_wts, 16)
            sp.dma_start(wmask[:, :], d["wmask"]).then_inc(s_wts, 16)
            sp.dma_start(ident[:, :], d["ident"]).then_inc(s_wts, 16)
            sp.dma_start(cols[:, :], d["cols"]).then_inc(s_wts, 16)
            sp.dma_start(n0w[:, :], d["n0w"].partition_broadcast(P)).then_inc(s_wts, 16)
            for i in range(2):
                sp.dma_start(xw[i][:, :], d["x"][:, i, :]).then_inc(s_x, 16)
            sp.dma_start(w1[:, :, :], d["w1"]).then_inc(s_wts, 16)
            sp.dma_start(w2[:, :, :], d["w2"]).then_inc(s_wts, 16)
            sp.dma_start(w3[:, :, :], d["w3"]).then_inc(s_wts, 16)
            with sp.Fori(0, NGRP // 2 - 1) as pair:
                for u in range(2):
                    sp.wait_ge(s_a0, pair * 32 + 16 * (u + 1))
                    sp.dma_start(xw[u][:, :], d["x"][:, bass.ds(pair * 2 + (u + 2), 1), :].rearrange("p a n -> p (a n)")).then_inc(s_x, 16)

        @block.gpsimd
        def _(pool):
            def edges0(i, u):
                pool.wait_ge(s_a0free, (i + 1) * 16)
                mark(pool, s_poolmark)
                h = h0[u % 2]
                e = L0 + 2 * PAD1
                pool.tensor_copy(h[:, :, 0:1], h[:, :, 4:5]).then_inc(s_halo0, 1)
                pool.tensor_copy(h[:, :, 1:2], h[:, :, 3:4]).then_inc(s_halo0, 1)
                pool.tensor_copy(h[:, :, e - 2:e - 1], h[:, :, e - 4:e - 3]).then_inc(s_halo0, 1)
                pool.tensor_copy(h[:, :, e - 1:e], h[:, :, e - 5:e - 4]).then_inc(s_halo0, 1)

            def edges(i, t, i0, last=False):
                if last:
                    which, part = "h2", 1
                else:
                    which, part = HALOS[t]
                pool.wait_ge(s_relu, n_of(i, t, i0, last))
                mark(pool, s_poolmark)
                if which == "h1":
                    v, e = h1[:, part:part + 1, :], L1 + 2 * PAD2
                else:
                    v, e = h2[:, 2 * part:2 * part + 2, :], L2 + 2 * PAD3
                pool.tensor_copy(v[:, :, 0:1], v[:, :, 2:3])
                pool.tensor_copy(v[:, :, e - 1:e], v[:, :, e - 3:e - 2]).then_inc(s_halo, 1)

            def body(i, u, i0=False, more=True):
                for t, kind, part in slots(i0):
                    if kind != "c3":
                        edges(i, t, i0)
                    if t == 3 and more:
                        edges0(i + 1, u + 1)
            edges0(0, 0)
            body(0, 0, i0=True)
            body(1, 1)
            with pool.Fori(1, NGRP // 2 - 1) as pair:
                for u in range(2):
                    body(pair * 2 + u, u)
            body(NGRP - 2, 0)
            body(NGRP - 1, 1, more=False)
            edges(NGRP, 0, False, last=True)

        @block.tensor
        def _(pe):
            pe.wait_ge(s_prep, 4)
            pe.transpose(pa[:, 0, 0:P], w0sum[:, :], ident[:, :]).then_inc(s_pprep, 1)
            pe.wait_ge(s_prep, 5)
            pe.matmul(pa[:, 1, 0:P], w0T[:, :], w0T[:, :], start=True, stop=True).then_inc(s_pprep, 1)
            pe.matmul(pa[:, 2, 0:3], onesm[:, :], cols[:, 0:3], start=True, stop=True).then_inc(s_pprep, 1)

            def stat_z(i, u, after_set):
                pe.wait_ge(s_x, (i + 1) * 16)
                if after_set is not None:
                    pe.wait_ge(s_a0free, after_set)
                for hf in range(2):
                    m = pe.matmul(pa[:, hf, :], gram[:, :], xw[u % 2][:, hf * BANK:(hf + 1) * BANK], start=True, stop=True)
                m.then_inc(s_z, 1)

            def stat_r(i, u, after_set):
                pe.wait_ge(s_zused, i + 1)
                if after_set is not None:
                    pe.wait_ge(s_a0free, after_set)
                for hf in range(2):
                    m = pe.matmul(pa[:, hf, :], vmask[:, :], prod[:, hf * BANK:(hf + 1) * BANK], start=True, stop=True)
                m.then_inc(s_r, 1)

            def conv0(i, u, s):
                if s == 0:
                    pe.wait_ge(s_xn, i + 1)
                if s or not isinstance(i, int) or i:
                    pe.wait_ge(s_a0free, i * 16 + 4 * s)
                for q in range(NQ):
                    r = slice(QUAD * q, QUAD * q + QUAD)
                    pe.matmul(pa[:, q, :], w0[r, s % 2, :], xw[u % 2][r, (s // 2) * BANK:(s // 2 + 1) * BANK],
                              start=True, stop=True).then_inc(s_a0, 1)

            def var(n, b):
                pe.wait_ge(s_sq, n)
                if not isinstance(n, int) or n > 2:
                    pe.wait_ge(s_dev, n - 2)
                pe.matmul(pv[:, b, :], ones[:, :], sq[b][:, :], start=True, stop=True).then_inc(s_var, 1)

            def tile(i, u, t, kind, part, i0, last=False):
                n, b = n_of(i, t, i0, last), bank_of(u, t, i0, last)
                if not isinstance(n, int) or n > 2:
                    pe.wait_ge(s_norm, n - 2)
                if kind == "c1":
                    if part == 0:
                        pe.wait_ge(s_halo0, (i + 1) * 4)
                    w, taps = w1, K1
                    src = [h0[u % 2][:, part, k:k + S1 * (L1 - 1) + 1:S1] for k in range(K1)]
                elif kind == "c2":
                    pe.wait_ge(s_halo, halo_count(i, kind, part, i0))
                    w, taps = w2, K2
                    src = [h1[:, 2 * part:2 * part + 2, k:k + S2 * (L2 - 1) + 1:S2] for k in range(K2)]
                else:
                    pe.wait_ge(s_halo, NGRP * 6 if last else halo_count(i, kind, part, i0))
                    w, taps = w3, K3
                    src = [h2[:, :, k:k + S3 * (L3 - 1) + 1:S3] for k in range(K3)]
                for k in range(taps):
                    m = pe.matmul(pc[:, b, :], w[:, k, :], src[k], start=(k == 0), stop=(k == taps - 1))
                m.then_inc(s_tile, 1)

            def body(i, u, i0=False, more=True, more2=True):
                for t, kind, part in slots(i0):
                    if t in SETS and more:
                        if t == 2 and more2:
                            pe.wait_ge(s_zused, i + 3)
                        if t == 5 and more2:
                            pe.wait_ge(s_rdev, i + 3)
                        conv0(i + 1, u + 1, SETS[t])
                    tile(i, u, t, kind, part, i0)
                    n, b = n_of(i, t, i0), bank_of(u, t, i0)
                    if not isinstance(n, int) or n > 1:
                        var(n - 1, 1 - b)
                    if more2:
                        if t == (Z_AT if not i0 else 0):
                            stat_z(i + 2, u, (i + 1) * 16 + 4)
                        if t == (R_AT if not i0 else 3):
                            stat_r(i + 2, u, (i + 1) * 16 + 12)

            pe.wait_ge(s_prep, 10)
            stat_z(0, 0, None)
            stat_r(0, 0, None)
            pe.wait_ge(s_rdev, 1)
            stat_z(1, 1, None)
            stat_r(1, 1, None)
            pe.wait_ge(s_rdev, 2)
            for s in range(4):
                conv0(0, 0, s)
            body(0, 0, i0=True)
            body(1, 1)
            with pe.Fori(1, NGRP // 2 - 1) as pair:
                for u in range(2):
                    body(pair * 2 + u, u)
            body(NGRP - 2, 0, more2=False)
            body(NGRP - 1, 1, more=False, more2=False)
            n, b = n_of(NGRP, 0, False, True), bank_of(0, 0, False, True)
            tile(NGRP, 0, 0, "c2", 1, False, last=True)
            var(n - 1, 1 - b)
            var(n, b)
            tile(NGRP, 0, 1, "c3", 0, False, last=True)
            var(n + 1, 1 - b)

        @block.scalar
        def _(act):
            cb = {"c1": (4, 5), "c2": (6, 7), "c3": (8, 9)}
            bias = {"c1": 0, "c2": 1, "c3": 2}

            def dev_x(i):
                act.wait_ge(s_r, i + 1)
                if not isinstance(i, int) or i > 0:
                    act.wait_ge(s_xn, i)
                act.activation(rx[:, :].rearrange("p (a n) -> p a n", a=2), pa[:, 0:2, :], ACT.Sqrt,
                               bias=epsc[:, 0:1]).then_inc(s_rdev, 1)

            def take0(i, u, s):
                if s == 0 and (not isinstance(i, int) or i >= 2):
                    act.wait_ge(s_tile, i * 7 - 10)
                for q in range(NQ):
                    j = 2 * q + s % 2 + PAD1
                    act.wait_ge(s_a0, i * 16 + (4 * s + q + 1))
                    dst = h0[u % 2][:, 2 * (s // 2):2 * (s // 2) + 2, j:j + JW * (CH0 - 1) + 1:JW]
                    act.activation(dst, pa[:, q, :].rearrange("p (b n) -> p b n", b=2), ACT.Relu,
                                   bias=cols[:, 3:4]).then_inc(s_a0free, 1)

            def square(n, b, kind):
                act.wait_ge(s_tile, n)
                if not isinstance(n, int) or n > 2:
                    act.wait_ge(s_var, n - 2)
                act.activation(sq[b][:, :], pc[:, b, :], ACT.Square, bias=bc[:, bias[kind]:bias[kind] + 1]).then_inc(s_sq, 1)

            def deviation(n, b):
                act.wait_ge(s_var, n)
                if not isinstance(n, int) or n > 2:
                    act.wait_ge(s_norm, n - 2)
                act.activation(dev[b][:, :], pv[:, b, :], ACT.Sqrt, bias=epsc[:, 0:1]).then_inc(s_dev, 1)

            def relu(i, n, b, kind, part):
                act.wait_ge(s_norm, n)
                y = yn[b][:, :]
                if kind == "c1":
                    dst = h1[:, part, PAD2:PAD2 + L1]
                elif kind == "c2":
                    dst, y = h2[:, 2 * part:2 * part + 2, PAD3:PAD3 + L2], y.rearrange("p (b n) -> p b n", b=2)
                elif isinstance(i, int):
                    dst = feat[:, (i - 1) * G * T:i * G * T]
                else:
                    dst = feat[:, bass.ds((i - 1) * G * T, G * T)]
                g, s = cb[kind]
                act.activation(dst, y, ACT.Relu, bias=cols[:, s:s + 1], scale=cols[:, g:g + 1]).then_inc(s_relu, 1)

            def back(i, u, t, i0, k):
                sl = slots(i0)
                at = [x[0] for x in sl].index(t) - k
                n = n_of(i, t, i0) - k
                b = (bank_of(u, t, i0) + k) % 2
                if at >= 0:
                    return i, n, b, sl[at][1], sl[at][2]
                if i0:
                    return None
                return i - 1, n, b, TILES[at][0], TILES[at][1]

            def body(i, u, i0=False, more=True, more2=True):
                for t, kind, part in slots(i0):
                    two = back(i, u, t, i0, 2)
                    if two:
                        relu(*two)
                    if t in SETS and more:
                        take0(i + 1, u + 1, SETS[t])
                    n, b = n_of(i, t, i0), bank_of(u, t, i0)
                    square(n, b, kind)
                    if back(i, u, t, i0, 1):
                        deviation(n - 1, 1 - b)
                    if more2 and t == (R_AT if not i0 else 3):
                        dev_x(i + 2)

            act.wait_ge(s_prep, 10)
            dev_x(0)
            dev_x(1)
            for s in range(4):
                take0(0, 0, s)
            body(0, 0, i0=True)
            body(1, 1)
            with act.Fori(1, NGRP // 2 - 1) as pair:
                for u in range(2):
                    body(pair * 2 + u, u)
            body(NGRP - 2, 0, more2=False)
            body(NGRP - 1, 1, more=False, more2=False)
            n, b = n_of(NGRP, 0, False, True), bank_of(0, 0, False, True)
            relu(NGRP - 1, n - 2, b, *TILES[5])
            square(n, b, "c2")
            deviation(n - 1, 1 - b)
            relu(NGRP - 1, n - 1, 1 - b, *TILES[6])
            deviation(n, b)
            relu(NGRP, n, b, "c2", 1)
            square(n + 1, 1 - b, "c3")
            deviation(n + 1, 1 - b)
            relu(NGRP, n + 1, 1 - b, "c3", 0)

        @block.vector
        def _(dve):
            step = [0]

            def prep(ins):
                ins.then_inc(s_prep, 1)
                step[0] += 1
                dve.wait_ge(s_prep, step[0])

            dve.memset(ones[:, :], 1.0 / (C - 1))
            dve.memset(onesm[:, :], 1.0 / C)
            dve.memset(epsc[:, :], EPS)
            dve.wait_ge(s_wts, 8 * 16)
            prep(dve.tensor_reduce(wmean[:, 0:2], w0[:, :, :], AX.X, ALU.add))
            prep(dve.tensor_scalar(wmean[:, 0:2], wmean[:, 0:2], 1.0 / C, None, ALU.mult))
            prep(dve.tensor_tensor(w0[:, :, :], w0[:, :, :], wmean[:, 0:2].unsqueeze(2).broadcast_to((P, 2, C)), ALU.subtract))
            prep(dve.tensor_tensor(w0sum[:, :], w0[:, 0, :], w0[:, 1, :], ALU.add))
            dve.wait_ge(s_pprep, 1)
            prep(dve.tensor_copy(w0T[:, :], pa[:, 0, 0:P]))
            dve.wait_ge(s_pprep, 3)
            dve.tensor_tensor(gram[:, :], pa[:, 1, 0:P], wmask[:, :], ALU.mult)
            dve.tensor_scalar(vmask[:, :], wmask[:, :], 1.0 / (C - 1), None, ALU.mult)
            dve.tensor_tensor(bc[:, :], cols[:, 0:3], pa[:, 2, 0:3], ALU.subtract)
            prep(dve.tensor_tensor(w0[:, :, :], w0[:, :, :], n0w[:, :].unsqueeze(1).broadcast_to((P, 2, C)), ALU.mult))
            dve.tensor_reduce(wmean[:, 2:10], w1[:, :, :], AX.X, ALU.add)
            dve.tensor_reduce(wmean[:, 10:14], w2[:, :, :], AX.X, ALU.add)
            prep(dve.tensor_reduce(wmean[:, 14:18], w3[:, :, :], AX.X, ALU.add))
            prep(dve.tensor_scalar(wmean[:, 2:18], wmean[:, 2:18], 1.0 / C, None, ALU.mult))
            dve.tensor_tensor(w1[:, :, :], w1[:, :, :], wmean[:, 2:10].unsqueeze(2).broadcast_to((P, K1, C)), ALU.subtract)
            prep(dve.tensor_tensor(w2[:, :, :], w2[:, :, :], wmean[:, 10:14].unsqueeze(2).broadcast_to((P, K2, C)), ALU.subtract))
            prep(dve.tensor_tensor(w3[:, :, :], w3[:, :, :], wmean[:, 14:18].unsqueeze(2).broadcast_to((P, K3, C)), ALU.subtract))

            def products(i, u):
                dve.wait_ge(s_z, i + 1)
                dve.wait_ge(s_x, (i + 1) * 16)
                if not isinstance(i, int) or i > 0:
                    dve.wait_ge(s_r, i)
                dve.tensor_tensor(prod[:, :].rearrange("p (a n) -> p a n", a=2), pa[:, 0:2, :],
                                  xw[u % 2][:, :].rearrange("p (a n) -> p a n", a=2), ALU.mult).then_inc(s_zused, 1)

            def normalise_x(i, u):
                dve.wait_ge(s_rdev, i + 1)
                dve.reciprocal(rx[:, :], rx[:, :]).then_inc(s_rx, 1)
                dve.wait_ge(s_rx, i + 1)
                dve.tensor_tensor(xw[u % 2][:, :], xw[u % 2][:, :], rx[:, :], ALU.mult).then_inc(s_xn, 1)

            def norm(n, b, kind):
                dve.wait_ge(s_dev, n)
                dve.reciprocal(dev[b][:, :], dev[b][:, :]).then_inc(s_rec, 1)
                dve.wait_ge(s_rec, n)
                if not isinstance(n, int) or n > 2:
                    dve.wait_ge(s_relu, n - 2)
                k = {"c1": 0, "c2": 1, "c3": 2}[kind]
                dve.scalar_tensor_tensor(yn[b][:, :], pc[:, b, :], bc[:, k:k + 1], dev[b][:, :], ALU.add,
                                         ALU.mult).then_inc(s_norm, 1)

            def body(i, u, i0=False, more2=True):
                sl = slots(i0)
                for at, (t, kind, part) in enumerate(sl):
                    n, b = n_of(i, t, i0), bank_of(u, t, i0)
                    if at > 0:
                        norm(n - 1, 1 - b, sl[at - 1][1])
                    elif not i0:
                        norm(n - 1, 1 - b, TILES[-1][0])
                    if more2 and t == (Z_AT if not i0 else 0):
                        products(i + 2, u)
                    if more2 and t == (R_AT if not i0 else 3):
                        normalise_x(i + 2, u)

            products(0, 0)
            normalise_x(0, 0)
            products(1, 1)
            normalise_x(1, 1)
            body(0, 0, i0=True)
            body(1, 1)
            with dve.Fori(1, NGRP // 2 - 1) as pair:
                for u in range(2):
                    body(pair * 2 + u, u)
            body(NGRP - 2, 0, more2=False)
            body(NGRP - 1, 1, more2=False)
            n, b = n_of(NGRP, 0, False, True), bank_of(0, 0, False, True)
            norm(n - 1, 1 - b, "c2")
            norm(n, b, "c2")
            norm(n + 1, 1 - b, "c3")


def mlp_phase(nc, sem, d, feat, imp):
    DM = 512
    KT = DM // P
    NT = B * T // BANK
    BT = BANK // T
    with ExitStack() as ph:
        def tmp(name, shape, dt=F32):
            return ph.enter_context(nc.sbuf_tensor("ml_" + name, shape, dt))

        w1 = tmp("w1", [P, DM])
        w2 = tmp("w2", [P, KT, DM])
        w3 = tmp("w3", [P, KT])
        b12 = tmp("b12", [P, 2, KT])
        b3 = tmp("b3", [P, 1])
        z1 = [tmp(f"z1_{i}", [P, KT, BANK]) for i in range(2)]
        z2 = [tmp(f"z2_{i}", [P, KT, BANK]) for i in range(2)]
        p1 = ph.enter_context(nc.psum_tensor("ml_p1", [P, 2, BANK], F32))
        p2 = ph.enter_context(nc.psum_tensor("ml_p2", [P, KT, BANK], F32))
        p3 = ph.enter_context(nc.psum_tensor("ml_p3", [P, B], F32))
        s_wts = sem("ml_wts")
        s_m1, s_g1 = sem("ml_m1"), sem("ml_g1")
        s_m2, s_g2 = sem("ml_m2"), sem("ml_g2")
        s_m3, s_sig = sem("ml_m3"), sem("ml_sig")
        block = ph.enter_context(nc.Block())

        @block.sync
        def _(sp):
            sp.dma_start(w1[:, :], d["mlp_w1"]).then_inc(s_wts, 16)
            sp.dma_start(w2[:, :, :], d["mlp_w2"].rearrange("(k p) n -> p k n", p=P)).then_inc(s_wts, 16)
            sp.dma_start(w3[:, :], d["mlp_w3"]).then_inc(s_wts, 16)
            sp.dma_start(b12[:, :, :], d["mlp_b12"]).then_inc(s_wts, 16)
            sp.dma_start(b3[:, :], d["mlp_b3"].partition_broadcast(P)).then_inc(s_wts, 16)

        @block.tensor
        def _(pe):
            pe.wait_ge(s_wts, 5 * 16)

            def body(it, r, has):
                c = it * 2 + r
                if has(0):
                    for m in range(KT):
                        ge(pe, s_g1, c * KT + (m - 1))
                        rhs = feat[:, c * BANK:(c + 1) * BANK] if isinstance(c, int) else feat[:, bass.ds(c * BANK, BANK)]
                        pe.matmul(p1[:, m % 2, :], w1[:, m * P:(m + 1) * P], rhs, start=True, stop=True).then_inc(s_m1, 1)
                if has(2):
                    ge(pe, s_g2, (c - 1) * KT)
                    for q in range(BT):
                        col = (c - 2) * BT + q
                        out = p3[:, col:col + 1] if isinstance(col, int) else p3[:, bass.ds(col, 1)]
                        for k in range(KT):
                            m3 = pe.matmul(out, z2[r % 2][:, k, q * T:(q + 1) * T], w3[:, k:k + 1],
                                           start=(k == 0), stop=(k == KT - 1))
                    m3.then_inc(s_m3, 1)
                if has(1):
                    ge(pe, s_g1, c * KT)
                    for m in range(KT):
                        ge(pe, s_g2, (c - 2) * KT + (m + 1))
                        for k in range(KT):
                            m2 = pe.matmul(p2[:, m, :], w2[:, k, m * P:(m + 1) * P], z1[1 - r % 2][:, k, :],
                                           start=(k == 0), stop=(k == KT - 1))
                        m2.then_inc(s_m2, 1)
            steps(pe, NT, 2, 2, body)

        @block.scalar
        def _(act):
            act.wait_ge(s_wts, 5 * 16)

            def body(it, r, has):
                c = it * 2 + r
                for m in range(KT):
                    if has(0):
                        act.wait_ge(s_m1, c * KT + (m + 1))
                        if m == 0:
                            ge(act, s_m2, (c - 1) * KT)
                        act.activation(z1[r % 2][:, m, :], p1[:, m % 2, :], ACT.Gelu, bias=b12[:, 0, m:m + 1]).then_inc(s_g1, 1)
                for m in range(KT):
                    if has(1):
                        act.wait_ge(s_m2, (c - 1) * KT + (m + 1))
                        if m == 0:
                            ge(act, s_m3, c - 2)
                        act.activation(z2[1 - r % 2][:, m, :], p2[:, m, :], ACT.Gelu, bias=b12[:, 1, m:m + 1]).then_inc(s_g2, 1)
            steps(act, NT, 2, 2, body)
            act.wait_ge(s_m3, NT)
            act.activation(imp[:, :], p3[:, :], ACT.Sigmoid, bias=b3[:, 0:1]).then_inc(s_sig, 1)


def pool_phase(nc, sem, d, feat, imp, tok):
    NB = BANK // TN
    NT = B // NB
    with ExitStack() as ph:
        def tmp(name, shape, dt=F32):
            return ph.enter_context(nc.sbuf_tensor("po_" + name, shape, dt))

        ident, upto, before, centre = (tmp(n, [P, P]) for n in ("ident", "upto", "before", "centre"))
        onev, one = tmp("onev", [P, P]), tmp("one", [P, P])
        iota = tmp("iota", [P, TN + 1])
        gb = tmp("gb", [P, 2])
        epsc = tmp("epsc", [P, 1])
        rsum = tmp("rsum", [P, B])
        cs = tmp("cs", [P, 2, B])
        over = tmp("over", [P, B, TN + 1])
        share = tmp("share", [P, B, TN])
        wm = tmp("wm", [P, B, TN])
        fin = [tmp(f"fin{i}", [P, NB * T]) for i in range(2)]
        fT = [tmp(f"fT{i}", [P, NB * T]) for i in range(2)]
        pooled, sq, dev, yn = ([tmp(f"{n}{i}", [P, BANK]) for i in range(2)] for n in ("pooled", "sq", "dev", "yn"))
        pt = ph.enter_context(nc.psum_tensor("po_pt", [P, NB * T], F32))
        pp = ph.enter_context(nc.psum_tensor("po_pp", [P, BANK], F32))
        py = ph.enter_context(nc.psum_tensor("po_py", [P, 2, BANK], F32))
        pv = ph.enter_context(nc.psum_tensor("po_pv", [P, BANK], F32))
        s_wts, s_imp, s_sum = sem("po_wts"), sem("po_imp"), sem("po_sum")
        s_fin, s_t, s_fT = sem("po_fin"), sem("po_t"), sem("po_fT")
        s_pool, s_pooled, s_cen, s_sq = sem("po_pool"), sem("po_pooled"), sem("po_cen"), sem("po_sq")
        s_var, s_dev, s_rec, s_norm, s_relu = (sem("po_" + n) for n in ("var", "dev", "rec", "norm", "relu"))
        block = ph.enter_context(nc.Block())

        @block.sync
        def _(sp):
            for t, n in ((ident, "ident"), (upto, "upto"), (before, "before"), (centre, "centre"), (iota, "iota"), (gb, "n4")):
                sp.dma_start(t[:, :], d[n]).then_inc(s_wts, 16)

        @block.tensor
        def _(pe):
            pe.wait_ge(s_wts, 6 * 16)
            pe.wait_ge(s_imp, 1)
            pe.matmul(pv[:, 0:B], one[:, :], imp[:, :], start=True, stop=True).then_inc(s_sum, 1)
            pe.wait_ge(s_imp, 3)
            pe.matmul(pp[:, 0:B], upto[:, :], imp[:, :], start=True, stop=True)
            pe.matmul(pp[:, B:2 * B], before[:, :], imp[:, :], start=True, stop=True).then_inc(s_sum, 1)

            def body(it, r, has):
                j = it * 2 + r
                if has(0):
                    pe.wait_ge(s_fin, j + 1)
                    ge(pe, s_fT, j)
                    for q in range(NB):
                        m = pe.transpose(pt[:, q * T:(q + 1) * T], fin[r][:, q * T:(q + 1) * T], ident[:, :])
                    m.then_inc(s_t, 1)
                if has(1):
                    ge(pe, s_fT, j)
                    ge(pe, s_imp, 4)
                    ge(pe, s_pooled, j - 1)
                    for q in range(NB):
                        b = (j - 1) * NB + q
                        w = wm[:, b, :] if isinstance(b, int) else wm[:, bass.ds(b, 1), :].rearrange("p a n -> p (a n)")
                        m = pe.matmul(pp[:, q * TN:(q + 1) * TN], fT[1 - r][:, q * T:(q + 1) * T], w, start=True, stop=True)
                    m.then_inc(s_pool, 1)
                if has(2):
                    ge(pe, s_pooled, j - 1)
                    ge(pe, s_norm, j - 3)
                    pe.matmul(py[:, r, :], centre[:, :], pooled[r][:, :], start=True, stop=True).then_inc(s_cen, 1)
                if has(3):
                    ge(pe, s_sq, j - 2)
                    ge(pe, s_dev, j - 3)
                    pe.matmul(pv[:, :], onev[:, :], sq[1 - r][:, :], start=True, stop=True).then_inc(s_var, 1)
            steps(pe, NT, 4, 2, body)

        @block.scalar
        def _(act):
            act.wait_ge(s_wts, 6 * 16)

            def body(it, r, has):
                j = it * 2 + r
                if has(4):
                    act.wait_ge(s_norm, j - 3)
                    v = (j - 4) * NB
                    dst = tok[:, v:v + NB, :] if isinstance(v, int) else tok[:, bass.ds(v, NB), :]
                    act.activation(dst, yn[r][:, :].rearrange("p (b n) -> p b n", n=TN), ACT.Relu, bias=gb[:, 1:2],
                                   scale=gb[:, 0:1]).then_inc(s_relu, 1)
                if has(0):
                    ge(act, s_t, j - 1)
                    v = j * NB * T
                    src = feat[:, v:v + NB * T] if isinstance(v, int) else feat[:, bass.ds(v, NB * T)]
                    act.activation(fin[r][:, :], src, ACT.Copy).then_inc(s_fin, 1)
                if has(2):
                    act.wait_ge(s_cen, j - 1)
                    ge(act, s_var, j - 3)
                    act.activation(sq[r][:, :], py[:, r, :], ACT.Square).then_inc(s_sq, 1)
                if has(3):
                    act.wait_ge(s_var, j - 2)
                    ge(act, s_norm, j - 4)
                    act.activation(dev[1 - r][:, :], pv[:, :], ACT.Sqrt, bias=epsc[:, 0:1]).then_inc(s_dev, 1)
            act.wait_ge(s_imp, 1)
            steps(act, NT, 4, 2, body)

        @block.vector
        def _(dve):
            dve.memset(onev[:, :], 1.0 / (C - 1))
            dve.memset(one[:, :], 1.0)
            dve.memset(epsc[:, :], EPS)
            dve.tensor_scalar(imp[:, :], imp[:, :], 1e-5, None, ALU.add).then_inc(s_imp, 1)
            dve.wait_ge(s_sum, 1)
            dve.reciprocal(rsum[:, :], pv[:, 0:B]).then_inc(s_imp, 1)
            dve.wait_ge(s_imp, 2)
            dve.scalar_tensor_tensor(imp[:, :], imp[:, :], float(TN), rsum[:, :], ALU.mult, ALU.mult).then_inc(s_imp, 1)
            dve.wait_ge(s_sum, 2)
            dve.wait_ge(s_wts, 6 * 16)
            dve.tensor_copy(cs[:, :, :], pp[:, 0:2 * B].rearrange("p (a b) -> p a b", a=2)).then_inc(s_rec, 1)
            dve.wait_ge(s_rec, 1)
            num = 1
            for a in range(2):
                def link(ins):
                    nonlocal num
                    num += 1
                    ins.then_inc(s_rec, 1)
                    dve.wait_ge(s_rec, num)
                link(dve.tensor_tensor(over[:, :, :], cs[:, a, :].unsqueeze(2).broadcast_to((P, B, TN + 1)),
                                       iota[:, :].unsqueeze(1).broadcast_to((P, B, TN + 1)), ALU.subtract))
                link(dve.tensor_scalar(over[:, :, :], over[:, :, :], 0.0, None, ALU.max))
                link(dve.memset(over[:, :, TN:TN + 1], 0.0))
                dst = share if a == 0 else wm
                link(dve.tensor_tensor(dst[:, :, :], over[:, :, 0:TN], over[:, :, 1:TN + 1], ALU.subtract))
            dve.tensor_tensor(wm[:, :, :], share[:, :, :], wm[:, :, :], ALU.subtract).then_inc(s_imp, 1)

            def body(it, r, has):
                j = it * 2 + r
                if has(0):
                    dve.wait_ge(s_t, j + 1)
                    ge(dve, s_pool, j - 1)
                    dve.tensor_copy(fT[r][:, :], pt[:, :]).then_inc(s_fT, 1)
                if has(1):
                    dve.wait_ge(s_pool, j)
                    ge(dve, s_cen, j - 2)
                    dve.tensor_copy(pooled[1 - r][:, :], pp[:, :]).then_inc(s_pooled, 1)
                if has(3):
                    dve.wait_ge(s_dev, j - 2)
                    dve.reciprocal(dev[1 - r][:, :], dev[1 - r][:, :]).then_inc(s_rec, 1)
                    dve.wait_ge(s_rec, j - 3 + (num + 1))
                    ge(dve, s_relu, j - 4)
                    dve.tensor_tensor(yn[1 - r][:, :], py[:, 1 - r, :], dev[1 - r][:, :], ALU.mult).then_inc(s_norm, 1)
            steps(dve, NT, 4, 2, body)


def layernorm(dve, act, s_v, s_a, count, x, out, work, stat, groups, width, eps):
    xv, ov, wv = x, out, work

    def bc(a):
        return a.unsqueeze(2).broadcast_to((P, groups, width))

    def vector():
        dve.tensor_reduce(stat[:, 0, 0:groups], xv, AX.X, ALU.add).then_inc(s_v, 1)
        dve.wait_ge(s_v, count + 1)
        dve.tensor_scalar(stat[:, 0, 0:groups], stat[:, 0, 0:groups], 1.0 / width, None, ALU.mult).then_inc(s_v, 1)
        dve.wait_ge(s_v, count + 2)
        dve.tensor_tensor(ov, xv, bc(stat[:, 0, 0:groups]), ALU.subtract).then_inc(s_v, 1)
        dve.wait_ge(s_a, count // 5 * 2 + 1)
        dve.tensor_reduce(stat[:, 1, 0:groups], wv, AX.X, ALU.add).then_inc(s_v, 1)
        dve.wait_ge(s_a, count // 5 * 2 + 2)
        dve.reciprocal(stat[:, 1, 0:groups], stat[:, 1, 0:groups]).then_inc(s_v, 1)
        dve.wait_ge(s_v, count + 5)
        return dve.tensor_tensor(ov, ov, bc(stat[:, 1, 0:groups]), ALU.mult)

    def scalar():
        act.wait_ge(s_v, count + 3)
        act.activation(wv, ov, ACT.Square).then_inc(s_a, 1)
        act.wait_ge(s_v, count + 4)
        act.activation(stat[:, 1, 0:groups], stat[:, 1, 0:groups], ACT.Sqrt, bias=eps, scale=1.0 / width).then_inc(s_a, 1)
    return vector, scalar


D = TN
H1, R1 = 8, 32
NH, NE, DH = 4, 4, 16


def norm_phase(nc, sem, name, tok, xn):
    with ExitStack() as ph:
        work = ph.enter_context(nc.sbuf_tensor(name + "_work", [P, B, D], F32))
        stat = ph.enter_context(nc.sbuf_tensor(name + "_stat", [P, 2, B], F32))
        epsc = ph.enter_context(nc.sbuf_tensor(name + "_eps", [P, 1], F32))
        s_v, s_a = sem(name + "_v"), sem(name + "_a")
        block = ph.enter_context(nc.Block())
        v, a = layernorm(nc.vector, nc.scalar, s_v, s_a, 0, tok[:, :, :], xn[:, :, 0:D], work[:, :, :], stat, B, D, epsc[:, 0:1])

        @block.vector
        def _(dve):
            dve.memset(epsc[:, :], EPS)
            if xn.shape[2] > D:
                dve.memset(xn[:, :, D:D + 1], 1.0)
            v().then_inc(s_v, 1)

        @block.scalar
        def _(act):
            a()


def attn_phase(nc, sem, d, xn, tok):
    GB = BANK // P
    NG = B // GB
    HG = H1 // 4
    SCALE = 1.0 / float(np.sqrt(D))
    with ExitStack() as ph:
        def tmp(name, shape, dt=F32):
            return ph.enter_context(nc.sbuf_tensor("at_" + name, shape, dt))

        def bank(name, shape):
            return ph.enter_context(nc.psum_tensor("at_" + name, shape, F32))

        ident = tmp("ident", [P, P])
        wqk = tmp("wqk", [D, 2 * HG, P])
        vo = tmp("vo", [P, 4, D])
        xs = tmp("xs", [P, GB, D])
        xT = tmp("xT", [D, BANK])
        qk = [tmp(f"qk{i}", [P, 2 * HG, BANK]) for i in range(2)]
        mx = tmp("mx", [P, 2, H1])
        ex = [tmp(f"ex{i}", [P, 4, HG, P]) for i in range(2)]
        exT = [tmp(f"exT{i}", [P, HG, 4, P]) for i in range(2)]
        rs = tmp("rs", [P, 2, H1])
        cx = [tmp(f"cx{i}", [P, H1, D]) for i in range(2)]
        cxT = tmp("cxT", [P, 4, P])
        pS = bank("pS", [P, 4, BANK])
        pT = bank("pT", [P, 4, P])
        pO = bank("pO", [P, HG, BANK])
        pM = bank("pM", [P, BANK])
        s_wts, s_xs, s_q, s_qev = (sem("at_" + n) for n in ("wts", "xs", "q", "qev"))
        s_pemark, s_poolmark = sem("at_pemark"), sem("at_poolmark")
        s_s, s_max, s_sub, s_exp = (sem("at_" + n) for n in ("s", "max", "sub", "exp"))
        s_t0, s_t1, s_ev0, s_ev1 = (sem("at_" + n) for n in ("t0", "t1", "ev0", "ev1"))
        s_pv, s_rs, s_ctx, s_ct, s_cev, s_pr, s_add = (sem("at_" + n) for n in ("pv", "rs", "ctx", "ct", "cev", "pr", "add"))
        PIECES = {0: (0, 1), 1: (2,), 2: (3,), 3: (4,)}
        DONE = {0: 0, 1: 2, 2: 3, 3: 4}
        block = ph.enter_context(nc.Block())

        def pieces_before(it, r):
            g = it * 2 + r // GB
            if isinstance(g, int) and g >= NG - 1:
                return 5 * NG
            return (g + 1) * 5 + DONE[r % GB]

        def more(it, r):
            g = it * 2 + r // GB
            return not isinstance(g, int) or g < NG - 1

        @block.sync
        def _(sp):
            sp.dma_start(ident[:, :], d["ident"]).then_inc(s_wts, 16)
            sp.dma_start(wqk[:, :, :], d["wqk"]).then_inc(s_wts, 16)
            sp.dma_start(vo[:, :, :], d["vo"]).then_inc(s_wts, 16)

        @block.gpsimd
        def _(pool):
            pool.tensor_copy(xs[:, :, :], xn[:, 0:GB, 0:D]).then_inc(s_xs, 1)
            with pool.Fori(1, NG) as g:
                pool.wait_ge(s_q, g * 5 - 4)
                mark(pool, s_poolmark)
                pool.tensor_copy(xs[:, :, :], xn[:, bass.ds(g * GB, GB), 0:D]).then_inc(s_xs, 1)

        @block.tensor
        def _(pe):
            pe.wait_ge(s_wts, 3 * 16)

            def piece(g, k):
                if k == 0:
                    pe.wait_ge(s_xs, g + 1)
                    mark(pe, s_pemark)
                    for b in range(GB):
                        m = pe.transpose(pM[0:D, b * P:(b + 1) * P], xs[:, b, :], ident[:, :])
                else:
                    pe.wait_ge(s_qev, g * 5 + k)
                    m = pe.matmul(pM[:, :], wqk[:, k - 1, :], xT[:, :], start=True, stop=True)
                m.then_inc(s_q, 1)

            for k in range(5):
                piece(0, k)

            def body(it, r, has):
                j, g, b4, gp = it * 8 + r, it * 2 + r // GB, r % GB, r // GB
                if has(0):
                    if b4 == 0:
                        pe.wait_ge(s_qev, (g + 1) * 5)
                    cols = slice(b4 * P, b4 * P + P)
                    for half in range(2):
                        ge(pe, s_sub, j * 2 + (half - 1))
                        for hg in range(HG):
                            for i in (2 * half, 2 * half + 1):
                                rows = slice(R1 * i, R1 * i + R1)
                                m = pe.matmul(pS[:, i, hg * P:(hg + 1) * P], qk[gp][rows, hg, cols],
                                              qk[gp][rows, HG + hg, cols], start=True, stop=True)
                        m.then_inc(s_s, 1)
                if has(1):
                    pe.wait_ge(s_exp, j)
                    ge(pe, s_ev1, j - 1)
                    for i in range(4):
                        m = pe.transpose(pT[:, i, :], ex[1 - r % 2][:, i, 0, :], ident[:, :])
                    m.then_inc(s_t0, 1)
                if has(3):
                    pe.wait_ge(s_ctx, j - 2)
                    pe.wait_ge(s_qev, pieces_before(it, r))
                    for k in range(4):
                        m = pe.transpose(pM[:, k * P:(k + 1) * P], cx[1 - r % 2][:, 2 * k:2 * k + 2, :].rearrange("p a n -> p (a n)"), ident[:, :])
                    m.then_inc(s_ct, 1)
                if has(0) and more(it, r):
                    ge(pe, s_cev, j - 2)
                    ge(pe, s_qev, pieces_before(it, r))
                    for k in PIECES[b4]:
                        piece(g + 1, k)
                if has(1):
                    pe.wait_ge(s_ev0, j)
                    for i in range(4):
                        m = pe.transpose(pT[:, i, :], ex[1 - r % 2][:, i, 1, :], ident[:, :])
                    m.then_inc(s_t1, 1)
                if has(2):
                    pe.wait_ge(s_ev0, j - 1)
                    pe.wait_ge(s_ev1, j - 1)
                    ge(pe, s_ctx, j - 2)
                    ge(pe, s_add, j - 3)
                    b = j - 2
                    rhs = xn[:, b, :] if isinstance(b, int) else xn[:, bass.ds(b, 1), :].rearrange("p a n -> p (a n)")
                    for hg in range(HG):
                        for i in range(4):
                            m = pe.matmul(pO[:, hg, i * (D + 1):(i + 1) * (D + 1)], exT[r % 2][:, hg, i, :], rhs,
                                          start=True, stop=True)
                    m.then_inc(s_pv, 1)
                if has(3):
                    pe.wait_ge(s_cev, j - 2)
                    ge(pe, s_add, j - 3)
                    for k in range(4):
                        m = pe.matmul(pO[:, 1, 320:320 + D], cxT[:, k, :], vo[:, k, :], start=(k == 0), stop=(k == 3))
                    m.then_inc(s_pr, 1)
            steps(pe, B, 3, 8, body)

        @block.scalar
        def _(act):
            def take(g, k, gp):
                act.wait_ge(s_q, g * 5 + (k + 1))
                if k == 0:
                    act.activation(xT[:, :], pM[0:D, :], ACT.Copy).then_inc(s_qev, 1)
                else:
                    act.activation(qk[gp][:, k - 1, :], pM[:, :], ACT.Copy).then_inc(s_qev, 1)

            for k in range(5):
                take(0, k, 0)

            def body(it, r, has):
                j, g, b4, gp = it * 8 + r, it * 2 + r // GB, r % GB, r // GB
                if has(1):
                    act.wait_ge(s_t0, j)
                    ge(act, s_pv, j - 2)
                    act.activation(exT[1 - r % 2][:, 0, :, :], pT[:, :, :], ACT.Copy).then_inc(s_ev0, 1)
                if has(3):
                    act.wait_ge(s_ct, j - 2)
                    ge(act, s_pr, j - 3)
                    act.activation(cxT[:, :, :], pM[:, :].rearrange("p (k t) -> p k t", k=4), ACT.Copy).then_inc(s_cev, 1)
                if has(0) and more(it, r):
                    for k in PIECES[b4]:
                        take(g + 1, k, 1 - gp)
                if has(0):
                    act.wait_ge(s_sub, j * 2 + 2)
                    act.activation(ex[r % 2][:, :, :, :], ex[r % 2][:, :, :, :], ACT.Exp, scale=SCALE).then_inc(s_exp, 1)
            steps(act, B, 3, 8, body)

        @block.vector
        def _(dve):
            def body(it, r, has):
                j = it * 8 + r
                if has(0):
                    for half in range(2):
                        i = slice(2 * half, 2 * half + 2)
                        dve.wait_ge(s_s, j * 2 + (half + 1))
                        sc = pS[:, i, 0:HG * P].rearrange("p i (h u) -> p i h u", h=HG)
                        m = mx[:, r % 2, 4 * half:4 * half + 4].rearrange("p (i h) -> p i h", i=2)
                        dve.tensor_reduce(m, sc, AX.X, ALU.max).then_inc(s_max, 1)
                        dve.wait_ge(s_max, j * 2 + (half + 1))
                        ge(dve, s_t1, j - 1)
                        dve.tensor_tensor(ex[r % 2][:, i, :, :], sc, m.unsqueeze(3).broadcast_to((P, 2, HG, P)),
                                          ALU.subtract).then_inc(s_sub, 1)
                if has(1):
                    dve.wait_ge(s_t1, j)
                    ge(dve, s_pv, j - 2)
                    dve.tensor_copy(exT[1 - r % 2][:, 1, :, :], pT[:, :, :]).then_inc(s_ev1, 1)
                if has(2):
                    dve.wait_ge(s_pv, j - 1)
                    ge(dve, s_pr, j - 2)
                    o = pO[:, :, 0:4 * (D + 1)].rearrange("p h (i e) -> p h i e", i=4)
                    q = rs[:, r % 2, :].rearrange("p (h i) -> p h i", h=HG)
                    dve.reciprocal(q, o[:, :, :, D:D + 1].rearrange("p h i e -> p h (i e)")).then_inc(s_rs, 1)
                    dve.wait_ge(s_rs, j - 1)
                    ge(dve, s_ct, j - 3)
                    dve.tensor_tensor(cx[r % 2][:, :, :].rearrange("p (h i) e -> p h i e", h=HG), o[:, :, :, 0:D],
                                      q.unsqueeze(3).broadcast_to((P, HG, 4, D)), ALU.mult).then_inc(s_ctx, 1)
                if has(3):
                    dve.wait_ge(s_pr, j - 2)
                    b = j - 3
                    t = tok[:, b, :] if isinstance(b, int) else tok[:, bass.ds(b, 1), :].rearrange("p a n -> p (a n)")
                    dve.tensor_tensor(t, t, pO[:, 1, 320:320 + D], ALU.add).then_inc(s_add, 1)
            steps(dve, B, 3, 8, body)


def mix_phase(nc, sem, d, xn, outs, logits, sxs):
    GB = BANK // P
    NG = B // GB
    QP = 7
    HOLD = 320
    SCALE = float(np.sqrt(DH))
    with ExitStack() as ph:
        def tmp(name, shape, dt=F32):
            return ph.enter_context(nc.sbuf_tensor("mx_" + name, shape, dt))

        def bank(name, shape):
            return ph.enter_context(nc.psum_tensor("mx_" + name, shape, F32))

        ident = tmp("ident", [P, P])
        identb = tmp("identb", [P, P], BF16)
        causal = tmp("causal", [P, P])
        causalb = tmp("causalb", [P, NE, P], BF16)
        hlw, hlbc, hlb = tmp("hlw", [D, D]), tmp("hlbc", [D, 1]), tmp("hlb", [P, D])
        wqk = tmp("wqk", [D, NE + 1, P])
        wv = tmp("wv", [D, D])
        gate, gateb = tmp("gate", [P, 2, NH * NE]), tmp("gateb", [P, NH * NE])
        xs = tmp("xs", [P, GB, D])
        xT = [tmp(f"xT{i}", [D, BANK]) for i in range(2)]
        sxT = [tmp(f"sxT{i}", [D, BANK]) for i in range(2)]
        qk = [tmp(f"qk{i}", [P, NE + 1, BANK]) for i in range(2)]
        v1 = [tmp(f"v1_{i}", [P, NH, DH + 1]) for i in range(2)]
        msk = [tmp(f"msk{i}", [P, NH, DH]) for i in range(2)]
        mx = tmp("mx", [P, NH, NE])
        ex = [tmp(f"ex{i}", [P, NH, NE, P]) for i in range(2)]
        exT = [tmp(f"exT{i}", [P, NH, NE, P]) for i in range(2)]
        rs = tmp("rs", [P, NH * NE])
        raw = tmp("raw", [P, NH * NE, DH])
        om = [tmp(f"om{i}", [P, NH, NE, DH]) for i in range(2)]
        oT = tmp("oT", [P, 2, P])
        pS = bank("pS", [P, NH, BANK])
        pT = bank("pT", [P, 2, NE, P])
        pO = bank("pO", [P, BANK])
        pM = bank("pM", [P, BANK])
        s_wts, s_prep, s_xs, s_q, s_qev = (sem("mx_" + n) for n in ("wts", "prep", "xs", "q", "qev"))
        s_s, s_max, s_sub, s_exp, s_t, s_ev = (sem("mx_" + n) for n in ("s", "max", "sub", "exp", "t", "ev"))
        s_sv, s_sx, s_svev, s_pv, s_rs, s_raw, s_om, s_oc = (sem("mx_" + n) for n in ("sv", "sx", "svev", "pv", "rs", "raw", "om", "oc"))
        s_pemark, s_poolmark = sem("mx_pemark"), sem("mx_poolmark")
        s_gt, s_gev, s_gl, s_lg = (sem("mx_" + n) for n in ("gt", "gev", "gl", "lg"))
        PIECES = {0: (0, 1), 1: (2, 3), 2: (4, 5), 3: (6,)}
        DONE = {0: 0, 1: 2, 2: 4, 3: 6}
        block = ph.enter_context(nc.Block())

        def pieces_before(it, r):
            g = it * 2 + r // GB
            if isinstance(g, int) and g >= NG - 1:
                return QP * NG
            return (g + 1) * QP + DONE[r % GB]

        def more(it, r):
            g = it * 2 + r // GB
            return not isinstance(g, int) or g < NG - 1

        def upto(v):
            return min(v, B) if isinstance(v, int) else v

        @block.sync
        def _(sp):
            for t, n in ((ident, "ident"), (causal, "causal"), (hlw, "hlw"), (hlbc, "hlb_col"), (wv, "ffv")):
                sp.dma_start(t[:, :], d[n]).then_inc(s_wts, 16)
            sp.dma_start(wqk[:, :, :], d["ffq"]).then_inc(s_wts, 16)
            sp.dma_start(gate[:, :, :], d["gate"]).then_inc(s_wts, 16)
            sp.dma_start(hlb[:, :], d["hlb"].partition_broadcast(P)).then_inc(s_wts, 16)
            sp.dma_start(gateb[:, :], d["gateb"].partition_broadcast(P)).then_inc(s_wts, 16)

        @block.gpsimd
        def _(pool):
            pool.tensor_copy(xs[:, :, :], xn[:, 0:GB, 0:D]).then_inc(s_xs, 1)

            def body(it, r, has):
                j, g = it * 8 + r, it * 2 + r // GB
                if has(0) and r % GB == 0 and more(it, r):
                    pool.wait_ge(s_q, g * QP + 1)
                    mark(pool, s_poolmark)
                    b = (g + 1) * GB
                    src = xn[:, b:b + GB, 0:D] if isinstance(b, int) else xn[:, bass.ds(b, GB), 0:D]
                    pool.tensor_copy(xs[:, :, :], src).then_inc(s_xs, 1)
                if has(2):
                    pool.wait_ge(s_om, j - 1)
                    mark(pool, s_poolmark)
                    b = j - 2
                    dst = outs[:, b:b + 1, :] if isinstance(b, int) else outs[:, bass.ds(b, 1), :]
                    pool.tensor_copy(dst, om[r % 2][:, :, :, :].rearrange("p n e d -> p (n e d)").unsqueeze(1)).then_inc(s_oc, 1)
            steps(pool, B, 3, 8, body)

        @block.tensor
        def _(pe):
            pe.wait_ge(s_wts, 9 * 16)
            pe.wait_ge(s_prep, 1)

            def piece(g, k, gp):
                if k == 0:
                    pe.wait_ge(s_xs, g + 1)
                    mark(pe, s_pemark)
                    for b in range(GB):
                        m = pe.transpose(pM[0:D, b * P:(b + 1) * P], xs[:, b, :], ident[:, :])
                else:
                    pe.wait_ge(s_qev, g * QP + k)
                    mark(pe, s_pemark)
                    if k == 1:
                        m = pe.matmul(pM[0:D, :], hlw[:, :], xT[gp][:, :], start=True, stop=True)
                    else:
                        m = pe.matmul(pM[:, :], wqk[:, k - 2, :], sxT[gp][:, :], start=True, stop=True)
                m.then_inc(s_q, 1)

            for k in range(QP):
                piece(0, k, 0)

            def body(it, r, has):
                j, g, b4, gp = it * 8 + r, it * 2 + r // GB, r % GB, r // GB
                cols = slice(b4 * P, b4 * P + P)
                if has(2):
                    pe.wait_ge(s_ev, (j - 1) * 4)
                    pe.wait_ge(s_svev, j - 1)
                    ge(pe, s_lg, j - 3)
                    ge(pe, s_om, j - 2)
                    for n in range(NH):
                        for e in range(NE):
                            at = (n * NE + e) * (DH + 1)
                            m = pe.matmul(pO[:, at:at + DH + 1], exT[r % 2][:, n, e, :], v1[r % 2][:, n, :],
                                          start=True, stop=True)
                    m.then_inc(s_pv, 1)
                for n in range(NH):
                    if has(0):
                        if b4 == 0 and n == 0:
                            pe.wait_ge(s_qev, (g + 1) * QP)
                        ge(pe, s_sub, j * 4 + (n - 3))
                        rows = slice(32 * n, 32 * n + DH)
                        pe.matmul(pS[:, n, :], identb[:, :], causalb[:, :, :].rearrange("p e u -> p (e u)"),
                                  start=True, stop=True)
                        for e in range(NE):
                            m = pe.matmul(pS[:, n, e * P:(e + 1) * P], qk[gp][rows, e, cols], qk[gp][rows, NE, cols],
                                          start=False, stop=True, skip_group_check=True)
                        m.then_inc(s_s, 1)
                    if has(1):
                        pe.wait_ge(s_exp, j * 4 + (n - 3))
                        ge(pe, s_ev, j * 4 + (n - 5))
                        for e in range(NE):
                            m = pe.transpose(pT[:, n % 2, e, :], ex[1 - r % 2][:, n, e, :], ident[:, :])
                        m.then_inc(s_t, 1)
                if has(0):
                    pe.wait_ge(s_qev, pieces_before(it, r))
                    ge(pe, s_gev, j - 3)
                    pe.matmul(pM[:, 0:D], xT[gp][:, cols], hlw[:, :], start=True, stop=True)
                    pe.matmul(pM[:, D:2 * D], sxT[gp][:, cols], wv[:, :], start=True, stop=True).then_inc(s_sv, 1)
                if has(3):
                    pe.wait_ge(s_om, j - 2)
                    pe.wait_ge(s_svev, upto(j + 1))
                    for k in range(2):
                        m = pe.transpose(pM[:, k * P:(k + 1) * P], om[1 - r % 2][:, 2 * k:2 * k + 2, :, :].rearrange("p n e d -> p (n e d)"), ident[:, :])
                    m.then_inc(s_gt, 1)
                if has(0) and more(it, r):
                    ge(pe, s_gev, j - 2)
                    pe.wait_ge(s_svev, j + 1)
                    for k in PIECES[b4]:
                        piece(g + 1, k, 1 - gp)
                if has(3):
                    pe.wait_ge(s_gev, j - 2)
                    pe.wait_ge(s_om, upto(j - 1))
                    ge(pe, s_lg, j - 3)
                    for k in range(2):
                        m = pe.matmul(pO[:, HOLD:HOLD + NH * NE], oT[:, k, :], gate[:, k, :], start=(k == 0), stop=(k == 1))
                    m.then_inc(s_gl, 1)
            steps(pe, B, 3, 8, body)

        @block.scalar
        def _(act):
            act.wait_ge(s_wts, 9 * 16)

            def take(g, k, gp):
                act.wait_ge(s_q, g * QP + (k + 1))
                if k == 0:
                    act.activation(xT[gp][:, :], pM[0:D, :], ACT.Copy).then_inc(s_qev, 1)
                elif k == 1:
                    act.activation(sxT[gp][:, :], pM[0:D, :], ACT.Identity, bias=hlbc[:, 0:1]).then_inc(s_qev, 1)
                else:
                    act.activation(qk[gp][:, k - 2, :], pM[:, :], ACT.Copy).then_inc(s_qev, 1)

            for k in range(QP):
                take(0, k, 0)

            def body(it, r, has):
                j, g, b4, gp = it * 8 + r, it * 2 + r // GB, r % GB, r // GB
                for n in range(NH):
                    if has(1):
                        act.wait_ge(s_t, j * 4 + (n - 3))
                        ge(act, s_pv, j - 2)
                        act.activation(exT[1 - r % 2][:, n, :, :], pT[:, n % 2, :, :], ACT.Copy).then_inc(s_ev, 1)
                    if has(0):
                        act.wait_ge(s_sub, j * 4 + (n + 1))
                        e = ex[r % 2][:, n, :, :]
                        act.activation(e, e, ACT.Exp, scale=SCALE).then_inc(s_exp, 1)
                if has(3):
                    act.wait_ge(s_gt, j - 2)
                    ge(act, s_gl, j - 3)
                    act.activation(oT[:, :, :], pM[:, 0:2 * P].rearrange("p (k t) -> p k t", k=2), ACT.Copy).then_inc(s_gev, 1)
                if has(0) and more(it, r):
                    for k in PIECES[b4]:
                        take(g + 1, k, 1 - gp)
            steps(act, B, 3, 8, body)

        @block.vector
        def _(dve):
            for i in range(2):
                dve.memset(v1[i][:, :, DH:DH + 1], 1.0)
            dve.wait_ge(s_wts, 9 * 16)
            dve.tensor_copy(identb[:, :], ident[:, :])
            dve.tensor_copy(causalb[:, :, :], causal[:, :].unsqueeze(1).broadcast_to((P, NE, P))).then_inc(s_prep, 1)

            def body(it, r, has):
                j = it * 8 + r
                if has(2):
                    dve.wait_ge(s_pv, j - 1)
                    o = pO[:, 0:NH * NE * (DH + 1)].rearrange("p (h e) -> p h e", h=NH * NE)
                    dve.reciprocal(rs[:, :], o[:, :, DH:DH + 1].rearrange("p h e -> p (h e)")).then_inc(s_rs, 1)
                    dve.wait_ge(s_rs, j - 1)
                    dve.tensor_tensor(raw[:, :, :], o[:, :, 0:DH], rs[:, :].unsqueeze(2).broadcast_to((P, NH * NE, DH)), ALU.mult).then_inc(s_raw, 1)
                    dve.wait_ge(s_raw, j - 1)
                    ge(dve, s_gt, j - 3)
                    ge(dve, s_oc, j - 3)
                    dve.tensor_tensor(om[r % 2][:, :, :, :], raw[:, :, :].rearrange("p (n e) d -> p n e d", n=NH),
                                      msk[r % 2][:, :, :].unsqueeze(2).broadcast_to((P, NH, NE, DH)), ALU.mult).then_inc(s_om, 1)
                for n in range(NH):
                    if has(0):
                        dve.wait_ge(s_s, j * 4 + (n + 1))
                        sc = pS[:, n, :].rearrange("p (e u) -> p e u", e=NE)
                        dve.tensor_reduce(mx[:, n, :], sc, AX.X, ALU.max).then_inc(s_max, 1)
                        dve.wait_ge(s_max, j * 4 + (n + 1))
                        ge(dve, s_t, j * 4 + (n - 7))
                        dve.tensor_tensor(ex[r % 2][:, n, :, :], sc, mx[:, n, :].unsqueeze(2).broadcast_to((P, NE, P)),
                                          ALU.subtract).then_inc(s_sub, 1)
                if has(0):
                    dve.wait_ge(s_sv, j + 1)
                    sx = sxs[:, j, :] if isinstance(j, int) else sxs[:, bass.ds(j, 1), :].rearrange("p a n -> p (a n)")
                    dve.tensor_tensor(sx, pM[:, 0:D], hlb[:, :], ALU.add).then_inc(s_sx, 1)
                    dve.tensor_copy(v1[r % 2][:, :, 0:DH], pM[:, D:2 * D].rearrange("p (n o) -> p n o", n=NH))
                    dve.wait_ge(s_sx, j + 1)
                    dve.tensor_scalar(msk[r % 2][:, :, :].rearrange("p n o -> p (n o)"), sx, 0.0, None, ALU.not_equal).then_inc(s_svev, 1)
                if has(3):
                    dve.wait_ge(s_gl, j - 2)
                    b = j - 3
                    lg = logits[:, b, :] if isinstance(b, int) else logits[:, bass.ds(b, 1), :].rearrange("p a n -> p (a n)")
                    dve.tensor_tensor(lg, pO[:, HOLD:HOLD + NH * NE], gateb[:, :], ALU.add).then_inc(s_lg, 1)
            steps(dve, B, 3, 8, body)


def gain_bias(x, g, b):
    shape = (P, B * NH, DH)
    v = x.rearrange("p b (n d) -> p (b n) d", d=DH)
    return (lambda dve: dve.tensor_tensor(v, v, g[:, :].unsqueeze(1).broadcast_to(shape), ALU.mult),
            lambda dve: dve.tensor_tensor(v, v, b[:, :].unsqueeze(1).broadcast_to(shape), ALU.add))


def mixed_phase(nc, sem, d, outs, logits, sxs, fx):
    GR = B * NH
    with ExitStack() as ph:
        def tmp(name, shape):
            return ph.enter_context(nc.sbuf_tensor("mi_" + name, shape, F32))
        lng, lnb = tmp("lng", [P, DH]), tmp("lnb", [P, DH])
        epsc = tmp("eps", [P, 1])
        top, tot = tmp("top", [P, GR]), tmp("tot", [P, GR])
        work = tmp("work", [P, B, D])
        stat = tmp("stat", [P, 2, GR])
        resid = tmp("resid", [P, D])
        s_wts, s_c, s_e, s_v, s_a = (sem("mi_" + n) for n in ("wts", "c", "e", "v", "a"))
        block = ph.enter_context(nc.Block())
        lg = logits[:, :, :].rearrange("p b (n e) -> p (b n) e", n=NH)
        o = outs[:, :, :].rearrange("p b (h d) -> p (b h) d", d=DH)
        fxv = fx[:, :, :].rearrange("p b (n d) -> p (b n) d", d=DH)
        wv = work[:, :, :].rearrange("p b (n d) -> p (b n) d", d=DH)
        nv, na = layernorm(nc.vector, nc.scalar, s_v, s_a, 0, fxv, fxv, wv, stat, GR, DH, epsc[:, 0:1])

        @block.sync
        def _(sp):
            sp.dma_start(lng[:, :], d["lng"].partition_broadcast(P)).then_inc(s_wts, 16)
            sp.dma_start(lnb[:, :], d["lnb"].partition_broadcast(P)).then_inc(s_wts, 16)

        @block.scalar
        def _(act):
            act.wait_ge(s_c, 2)
            act.activation(lg, lg, ACT.Exp).then_inc(s_e, 1)
            na()

        @block.vector
        def _(dve):
            count = [0]

            def link(ins):
                count[0] += 1
                ins.then_inc(s_c, 1)
                dve.wait_ge(s_c, count[0])

            def bc(a, width):
                return a[:, :].unsqueeze(2).broadcast_to((P, GR, width))
            link(dve.tensor_reduce(top[:, :], lg, AX.X, ALU.max))
            link(dve.tensor_tensor(lg, lg, bc(top, NE), ALU.subtract))
            dve.memset(epsc[:, :], 1e-8)
            for n in range(NH):
                dve.tensor_copy(resid[:, n * DH:(n + 1) * DH], sxs[:, n, n * DH:(n + 1) * DH])
            dve.wait_ge(s_e, 1)
            link(dve.tensor_reduce(tot[:, :], lg, AX.X, ALU.add))
            link(dve.reciprocal(tot[:, :], tot[:, :]))
            link(dve.tensor_tensor(lg, lg, bc(tot, NE), ALU.mult))
            w = lg.rearrange("p g e -> p (g e)").unsqueeze(2).broadcast_to((P, GR * NE, DH))
            link(dve.tensor_tensor(o, o, w, ALU.mult))
            link(dve.tensor_reduce(fxv, o.rearrange("p (g e) d -> p g d e", e=NE), AX.X, ALU.add))
            link(dve.tensor_tensor(fx[:, :, :], fx[:, :, :], resid[:, :].unsqueeze(1).broadcast_to((P, B, D)), ALU.add))
            nv().then_inc(s_v, 1)
            dve.wait_ge(s_v, 6)
            dve.wait_ge(s_wts, 32)
            mul, add = gain_bias(fx[:, :, :], lng, lnb)
            link(mul(dve))
            link(add(dve))


def token_phase(nc, sem, name, d, src, out, two):
    GB = BANK // P
    NT = B // GB
    WO = D if two else NH
    with ExitStack() as ph:
        def tmp(n, shape):
            return ph.enter_context(nc.sbuf_tensor(name + n, shape, F32))

        def bank(n, shape):
            return ph.enter_context(nc.psum_tensor(name + n, shape, F32))
        ident = tmp("ident", [P, P])
        wa, ba = tmp("wa", [D, D]), tmp("ba", [D, 1])
        wb, bb = tmp("wb", [D, WO]), tmp("bb", [P, WO])
        xs, fT, msk, hr, hT = ([tmp(f"{n}{i}", [P if n == "xs" else D, GB * D if n == "xs" else BANK]) for i in range(2)]
                               for n in ("xs", "fT", "msk", "hr", "hT"))
        pX, pH, pY = bank("pX", [D, 2, BANK]), bank("pH", [D, 2, BANK]), bank("pY", [P, 2, BANK])
        s_wts, s_xs, s_t, s_fT, s_msk, s_h, s_hr, s_hT, s_y, s_out, s_zero = (
            sem(name + n) for n in ("wts", "xs", "t", "fTs", "msks", "h", "hrs", "hTs", "y", "out", "zero"))
        block = ph.enter_context(nc.Block())
        s_pemark, s_poolmark = sem(name + "pemark"), sem(name + "poolmark")
        rhs_in, s_in = (hT, s_hT) if two else (fT, s_fT)
        LAG = 2 if two else 1

        @block.sync
        def _(sp):
            sp.dma_start(ident[:, :], d["ident"]).then_inc(s_wts, 16)
            sp.dma_start(wb[:, :], d["fc2" if two else "fgate"]).then_inc(s_wts, 16)
            if two:
                sp.dma_start(wa[:, :], d["fc1"]).then_inc(s_wts, 16)
                sp.dma_start(ba[:, :], d["fc1b"]).then_inc(s_wts, 16)
                sp.dma_start(bb[:, :], d["fc2b"].partition_broadcast(P)).then_inc(s_wts, 16)

        @block.gpsimd
        def _(pool):
            def body(it, r, has):
                j = it * 2 + r
                if has(0):
                    ge(pool, s_t, j - 1)
                    mark(pool, s_poolmark)
                    v = j * GB
                    part = src[:, v:v + GB, :] if isinstance(v, int) else src[:, bass.ds(v, GB), :]
                    pool.tensor_copy(xs[r][:, :].rearrange("p (b n) -> p b n", b=GB), part).then_inc(s_xs, 1)
            steps(pool, NT, LAG, 2, body)

        @block.tensor
        def _(pe):
            pe.wait_ge(s_wts, (5 if two else 2) * 16)

            def body(it, r, has):
                j = it * 2 + r
                if has(0):
                    pe.wait_ge(s_xs, j + 1)
                    ge(pe, s_fT, j - 1)
                    mark(pe, s_pemark)
                    for b in range(GB):
                        m = pe.transpose(pX[:, r, b * P:(b + 1) * P], xs[r][:, b * D:(b + 1) * D], ident[:, :])
                    m.then_inc(s_t, 1)
                if two and has(1):
                    pe.wait_ge(s_fT, j)
                    ge(pe, s_hr, j - 2)
                    mark(pe, s_pemark)
                    pe.matmul(pH[:, 1 - r, :], wa[:, :], fT[1 - r][:, :], start=True, stop=True).then_inc(s_h, 1)
                if has(LAG):
                    u = (r - LAG) % 2
                    pe.wait_ge(s_in, j - (LAG - 1))
                    ge(pe, s_out, j - (LAG + 1))
                    for b in range(GB):
                        m = pe.matmul(pY[:, u, b * WO:(b + 1) * WO], rhs_in[u][:, b * P:(b + 1) * P], wb[:, :],
                                      start=True, stop=True)
                    m.then_inc(s_y, 1)
            steps(pe, NT, LAG, 2, body)

        @block.scalar
        def _(act):
            act.wait_ge(s_wts, (5 if two else 2) * 16)

            def body(it, r, has):
                j = it * 2 + r
                if has(0):
                    act.wait_ge(s_t, j + 1)
                    if two:
                        ge(act, s_h, j - 1)
                        ge(act, s_msk, j - 1)
                    else:
                        ge(act, s_y, j - 1)
                    act.activation(fT[r][:, :], pX[:, r, :], ACT.Copy).then_inc(s_fT, 1)
                if two and has(1):
                    act.wait_ge(s_h, j)
                    ge(act, s_hT, j - 2)
                    act.activation(hr[1 - r][:, :], pH[:, 1 - r, :], ACT.Relu, bias=ba[:, 0:1]).then_inc(s_hr, 1)
            steps(act, NT, LAG, 2, body)

        @block.vector
        def _(dve):
            if not two:
                dve.memset(bb[:, :], 0.0).then_inc(s_zero, 1)
                dve.wait_ge(s_zero, 1)
            else:
                dve.wait_ge(s_wts, 5 * 16)

            def body(it, r, has):
                j = it * 2 + r
                if two and has(0):
                    dve.wait_ge(s_fT, j + 1)
                    ge(dve, s_hT, j - 1)
                    dve.tensor_scalar(msk[r][:, :], fT[r][:, :], 0.0, None, ALU.not_equal).then_inc(s_msk, 1)
                if two and has(1):
                    dve.wait_ge(s_hr, j)
                    dve.wait_ge(s_msk, j)
                    ge(dve, s_y, j - 2)
                    dve.tensor_tensor(hT[1 - r][:, :], hr[1 - r][:, :], msk[1 - r][:, :], ALU.mult).then_inc(s_hT, 1)
                if has(LAG):
                    u = (r - LAG) % 2
                    dve.wait_ge(s_y, j - (LAG - 1))
                    v = (j - LAG) * GB
                    dst = out[:, v:v + GB, :] if isinstance(v, int) else out[:, bass.ds(v, GB), :]
                    dve.tensor_tensor(dst, pY[:, u, 0:GB * WO].rearrange("p (b n) -> p b n", b=GB),
                                      bb[:, :].unsqueeze(1).broadcast_to((P, GB, WO)), ALU.add).then_inc(s_out, 1)
            steps(dve, NT, LAG, 2, body)


def hidden_phase(nc, sem, d, fx, hx):
    GR = B * NH
    with ExitStack() as ph:
        def tmp(name, shape):
            return ph.enter_context(nc.sbuf_tensor("hi_" + name, shape, F32))
        g, b = tmp("g", [P, DH]), tmp("b", [P, DH])
        epsc = tmp("eps", [P, 1])
        work = tmp("work", [P, B, D])
        stat = tmp("stat", [P, 2, GR])
        s_wts, s_c, s_v, s_a = (sem("hi_" + n) for n in ("wts", "c", "v", "a"))
        block = ph.enter_context(nc.Block())
        hv = hx[:, :, :].rearrange("p b (n d) -> p (b n) d", d=DH)
        wv = work[:, :, :].rearrange("p b (n d) -> p (b n) d", d=DH)
        nv, na = layernorm(nc.vector, nc.scalar, s_v, s_a, 0, hv, hv, wv, stat, GR, DH, epsc[:, 0:1])

        @block.sync
        def _(sp):
            sp.dma_start(g[:, :], d["fng"].partition_broadcast(P)).then_inc(s_wts, 16)
            sp.dma_start(b[:, :], d["fnb"].partition_broadcast(P)).then_inc(s_wts, 16)

        @block.scalar
        def _(act):
            na()

        @block.vector
        def _(dve):
            dve.memset(epsc[:, :], 1e-8)
            dve.scalar_tensor_tensor(hx[:, :, :], fx[:, :, :], 0.0, hx[:, :, :], ALU.not_equal, ALU.mult).then_inc(s_c, 1)
            dve.wait_ge(s_c, 1)
            dve.tensor_tensor(hx[:, :, :], hx[:, :, :], fx[:, :, :], ALU.add).then_inc(s_c, 1)
            dve.wait_ge(s_c, 2)
            nv().then_inc(s_v, 1)
            dve.wait_ge(s_v, 6)
            dve.wait_ge(s_wts, 32)
            mul, add = gain_bias(hx[:, :, :], g, b)
            mul(dve).then_inc(s_c, 1)
            dve.wait_ge(s_c, 3)
            add(dve).then_inc(s_c, 1)


def gated_phase(nc, sem, hx, lg, tok):
    with ExitStack() as ph:
        top = ph.enter_context(nc.sbuf_tensor("ga_top", [P, B], F32))
        s_c, s_e = sem("ga_c"), sem("ga_e")
        block = ph.enter_context(nc.Block())

        @block.scalar
        def _(act):
            act.wait_ge(s_c, 2)
            act.activation(lg[:, :, :], lg[:, :, :], ACT.Exp).then_inc(s_e, 1)

        @block.vector
        def _(dve):
            count = [0]

            def link(ins):
                count[0] += 1
                ins.then_inc(s_c, 1)
                dve.wait_ge(s_c, count[0])
            bc = top[:, :].unsqueeze(2).broadcast_to((P, B, NH))
            link(dve.tensor_reduce(top[:, :], lg[:, :, :], AX.X, ALU.max))
            link(dve.tensor_tensor(lg[:, :, :], lg[:, :, :], bc, ALU.subtract))
            dve.wait_ge(s_e, 1)
            link(dve.tensor_reduce(top[:, :], lg[:, :, :], AX.X, ALU.add))
            link(dve.reciprocal(top[:, :], top[:, :]))
            link(dve.tensor_tensor(lg[:, :, :], lg[:, :, :], bc, ALU.mult))
            w = lg[:, :, :].rearrange("p b n -> p (b n)").unsqueeze(2).broadcast_to((P, B * NH, DH))
            hv = hx[:, :, :].rearrange("p b (n d) -> p (b n) d", d=DH)
            link(dve.tensor_tensor(hv, hv, w, ALU.mult))
            link(dve.tensor_tensor(tok[:, :, :], tok[:, :, :], hx[:, :, :], ALU.add))


def ffn_all(nc, sem, d, tok):
    with ExitStack() as ph:
        def buf(name, shape):
            return ph.enter_context(nc.sbuf_tensor("f_" + name, shape, F32))
        xn = buf("xn", [P, B, D])
        outs = buf("outs", [P, B, NH * NE * DH])
        logits = buf("logits", [P, B, NH * NE])
        sxs = buf("sxs", [P, B, D])
        lg = buf("lg", [P, B, NH])
        norm_phase(nc, sem, "n2", tok, xn)
        mix_phase(nc, sem, d, xn, outs, logits, sxs)
        mixed_phase(nc, sem, d, outs, logits, sxs, xn)
        token_phase(nc, sem, "fc_", d, xn, sxs, True)
        hidden_phase(nc, sem, d, xn, sxs)
        token_phase(nc, sem, "fg_", d, sxs, lg, False)
        gated_phase(nc, sem, sxs, lg, tok)


def window_layout(x):
    xp = np.pad(x[:, 0, :], ((0, 0), (PAD0, PAD0)), mode="reflect")
    rows = np.zeros((P, NGRP, GX), dtype=x.dtype)
    for q in range(NQ):
        for w in range(2):
            for k in range(K0):
                first = (2 * q + w) * S0 + k
                v = xp[:, first:first + JW * S0 * (CH0 - 1) + 1:JW * S0]
                rows[QUAD * q + WIN * w + k] = v.reshape(NGRP, GX)
            rows[QUAD * q + WIN * w + K0] = 1.0
    return rows


def conv0_layout(w, b):
    out = np.zeros((P, 2, C), dtype=w.dtype)
    for q in range(NQ):
        for i in range(2):
            r = QUAD * q + WIN * i
            out[r:r + K0, i] = w[:, 0, :].T
            out[r + K0, i] = b
    return out


def window_mask():
    m = np.zeros((P, P), dtype=np.float32)
    for q in range(NQ):
        for i in range(2):
            r = QUAD * q + WIN * i
            m[r:r + WIN, r:r + WIN] = 1.0
    return m


def host_inputs(a):
    tok = {k[len("L0_tok_"):]: v for k, v in a.items() if k.startswith("L0_tok_")}
    ffn = {k[len("L0_ffn_"):]: v for k, v in a.items() if k.startswith("L0_ffn_")}
    f32 = np.float32
    out = {
        "x": window_layout(a["x"]),
        "w0": conv0_layout(tok["conv0_w"], tok["conv0_b"]),
        "wmask": window_mask(),
        "ident": np.eye(P, dtype=f32),
        "cols": np.stack([tok[n] for n in ("conv1_b", "conv2_b", "conv3_b", "n0_b", "n1_w", "n1_b", "n2_w", "n2_b",
                                           "n3_w", "n3_b")], axis=1),
        "n0w": tok["n0_w"],
        "w1": tok["conv1_w"].transpose(1, 2, 0),
        "w2": tok["conv2_w"].transpose(1, 2, 0),
        "w3": tok["conv3_w"].transpose(1, 2, 0),
        "mlp_w1": tok["mlp_w1"],
        "mlp_w2": tok["mlp_w2"],
        "mlp_w3": tok["mlp_w3"].reshape(4, P).T,
        "mlp_b12": np.stack([tok["mlp_b1"].reshape(4, P).T, tok["mlp_b2"].reshape(4, P).T], axis=1),
        "mlp_b3": tok["mlp_b3"],
        "upto": np.triu(np.ones((P, P), f32)),
        "before": np.triu(np.ones((P, P), f32), 1),
        "centre": (np.eye(P) - 1.0 / P).astype(f32),
        "iota": np.broadcast_to(np.arange(TN + 1, dtype=f32), (P, TN + 1)),
        "n4": np.stack([tok["n4_w"], tok["n4_b"]], axis=1),
    }
    q, k = (a["L0_attn_" + n].reshape(2, 4 * R1, D).transpose(2, 0, 1) for n in "QK")
    out["wqk"] = np.concatenate([q, k], axis=1)
    out["vo"] = a["L0_attn_VO"].reshape(4, P, D).transpose(1, 0, 2)

    def heads(w):
        n, r, c = w.shape
        m = np.zeros((n * r, n * c), dtype=w.dtype)
        for i in range(n):
            m[i * r:(i + 1) * r, i * c:(i + 1) * c] = w[i]
        return m

    out["causal"] = np.triu(np.full((P, P), -1e30, f32), 1)
    out["hlw"] = ffn["hl_w"].transpose(2, 0, 1).reshape(D, D)
    out["hlb_col"] = ffn["hl_b"].reshape(D, 1)
    out["hlb"] = ffn["hl_b"].reshape(D)
    qk = np.zeros((D, NE + 1, P), dtype=f32)
    for n in range(NH):
        for e in range(NE):
            qk[n * DH:(n + 1) * DH, e, 32 * n:32 * n + DH] = ffn["wq"][n, e].T
        qk[n * DH:(n + 1) * DH, NE, 32 * n:32 * n + DH] = ffn["wk"][n].T
    out["ffq"] = qk
    out["ffv"] = heads(ffn["wv"].transpose(0, 2, 1))
    out["gate"] = heads(ffn["gate_w"].transpose(0, 2, 1)).reshape(2, P, NH * NE).transpose(1, 0, 2)
    out["gateb"] = ffn["gate_b"].reshape(NH * NE)
    out["lng"], out["lnb"], out["fng"], out["fnb"] = (ffn[n] for n in ("ln_g", "ln_b", "fnorm_g", "fnorm_b"))
    for n in ("fc1", "fc2"):
        out[n] = heads(np.broadcast_to(ffn[n + "_w"].T, (NH, DH, DH)))
    out["fc1b"] = np.tile(ffn["fc1_b"], NH).reshape(D, 1)
    out["fc2b"] = np.tile(ffn["fc2_b"], NH)
    out["fgate"] = ffn["fgate_w"].T
    return {k: np.ascontiguousarray(v) for k, v in out.items()}


def audio_tower(nc, d, out):
    with ExitStack() as ctx:
        def sem(name):
            return ctx.enter_context(nc.semaphore(name))

        tok = ctx.enter_context(nc.sbuf_tensor("tok", [P, B, TN], F32))
        with ExitStack() as ph:
            feat = ph.enter_context(nc.sbuf_tensor("feat", [P, B * T], F32))
            imp = ph.enter_context(nc.sbuf_tensor("imp", [P, B], F32))
            conv_phase(nc, sem, d, feat)
            mlp_phase(nc, sem, d, feat, imp)
            pool_phase(nc, sem, d, feat, imp, tok)
        with ExitStack() as ph:
            xn = ph.enter_context(nc.sbuf_tensor("xn", [P, B, TN + 1], F32))
            norm_phase(nc, sem, "n1", tok, xn)
            attn_phase(nc, sem, d, xn, tok)
        ffn_all(nc, sem, d, tok)
        s_out = sem("s_out")
        with nc.Block() as block:
            @block.sync
            def _(sp):
                sp.dma_start(out.rearrange("b c n -> c b n"), tok[:, :, :]).then_inc(s_out, 16)
                sp.wait_ge(s_out, 16)


def kernel(**inputs):
    import numpy as _np
    import concourse.bacc as _bacc
    from concourse import mybir as _mybir
    from concourse.bass_utils import run_bass_kernel_spmd as _run

    nc = _bacc.Bacc("TRN2", target_bir_lowering=False, num_devices=1)
    arrays = host_inputs({k: _np.asarray(v) for k, v in inputs.items()})
    d = {name: nc.dram_tensor(name, a.shape, _mybir.dt.from_np(a.dtype), kind="ExternalInput").ap()
         for name, a in arrays.items()}
    out = nc.dram_tensor("out", (B, C, TN), F32, kind="ExternalOutput").ap()
    audio_tower(nc, d, out)
    r = _run(nc, [arrays], core_ids=[0])
    return r.results[0]["out"]
```

```python
from contextlib import ExitStack

import numpy as np

import concourse.bass as bass
from concourse import mybir

F32 = mybir.dt.float32
BF16 = mybir.dt.bfloat16
ALU = mybir.AluOpType
ACT = mybir.ActivationFunctionType
AX = mybir.AxisListType

P = 128
B = 64
C = 128
BANK = 512
EPS = 1e-5

K0, S0, PAD0, L0 = 10, 5, 3, 2048
K1, S1, PAD1, L1 = 8, 4, 2, 512
K2, S2, PAD2, L2 = 4, 2, 1, 256
K3, S3, PAD3, L3 = 4, 2, 1, 128
T = L3
TN = T // 2
G = 4
NGRP = B // G
WIN = K0 + 1
QUAD = 32
NQ = P // QUAD
JW = 2 * NQ
CH0 = L0 // JW
GX = G * CH0




def ge(eng, sem, value):
    if not isinstance(value, int) or value > 0:
        eng.wait_ge(sem, value)


def mark(eng, sem):
    eng.sem_inc(sem, 1)


def steps(eng, n, lag, per, body):
    rounds = n // per
    head = -(-(lag + 2) // per)
    if rounds - 1 - head < 2:
        head = rounds - 1
    for j in range(head * per):
        body(j // per, j % per, lambda s: j >= s)
    if head < rounds - 1:
        with eng.Fori(head, rounds - 1) as it:
            for r in range(per):
                body(it, r, lambda s: True)
    for j in range(n - per, n + lag):
        body(j // per, j % per, lambda s: 0 <= j - s < n)


def conv_phase(nc, sem, d, feat):
    with ExitStack() as ph:
        def tmp(name, shape, dt=F32):
            return ph.enter_context(nc.sbuf_tensor("cv_" + name, shape, dt))

        xw = [tmp(f"xw{i}", [P, GX]) for i in range(2)]
        prod = tmp("prod", [P, GX])
        rx = tmp("rx", [P, GX])
        w0 = tmp("w0", [P, 2, C])
        w0sum = tmp("w0sum", [P, C])
        w0T = tmp("w0T", [C, P])
        n0w = tmp("n0w", [P, C])
        wmask = tmp("wmask", [P, P])
        gram = tmp("gram", [P, P])
        vmask = tmp("vmask", [P, P])
        ones = tmp("ones", [P, P])
        onesm = tmp("onesm", [P, P])
        ident = tmp("ident", [P, P])
        epsc = tmp("epsc", [P, 1])
        w1 = tmp("w1", [P, K1, C])
        w2 = tmp("w2", [P, K2, C])
        w3 = tmp("w3", [P, K3, C])
        wmean = tmp("wmean", [P, 18])
        cols = tmp("cols", [P, 10])
        bc = tmp("bc", [P, 3])
        h0 = [tmp(f"h0_{i}", [P, G, L0 + 2 * PAD1]) for i in range(2)]
        h1 = tmp("h1", [P, G, L1 + 2 * PAD2])
        h2 = tmp("h2", [P, G, L2 + 2 * PAD3])
        sq = [tmp(f"sq{i}", [P, BANK]) for i in range(2)]
        dev = [tmp(f"dev{i}", [P, BANK]) for i in range(2)]
        yn = [tmp(f"yn{i}", [P, BANK]) for i in range(2)]
        pa = ph.enter_context(nc.psum_tensor("pa", [P, NQ, BANK], F32))
        pc = ph.enter_context(nc.psum_tensor("pc", [P, 2, BANK], F32))
        pv = ph.enter_context(nc.psum_tensor("pv", [P, 2, BANK], F32))

        s_wts, s_x = sem("s_wts"), sem("s_x")
        s_prep = sem("s_prep")
        s_pprep = sem("s_pprep")
        s_a0 = sem("s_a0")
        s_a0free = sem("s_a0free")
        s_halo0 = sem("s_halo0")
        s_z, s_zused = sem("s_z"), sem("s_zused")
        s_r, s_rdev, s_xn = sem("s_r"), sem("s_rdev"), sem("s_xn")
        s_tile = sem("s_tile")
        s_sq, s_var, s_dev = sem("s_sq"), sem("s_var"), sem("s_dev")
        s_rec, s_norm, s_relu = sem("s_rec"), sem("s_norm"), sem("s_relu")
        s_halo = sem("s_halo")
        s_rx = sem("s_rx")
        s_poolmark = sem("s_poolmark")

        TILES = [("c1", 0), ("c2", 1), ("c1", 1), ("c1", 2), ("c3", 0), ("c1", 3), ("c2", 0)]
        SETS = {0: 0, 2: 1, 3: 2, 5: 3}
        Z_AT, R_AT = 1, 4

        def slots(i0, last=False):
            if last:
                return [(0, "c2", 1), (1, "c3", 0)]
            return [(t, k, a) for t, (k, a) in enumerate(TILES)
                    if not (i0 and (k, a) in (("c2", 1), ("c3", 0)))]

        def n_of(i, t, i0, last=False):
            if last:
                return 7 * NGRP - 1 + t
            if i0:
                return {0: 1, 2: 2, 3: 3, 5: 4, 6: 5}[t]
            return i * 7 + (t - 1)

        def bank_of(u, t, i0, last=False):
            if last:
                return (7 * NGRP - 2 + t) % 2
            if i0:
                return ({0: 1, 2: 2, 3: 3, 5: 4, 6: 5}[t] - 1) % 2
            return (7 * u + t - 2) % 2

        def halo_count(i, kind, part, i0):
            if kind == "c2" and part == 0:
                return 2 if i0 else i * 6 + 2
            if kind == "c2":
                return i * 6 - 2
            return i * 6 + 1

        HALOS = {0: ("h1", 0), 1: ("h2", 1), 2: ("h1", 1), 3: ("h1", 2), 5: ("h1", 3), 6: ("h2", 0)}

        def halo_done(i, t, i0, last=False):
            if last:
                return NGRP * 6
            if i0:
                return {0: 1, 2: 2, 3: 3, 5: 4, 6: 5}[t]
            return i * 6 + {0: 0, 1: 1, 2: 2, 3: 3, 5: 4, 6: 5}[t]

        block = ph.enter_context(nc.Block())

        @block.sync
        def _(sp):
            sp.dma_start(w0[:, :, :], d["w0"]).then_inc(s_wts, 16)
            sp.dma_start(wmask[:, :], d["wmask"]).then_inc(s_wts, 16)
            sp.dma_start(ident[:, :], d["ident"]).then_inc(s_wts, 16)
            sp.dma_start(cols[:, :], d["cols"]).then_inc(s_wts, 16)
            sp.dma_start(n0w[:, :], d["n0w"].partition_broadcast(P)).then_inc(s_wts, 16)
            for i in range(2):
                sp.dma_start(xw[i][:, :], d["x"][:, i, :]).then_inc(s_x, 16)
            sp.dma_start(w1[:, :, :], d["w1"]).then_inc(s_wts, 16)
            sp.dma_start(w2[:, :, :], d["w2"]).then_inc(s_wts, 16)
            sp.dma_start(w3[:, :, :], d["w3"]).then_inc(s_wts, 16)
            with sp.Fori(0, NGRP // 2 - 1) as pair:
                for u in range(2):
                    sp.wait_ge(s_a0, pair * 32 + 16 * (u + 1))
                    sp.dma_start(xw[u][:, :], d["x"][:, bass.ds(pair * 2 + (u + 2), 1), :].rearrange("p a n -> p (a n)")).then_inc(s_x, 16)

        @block.gpsimd
        def _(pool):
            def edges0(i, u):
                pool.wait_ge(s_a0free, (i + 1) * 16)
                mark(pool, s_poolmark)
                h = h0[u % 2]
                e = L0 + 2 * PAD1
                pool.tensor_copy(h[:, :, 0:1], h[:, :, 4:5]).then_inc(s_halo0, 1)
                pool.tensor_copy(h[:, :, 1:2], h[:, :, 3:4]).then_inc(s_halo0, 1)
                pool.tensor_copy(h[:, :, e - 2:e - 1], h[:, :, e - 4:e - 3]).then_inc(s_halo0, 1)
                pool.tensor_copy(h[:, :, e - 1:e], h[:, :, e - 5:e - 4]).then_inc(s_halo0, 1)

            def edges(i, t, i0, last=False):
                if last:
                    which, part = "h2", 1
                else:
                    which, part = HALOS[t]
                pool.wait_ge(s_relu, n_of(i, t, i0, last))
                mark(pool, s_poolmark)
                if which == "h1":
                    v, e = h1[:, part:part + 1, :], L1 + 2 * PAD2
                else:
                    v, e = h2[:, 2 * part:2 * part + 2, :], L2 + 2 * PAD3
                pool.tensor_copy(v[:, :, 0:1], v[:, :, 2:3])
                pool.tensor_copy(v[:, :, e - 1:e], v[:, :, e - 3:e - 2]).then_inc(s_halo, 1)

            def body(i, u, i0=False, more=True):
                for t, kind, part in slots(i0):
                    if kind != "c3":
                        edges(i, t, i0)
                    if t == 3 and more:
                        edges0(i + 1, u + 1)
            edges0(0, 0)
            body(0, 0, i0=True)
            body(1, 1)
            with pool.Fori(1, NGRP // 2 - 1) as pair:
                for u in range(2):
                    body(pair * 2 + u, u)
            body(NGRP - 2, 0)
            body(NGRP - 1, 1, more=False)
            edges(NGRP, 0, False, last=True)

        @block.tensor
        def _(pe):
            pe.wait_ge(s_prep, 4)
            pe.transpose(pa[:, 0, 0:P], w0sum[:, :], ident[:, :]).then_inc(s_pprep, 1)
            pe.wait_ge(s_prep, 5)
            pe.matmul(pa[:, 1, 0:P], w0T[:, :], w0T[:, :], start=True, stop=True).then_inc(s_pprep, 1)
            pe.matmul(pa[:, 2, 0:3], onesm[:, :], cols[:, 0:3], start=True, stop=True).then_inc(s_pprep, 1)

            def stat_z(i, u, after_set):
                pe.wait_ge(s_x, (i + 1) * 16)
                if after_set is not None:
                    pe.wait_ge(s_a0free, after_set)
                for hf in range(2):
                    m = pe.matmul(pa[:, hf, :], gram[:, :], xw[u % 2][:, hf * BANK:(hf + 1) * BANK], start=True, stop=True)
                m.then_inc(s_z, 1)

            def stat_r(i, u, after_set):
                pe.wait_ge(s_zused, i + 1)
                if after_set is not None:
                    pe.wait_ge(s_a0free, after_set)
                for hf in range(2):
                    m = pe.matmul(pa[:, hf, :], vmask[:, :], prod[:, hf * BANK:(hf + 1) * BANK], start=True, stop=True)
                m.then_inc(s_r, 1)

            def conv0(i, u, s):
                if s == 0:
                    pe.wait_ge(s_xn, i + 1)
                if s or not isinstance(i, int) or i:
                    pe.wait_ge(s_a0free, i * 16 + 4 * s)
                for q in range(NQ):
                    r = slice(QUAD * q, QUAD * q + QUAD)
                    pe.matmul(pa[:, q, :], w0[r, s % 2, :], xw[u % 2][r, (s // 2) * BANK:(s // 2 + 1) * BANK],
                              start=True, stop=True).then_inc(s_a0, 1)

            def var(n, b):
                pe.wait_ge(s_sq, n)
                if not isinstance(n, int) or n > 2:
                    pe.wait_ge(s_dev, n - 2)
                pe.matmul(pv[:, b, :], ones[:, :], sq[b][:, :], start=True, stop=True).then_inc(s_var, 1)

            def tile(i, u, t, kind, part, i0, last=False):
                n, b = n_of(i, t, i0, last), bank_of(u, t, i0, last)
                if not isinstance(n, int) or n > 2:
                    pe.wait_ge(s_norm, n - 2)
                if kind == "c1":
                    if part == 0:
                        pe.wait_ge(s_halo0, (i + 1) * 4)
                    w, taps = w1, K1
                    src = [h0[u % 2][:, part, k:k + S1 * (L1 - 1) + 1:S1] for k in range(K1)]
                elif kind == "c2":
                    pe.wait_ge(s_halo, halo_count(i, kind, part, i0))
                    w, taps = w2, K2
                    src = [h1[:, 2 * part:2 * part + 2, k:k + S2 * (L2 - 1) + 1:S2] for k in range(K2)]
                else:
                    pe.wait_ge(s_halo, NGRP * 6 if last else halo_count(i, kind, part, i0))
                    w, taps = w3, K3
                    src = [h2[:, :, k:k + S3 * (L3 - 1) + 1:S3] for k in range(K3)]
                for k in range(taps):
                    m = pe.matmul(pc[:, b, :], w[:, k, :], src[k], start=(k == 0), stop=(k == taps - 1))
                m.then_inc(s_tile, 1)

            def body(i, u, i0=False, more=True, more2=True):
                for t, kind, part in slots(i0):
                    if t in SETS and more:
                        if t == 2 and more2:
                            pe.wait_ge(s_zused, i + 3)
                        if t == 5 and more2:
                            pe.wait_ge(s_rdev, i + 3)
                        conv0(i + 1, u + 1, SETS[t])
                    tile(i, u, t, kind, part, i0)
                    n, b = n_of(i, t, i0), bank_of(u, t, i0)
                    if not isinstance(n, int) or n > 1:
                        var(n - 1, 1 - b)
                    if more2:
                        if t == (Z_AT if not i0 else 0):
                            stat_z(i + 2, u, (i + 1) * 16 + 4)
                        if t == (R_AT if not i0 else 3):
                            stat_r(i + 2, u, (i + 1) * 16 + 12)

            pe.wait_ge(s_prep, 10)
            stat_z(0, 0, None)
            stat_r(0, 0, None)
            pe.wait_ge(s_rdev, 1)
            stat_z(1, 1, None)
            stat_r(1, 1, None)
            pe.wait_ge(s_rdev, 2)
            for s in range(4):
                conv0(0, 0, s)
            body(0, 0, i0=True)
            body(1, 1)
            with pe.Fori(1, NGRP // 2 - 1) as pair:
                for u in range(2):
                    body(pair * 2 + u, u)
            body(NGRP - 2, 0, more2=False)
            body(NGRP - 1, 1, more=False, more2=False)
            n, b = n_of(NGRP, 0, False, True), bank_of(0, 0, False, True)
            tile(NGRP, 0, 0, "c2", 1, False, last=True)
            var(n - 1, 1 - b)
            var(n, b)
            tile(NGRP, 0, 1, "c3", 0, False, last=True)
            var(n + 1, 1 - b)

        @block.scalar
        def _(act):
            cb = {"c1": (4, 5), "c2": (6, 7), "c3": (8, 9)}
            bias = {"c1": 0, "c2": 1, "c3": 2}

            def dev_x(i):
                act.wait_ge(s_r, i + 1)
                if not isinstance(i, int) or i > 0:
                    act.wait_ge(s_xn, i)
                act.activation(rx[:, :].rearrange("p (a n) -> p a n", a=2), pa[:, 0:2, :], ACT.Sqrt,
                               bias=epsc[:, 0:1]).then_inc(s_rdev, 1)

            def take0(i, u, s):
                if s == 0 and (not isinstance(i, int) or i >= 2):
                    act.wait_ge(s_tile, i * 7 - 10)
                for q in range(NQ):
                    j = 2 * q + s % 2 + PAD1
                    act.wait_ge(s_a0, i * 16 + (4 * s + q + 1))
                    dst = h0[u % 2][:, 2 * (s // 2):2 * (s // 2) + 2, j:j + JW * (CH0 - 1) + 1:JW]
                    act.activation(dst, pa[:, q, :].rearrange("p (b n) -> p b n", b=2), ACT.Relu,
                                   bias=cols[:, 3:4]).then_inc(s_a0free, 1)

            def square(n, b, kind):
                act.wait_ge(s_tile, n)
                if not isinstance(n, int) or n > 2:
                    act.wait_ge(s_var, n - 2)
                act.activation(sq[b][:, :], pc[:, b, :], ACT.Square, bias=bc[:, bias[kind]:bias[kind] + 1]).then_inc(s_sq, 1)

            def deviation(n, b):
                act.wait_ge(s_var, n)
                if not isinstance(n, int) or n > 2:
                    act.wait_ge(s_norm, n - 2)
                act.activation(dev[b][:, :], pv[:, b, :], ACT.Sqrt, bias=epsc[:, 0:1]).then_inc(s_dev, 1)

            def relu(i, n, b, kind, part):
                act.wait_ge(s_norm, n)
                y = yn[b][:, :]
                if kind == "c1":
                    dst = h1[:, part, PAD2:PAD2 + L1]
                elif kind == "c2":
                    dst, y = h2[:, 2 * part:2 * part + 2, PAD3:PAD3 + L2], y.rearrange("p (b n) -> p b n", b=2)
                elif isinstance(i, int):
                    dst = feat[:, (i - 1) * G * T:i * G * T]
                else:
                    dst = feat[:, bass.ds((i - 1) * G * T, G * T)]
                g, s = cb[kind]
                act.activation(dst, y, ACT.Relu, bias=cols[:, s:s + 1], scale=cols[:, g:g + 1]).then_inc(s_relu, 1)

            def back(i, u, t, i0, k):
                sl = slots(i0)
                at = [x[0] for x in sl].index(t) - k
                n = n_of(i, t, i0) - k
                b = (bank_of(u, t, i0) + k) % 2
                if at >= 0:
                    return i, n, b, sl[at][1], sl[at][2]
                if i0:
                    return None
                return i - 1, n, b, TILES[at][0], TILES[at][1]

            def body(i, u, i0=False, more=True, more2=True):
                for t, kind, part in slots(i0):
                    two = back(i, u, t, i0, 2)
                    if two:
                        relu(*two)
                    if t in SETS and more:
                        take0(i + 1, u + 1, SETS[t])
                    n, b = n_of(i, t, i0), bank_of(u, t, i0)
                    square(n, b, kind)
                    if back(i, u, t, i0, 1):
                        deviation(n - 1, 1 - b)
                    if more2 and t == (R_AT if not i0 else 3):
                        dev_x(i + 2)

            act.wait_ge(s_prep, 10)
            dev_x(0)
            dev_x(1)
            for s in range(4):
                take0(0, 0, s)
            body(0, 0, i0=True)
            body(1, 1)
            with act.Fori(1, NGRP // 2 - 1) as pair:
                for u in range(2):
                    body(pair * 2 + u, u)
            body(NGRP - 2, 0, more2=False)
            body(NGRP - 1, 1, more=False, more2=False)
            n, b = n_of(NGRP, 0, False, True), bank_of(0, 0, False, True)
            relu(NGRP - 1, n - 2, b, *TILES[5])
            square(n, b, "c2")
            deviation(n - 1, 1 - b)
            relu(NGRP - 1, n - 1, 1 - b, *TILES[6])
            deviation(n, b)
            relu(NGRP, n, b, "c2", 1)
            square(n + 1, 1 - b, "c3")
            deviation(n + 1, 1 - b)
            relu(NGRP, n + 1, 1 - b, "c3", 0)

        @block.vector
        def _(dve):
            step = [0]

            def prep(ins):
                ins.then_inc(s_prep, 1)
                step[0] += 1
                dve.wait_ge(s_prep, step[0])

            dve.memset(ones[:, :], 1.0 / (C - 1))
            dve.memset(onesm[:, :], 1.0 / C)
            dve.memset(epsc[:, :], EPS)
            dve.wait_ge(s_wts, 8 * 16)
            prep(dve.tensor_reduce(wmean[:, 0:2], w0[:, :, :], AX.X, ALU.add))
            prep(dve.tensor_scalar(wmean[:, 0:2], wmean[:, 0:2], 1.0 / C, None, ALU.mult))
            prep(dve.tensor_tensor(w0[:, :, :], w0[:, :, :], wmean[:, 0:2].unsqueeze(2).broadcast_to((P, 2, C)), ALU.subtract))
            prep(dve.tensor_tensor(w0sum[:, :], w0[:, 0, :], w0[:, 1, :], ALU.add))
            dve.wait_ge(s_pprep, 1)
            prep(dve.tensor_copy(w0T[:, :], pa[:, 0, 0:P]))
            dve.wait_ge(s_pprep, 3)
            dve.tensor_tensor(gram[:, :], pa[:, 1, 0:P], wmask[:, :], ALU.mult)
            dve.tensor_scalar(vmask[:, :], wmask[:, :], 1.0 / (C - 1), None, ALU.mult)
            dve.tensor_tensor(bc[:, :], cols[:, 0:3], pa[:, 2, 0:3], ALU.subtract)
            prep(dve.tensor_tensor(w0[:, :, :], w0[:, :, :], n0w[:, :].unsqueeze(1).broadcast_to((P, 2, C)), ALU.mult))
            dve.tensor_reduce(wmean[:, 2:10], w1[:, :, :], AX.X, ALU.add)
            dve.tensor_reduce(wmean[:, 10:14], w2[:, :, :], AX.X, ALU.add)
            prep(dve.tensor_reduce(wmean[:, 14:18], w3[:, :, :], AX.X, ALU.add))
            prep(dve.tensor_scalar(wmean[:, 2:18], wmean[:, 2:18], 1.0 / C, None, ALU.mult))
            dve.tensor_tensor(w1[:, :, :], w1[:, :, :], wmean[:, 2:10].unsqueeze(2).broadcast_to((P, K1, C)), ALU.subtract)
            prep(dve.tensor_tensor(w2[:, :, :], w2[:, :, :], wmean[:, 10:14].unsqueeze(2).broadcast_to((P, K2, C)), ALU.subtract))
            prep(dve.tensor_tensor(w3[:, :, :], w3[:, :, :], wmean[:, 14:18].unsqueeze(2).broadcast_to((P, K3, C)), ALU.subtract))

            def products(i, u):
                dve.wait_ge(s_z, i + 1)
                dve.wait_ge(s_x, (i + 1) * 16)
                if not isinstance(i, int) or i > 0:
                    dve.wait_ge(s_r, i)
                dve.tensor_tensor(prod[:, :].rearrange("p (a n) -> p a n", a=2), pa[:, 0:2, :],
                                  xw[u % 2][:, :].rearrange("p (a n) -> p a n", a=2), ALU.mult).then_inc(s_zused, 1)

            def normalise_x(i, u):
                dve.wait_ge(s_rdev, i + 1)
                dve.reciprocal(rx[:, :], rx[:, :]).then_inc(s_rx, 1)
                dve.wait_ge(s_rx, i + 1)
                dve.tensor_tensor(xw[u % 2][:, :], xw[u % 2][:, :], rx[:, :], ALU.mult).then_inc(s_xn, 1)

            def norm(n, b, kind):
                dve.wait_ge(s_dev, n)
                dve.reciprocal(dev[b][:, :], dev[b][:, :]).then_inc(s_rec, 1)
                dve.wait_ge(s_rec, n)
                if not isinstance(n, int) or n > 2:
                    dve.wait_ge(s_relu, n - 2)
                k = {"c1": 0, "c2": 1, "c3": 2}[kind]
                dve.scalar_tensor_tensor(yn[b][:, :], pc[:, b, :], bc[:, k:k + 1], dev[b][:, :], ALU.add,
                                         ALU.mult).then_inc(s_norm, 1)

            def body(i, u, i0=False, more2=True):
                sl = slots(i0)
                for at, (t, kind, part) in enumerate(sl):
                    n, b = n_of(i, t, i0), bank_of(u, t, i0)
                    if at > 0:
                        norm(n - 1, 1 - b, sl[at - 1][1])
                    elif not i0:
                        norm(n - 1, 1 - b, TILES[-1][0])
                    if more2 and t == (Z_AT if not i0 else 0):
                        products(i + 2, u)
                    if more2 and t == (R_AT if not i0 else 3):
                        normalise_x(i + 2, u)

            products(0, 0)
            normalise_x(0, 0)
            products(1, 1)
            normalise_x(1, 1)
            body(0, 0, i0=True)
            body(1, 1)
            with dve.Fori(1, NGRP // 2 - 1) as pair:
                for u in range(2):
                    body(pair * 2 + u, u)
            body(NGRP - 2, 0, more2=False)
            body(NGRP - 1, 1, more2=False)
            n, b = n_of(NGRP, 0, False, True), bank_of(0, 0, False, True)
            norm(n - 1, 1 - b, "c2")
            norm(n, b, "c2")
            norm(n + 1, 1 - b, "c3")


def mlp_phase(nc, sem, d, feat, imp):
    DM = 512
    KT = DM // P
    NT = B * T // BANK
    BT = BANK // T
    with ExitStack() as ph:
        def tmp(name, shape, dt=F32):
            return ph.enter_context(nc.sbuf_tensor("ml_" + name, shape, dt))

        w1 = tmp("w1", [P, DM])
        w2 = tmp("w2", [P, KT, DM])
        w3 = tmp("w3", [P, KT])
        b12 = tmp("b12", [P, 2, KT])
        b3 = tmp("b3", [P, 1])
        z1 = [tmp(f"z1_{i}", [P, KT, BANK]) for i in range(2)]
        z2 = [tmp(f"z2_{i}", [P, KT, BANK]) for i in range(2)]
        p1 = ph.enter_context(nc.psum_tensor("ml_p1", [P, 2, BANK], F32))
        p2 = ph.enter_context(nc.psum_tensor("ml_p2", [P, KT, BANK], F32))
        p3 = ph.enter_context(nc.psum_tensor("ml_p3", [P, B], F32))
        s_wts = sem("ml_wts")
        s_m1, s_g1 = sem("ml_m1"), sem("ml_g1")
        s_m2, s_g2 = sem("ml_m2"), sem("ml_g2")
        s_m3, s_sig = sem("ml_m3"), sem("ml_sig")
        block = ph.enter_context(nc.Block())

        @block.sync
        def _(sp):
            sp.dma_start(w1[:, :], d["mlp_w1"]).then_inc(s_wts, 16)
            sp.dma_start(w2[:, :, :], d["mlp_w2"].rearrange("(k p) n -> p k n", p=P)).then_inc(s_wts, 16)
            sp.dma_start(w3[:, :], d["mlp_w3"]).then_inc(s_wts, 16)
            sp.dma_start(b12[:, :, :], d["mlp_b12"]).then_inc(s_wts, 16)
            sp.dma_start(b3[:, :], d["mlp_b3"].partition_broadcast(P)).then_inc(s_wts, 16)

        @block.tensor
        def _(pe):
            pe.wait_ge(s_wts, 5 * 16)

            def body(it, r, has):
                c = it * 2 + r
                if has(0):
                    for m in range(KT):
                        ge(pe, s_g1, c * KT + (m - 1))
                        rhs = feat[:, c * BANK:(c + 1) * BANK] if isinstance(c, int) else feat[:, bass.ds(c * BANK, BANK)]
                        pe.matmul(p1[:, m % 2, :], w1[:, m * P:(m + 1) * P], rhs, start=True, stop=True).then_inc(s_m1, 1)
                if has(2):
                    ge(pe, s_g2, (c - 1) * KT)
                    for q in range(BT):
                        col = (c - 2) * BT + q
                        out = p3[:, col:col + 1] if isinstance(col, int) else p3[:, bass.ds(col, 1)]
                        for k in range(KT):
                            m3 = pe.matmul(out, z2[r % 2][:, k, q * T:(q + 1) * T], w3[:, k:k + 1],
                                           start=(k == 0), stop=(k == KT - 1))
                    m3.then_inc(s_m3, 1)
                if has(1):
                    ge(pe, s_g1, c * KT)
                    for m in range(KT):
                        ge(pe, s_g2, (c - 2) * KT + (m + 1))
                        for k in range(KT):
                            m2 = pe.matmul(p2[:, m, :], w2[:, k, m * P:(m + 1) * P], z1[1 - r % 2][:, k, :],
                                           start=(k == 0), stop=(k == KT - 1))
                        m2.then_inc(s_m2, 1)
            steps(pe, NT, 2, 2, body)

        @block.scalar
        def _(act):
            act.wait_ge(s_wts, 5 * 16)

            def body(it, r, has):
                c = it * 2 + r
                for m in range(KT):
                    if has(0):
                        act.wait_ge(s_m1, c * KT + (m + 1))
                        if m == 0:
                            ge(act, s_m2, (c - 1) * KT)
                        act.activation(z1[r % 2][:, m, :], p1[:, m % 2, :], ACT.Gelu, bias=b12[:, 0, m:m + 1]).then_inc(s_g1, 1)
                for m in range(KT):
                    if has(1):
                        act.wait_ge(s_m2, (c - 1) * KT + (m + 1))
                        if m == 0:
                            ge(act, s_m3, c - 2)
                        act.activation(z2[1 - r % 2][:, m, :], p2[:, m, :], ACT.Gelu, bias=b12[:, 1, m:m + 1]).then_inc(s_g2, 1)
            steps(act, NT, 2, 2, body)
            act.wait_ge(s_m3, NT)
            act.activation(imp[:, :], p3[:, :], ACT.Sigmoid, bias=b3[:, 0:1]).then_inc(s_sig, 1)


def pool_phase(nc, sem, d, feat, imp, tok):
    NB = BANK // TN
    NT = B // NB
    with ExitStack() as ph:
        def tmp(name, shape, dt=F32):
            return ph.enter_context(nc.sbuf_tensor("po_" + name, shape, dt))

        ident, upto, before, centre = (tmp(n, [P, P]) for n in ("ident", "upto", "before", "centre"))
        onev, one = tmp("onev", [P, P]), tmp("one", [P, P])
        iota = tmp("iota", [P, TN + 1])
        gb = tmp("gb", [P, 2])
        epsc = tmp("epsc", [P, 1])
        rsum = tmp("rsum", [P, B])
        cs = tmp("cs", [P, 2, B])
        over = tmp("over", [P, B, TN + 1])
        share = tmp("share", [P, B, TN])
        wm = tmp("wm", [P, B, TN])
        fin = [tmp(f"fin{i}", [P, NB * T]) for i in range(2)]
        fT = [tmp(f"fT{i}", [P, NB * T]) for i in range(2)]
        pooled, sq, dev, yn = ([tmp(f"{n}{i}", [P, BANK]) for i in range(2)] for n in ("pooled", "sq", "dev", "yn"))
        pt = ph.enter_context(nc.psum_tensor("po_pt", [P, NB * T], F32))
        pp = ph.enter_context(nc.psum_tensor("po_pp", [P, BANK], F32))
        py = ph.enter_context(nc.psum_tensor("po_py", [P, 2, BANK], F32))
        pv = ph.enter_context(nc.psum_tensor("po_pv", [P, BANK], F32))
        s_wts, s_imp, s_sum = sem("po_wts"), sem("po_imp"), sem("po_sum")
        s_fin, s_t, s_fT = sem("po_fin"), sem("po_t"), sem("po_fT")
        s_pool, s_pooled, s_cen, s_sq = sem("po_pool"), sem("po_pooled"), sem("po_cen"), sem("po_sq")
        s_var, s_dev, s_rec, s_norm, s_relu = (sem("po_" + n) for n in ("var", "dev", "rec", "norm", "relu"))
        block = ph.enter_context(nc.Block())

        @block.sync
        def _(sp):
            for t, n in ((ident, "ident"), (upto, "upto"), (before, "before"), (centre, "centre"), (iota, "iota"), (gb, "n4")):
                sp.dma_start(t[:, :], d[n]).then_inc(s_wts, 16)

        @block.tensor
        def _(pe):
            pe.wait_ge(s_wts, 6 * 16)
            pe.wait_ge(s_imp, 1)
            pe.matmul(pv[:, 0:B], one[:, :], imp[:, :], start=True, stop=True).then_inc(s_sum, 1)
            pe.wait_ge(s_imp, 3)
            pe.matmul(pp[:, 0:B], upto[:, :], imp[:, :], start=True, stop=True)
            pe.matmul(pp[:, B:2 * B], before[:, :], imp[:, :], start=True, stop=True).then_inc(s_sum, 1)

            def body(it, r, has):
                j = it * 2 + r
                if has(0):
                    pe.wait_ge(s_fin, j + 1)
                    ge(pe, s_fT, j)
                    for q in range(NB):
                        m = pe.transpose(pt[:, q * T:(q + 1) * T], fin[r][:, q * T:(q + 1) * T], ident[:, :])
                    m.then_inc(s_t, 1)
                if has(1):
                    ge(pe, s_fT, j)
                    ge(pe, s_imp, 4)
                    ge(pe, s_pooled, j - 1)
                    for q in range(NB):
                        b = (j - 1) * NB + q
                        w = wm[:, b, :] if isinstance(b, int) else wm[:, bass.ds(b, 1), :].rearrange("p a n -> p (a n)")
                        m = pe.matmul(pp[:, q * TN:(q + 1) * TN], fT[1 - r][:, q * T:(q + 1) * T], w, start=True, stop=True)
                    m.then_inc(s_pool, 1)
                if has(2):
                    ge(pe, s_pooled, j - 1)
                    ge(pe, s_norm, j - 3)
                    pe.matmul(py[:, r, :], centre[:, :], pooled[r][:, :], start=True, stop=True).then_inc(s_cen, 1)
                if has(3):
                    ge(pe, s_sq, j - 2)
                    ge(pe, s_dev, j - 3)
                    pe.matmul(pv[:, :], onev[:, :], sq[1 - r][:, :], start=True, stop=True).then_inc(s_var, 1)
            steps(pe, NT, 4, 2, body)

        @block.scalar
        def _(act):
            act.wait_ge(s_wts, 6 * 16)

            def body(it, r, has):
                j = it * 2 + r
                if has(4):
                    act.wait_ge(s_norm, j - 3)
                    v = (j - 4) * NB
                    dst = tok[:, v:v + NB, :] if isinstance(v, int) else tok[:, bass.ds(v, NB), :]
                    act.activation(dst, yn[r][:, :].rearrange("p (b n) -> p b n", n=TN), ACT.Relu, bias=gb[:, 1:2],
                                   scale=gb[:, 0:1]).then_inc(s_relu, 1)
                if has(0):
                    ge(act, s_t, j - 1)
                    v = j * NB * T
                    src = feat[:, v:v + NB * T] if isinstance(v, int) else feat[:, bass.ds(v, NB * T)]
                    act.activation(fin[r][:, :], src, ACT.Copy).then_inc(s_fin, 1)
                if has(2):
                    act.wait_ge(s_cen, j - 1)
                    ge(act, s_var, j - 3)
                    act.activation(sq[r][:, :], py[:, r, :], ACT.Square).then_inc(s_sq, 1)
                if has(3):
                    act.wait_ge(s_var, j - 2)
                    ge(act, s_norm, j - 4)
                    act.activation(dev[1 - r][:, :], pv[:, :], ACT.Sqrt, bias=epsc[:, 0:1]).then_inc(s_dev, 1)
            act.wait_ge(s_imp, 1)
            steps(act, NT, 4, 2, body)

        @block.vector
        def _(dve):
            dve.memset(onev[:, :], 1.0 / (C - 1))
            dve.memset(one[:, :], 1.0)
            dve.memset(epsc[:, :], EPS)
            dve.tensor_scalar(imp[:, :], imp[:, :], 1e-5, None, ALU.add).then_inc(s_imp, 1)
            dve.wait_ge(s_sum, 1)
            dve.reciprocal(rsum[:, :], pv[:, 0:B]).then_inc(s_imp, 1)
            dve.wait_ge(s_imp, 2)
            dve.scalar_tensor_tensor(imp[:, :], imp[:, :], float(TN), rsum[:, :], ALU.mult, ALU.mult).then_inc(s_imp, 1)
            dve.wait_ge(s_sum, 2)
            dve.wait_ge(s_wts, 6 * 16)
            dve.tensor_copy(cs[:, :, :], pp[:, 0:2 * B].rearrange("p (a b) -> p a b", a=2)).then_inc(s_rec, 1)
            dve.wait_ge(s_rec, 1)
            num = 1
            for a in range(2):
                def link(ins):
                    nonlocal num
                    num += 1
                    ins.then_inc(s_rec, 1)
                    dve.wait_ge(s_rec, num)
                link(dve.tensor_tensor(over[:, :, :], cs[:, a, :].unsqueeze(2).broadcast_to((P, B, TN + 1)),
                                       iota[:, :].unsqueeze(1).broadcast_to((P, B, TN + 1)), ALU.subtract))
                link(dve.tensor_scalar(over[:, :, :], over[:, :, :], 0.0, None, ALU.max))
                link(dve.memset(over[:, :, TN:TN + 1], 0.0))
                dst = share if a == 0 else wm
                link(dve.tensor_tensor(dst[:, :, :], over[:, :, 0:TN], over[:, :, 1:TN + 1], ALU.subtract))
            dve.tensor_tensor(wm[:, :, :], share[:, :, :], wm[:, :, :], ALU.subtract).then_inc(s_imp, 1)

            def body(it, r, has):
                j = it * 2 + r
                if has(0):
                    dve.wait_ge(s_t, j + 1)
                    ge(dve, s_pool, j - 1)
                    dve.tensor_copy(fT[r][:, :], pt[:, :]).then_inc(s_fT, 1)
                if has(1):
                    dve.wait_ge(s_pool, j)
                    ge(dve, s_cen, j - 2)
                    dve.tensor_copy(pooled[1 - r][:, :], pp[:, :]).then_inc(s_pooled, 1)
                if has(3):
                    dve.wait_ge(s_dev, j - 2)
                    dve.reciprocal(dev[1 - r][:, :], dev[1 - r][:, :]).then_inc(s_rec, 1)
                    dve.wait_ge(s_rec, j - 3 + (num + 1))
                    ge(dve, s_relu, j - 4)
                    dve.tensor_tensor(yn[1 - r][:, :], py[:, 1 - r, :], dev[1 - r][:, :], ALU.mult).then_inc(s_norm, 1)
            steps(dve, NT, 4, 2, body)


def layernorm(dve, act, s_v, s_a, count, x, out, work, stat, groups, width, eps):
    xv, ov, wv = x, out, work

    def bc(a):
        return a.unsqueeze(2).broadcast_to((P, groups, width))

    def vector():
        dve.tensor_reduce(stat[:, 0, 0:groups], xv, AX.X, ALU.add).then_inc(s_v, 1)
        dve.wait_ge(s_v, count + 1)
        dve.tensor_scalar(stat[:, 0, 0:groups], stat[:, 0, 0:groups], 1.0 / width, None, ALU.mult).then_inc(s_v, 1)
        dve.wait_ge(s_v, count + 2)
        dve.tensor_tensor(ov, xv, bc(stat[:, 0, 0:groups]), ALU.subtract).then_inc(s_v, 1)
        dve.wait_ge(s_a, count // 5 * 2 + 1)
        dve.tensor_reduce(stat[:, 1, 0:groups], wv, AX.X, ALU.add).then_inc(s_v, 1)
        dve.wait_ge(s_a, count // 5 * 2 + 2)
        dve.reciprocal(stat[:, 1, 0:groups], stat[:, 1, 0:groups]).then_inc(s_v, 1)
        dve.wait_ge(s_v, count + 5)
        return dve.tensor_tensor(ov, ov, bc(stat[:, 1, 0:groups]), ALU.mult)

    def scalar():
        act.wait_ge(s_v, count + 3)
        act.activation(wv, ov, ACT.Square).then_inc(s_a, 1)
        act.wait_ge(s_v, count + 4)
        act.activation(stat[:, 1, 0:groups], stat[:, 1, 0:groups], ACT.Sqrt, bias=eps, scale=1.0 / width).then_inc(s_a, 1)
    return vector, scalar


D = TN
H1, R1 = 8, 32
NH, NE, DH = 4, 4, 16


def norm_phase(nc, sem, name, tok, xn):
    with ExitStack() as ph:
        work = ph.enter_context(nc.sbuf_tensor(name + "_work", [P, B, D], F32))
        stat = ph.enter_context(nc.sbuf_tensor(name + "_stat", [P, 2, B], F32))
        epsc = ph.enter_context(nc.sbuf_tensor(name + "_eps", [P, 1], F32))
        s_v, s_a = sem(name + "_v"), sem(name + "_a")
        block = ph.enter_context(nc.Block())
        v, a = layernorm(nc.vector, nc.scalar, s_v, s_a, 0, tok[:, :, :], xn[:, :, 0:D], work[:, :, :], stat, B, D, epsc[:, 0:1])

        @block.vector
        def _(dve):
            dve.memset(epsc[:, :], EPS)
            if xn.shape[2] > D:
                dve.memset(xn[:, :, D:D + 1], 1.0)
            v().then_inc(s_v, 1)

        @block.scalar
        def _(act):
            a()


def attn_phase(nc, sem, d, xn, tok):
    GB = BANK // P
    NG = B // GB
    HB = P // R1
    HG = H1 // HB
    QP = 1 + 2 * HG
    SCALE = 1.0 / float(np.sqrt(D))
    with ExitStack() as ph:
        def tmp(name, shape, dt=F32):
            return ph.enter_context(nc.sbuf_tensor("at_" + name, shape, dt))

        def bank(name, shape):
            return ph.enter_context(nc.psum_tensor("at_" + name, shape, F32))

        ident = tmp("ident", [P, P])
        wqk = tmp("wqk", [D, 2 * HG, P])
        vo = tmp("vo", [P, 4, D])
        xs = tmp("xs", [P, GB, D])
        xT = tmp("xT", [D, BANK])
        qT = [tmp(f"qT{i}", [P, HG, BANK]) for i in range(2)]
        kT = [tmp(f"kT{i}", [P, HG, HB, BANK]) for i in range(2)]
        mx = tmp("mx", [P, 2, H1])
        ex = [tmp(f"ex{i}", [P, HG, HB, P]) for i in range(2)]
        exT = [tmp(f"exT{i}", [P, HG, HB, P]) for i in range(2)]
        rs = tmp("rs", [P, 2, H1])
        cx = [tmp(f"cx{i}", [P, H1, D]) for i in range(2)]
        cxT = tmp("cxT", [P, 4, P])
        pS = bank("pS", [P, HG, BANK])
        pT = bank("pT", [P, HG, BANK])
        pO = bank("pO", [P, HG, BANK])
        pM = bank("pM", [P, BANK])
        pR = bank("pR", [P, D])
        s_wts, s_zero, s_xs, s_q, s_qev = (sem("at_" + n) for n in ("wts", "zero", "xs", "q", "qev"))
        s_pemark, s_poolmark = sem("at_pemark"), sem("at_poolmark")
        s_s, s_max, s_sub, s_exp, s_t, s_ev = (sem("at_" + n) for n in ("s", "max", "sub", "exp", "t", "ev"))
        s_pv, s_rs, s_ctx, s_ct, s_cev, s_pr, s_add = (sem("at_" + n) for n in ("pv", "rs", "ctx", "ct", "cev", "pr", "add"))
        PIECES = {(0, 1): 0, (1, 0): 1, (1, 1): 2, (2, 1): 3, (3, 0): 4}
        block = ph.enter_context(nc.Block())

        def before(it, r, slot):
            g = it * 2 + r // GB
            if isinstance(g, int) and g >= NG - 1:
                return QP * NG
            return (g + 1) * QP + sum(1 for at in PIECES if at < (r % GB, slot))

        def piece_at(it, r, slot):
            g = it * 2 + r // GB
            if isinstance(g, int) and g >= NG - 1:
                return None
            return PIECES.get((r % GB, slot))

        @block.sync
        def _(sp):
            sp.dma_start(ident[:, :], d["ident"]).then_inc(s_wts, 16)
            sp.dma_start(wqk[:, :, :], d["wqk"]).then_inc(s_wts, 16)
            sp.dma_start(vo[:, :, :], d["vo"]).then_inc(s_wts, 16)

        @block.gpsimd
        def _(pool):
            for i in range(2):
                pool.memset(kT[i][:, :, :, :], 0.0).then_inc(s_zero, 1)
            pool.tensor_copy(xs[:, :, :], xn[:, 0:GB, 0:D]).then_inc(s_xs, 1)
            with pool.Fori(1, NG) as g:
                pool.wait_ge(s_q, g * QP - (QP - 1))
                mark(pool, s_poolmark)
                pool.tensor_copy(xs[:, :, :], xn[:, bass.ds(g * GB, GB), 0:D]).then_inc(s_xs, 1)

        @block.tensor
        def _(pe):
            pe.wait_ge(s_wts, 3 * 16)

            def piece(g, k):
                if k == 0:
                    pe.wait_ge(s_xs, g + 1)
                    ge(pe, s_qev, g * QP)
                    mark(pe, s_pemark)
                    for b in range(GB):
                        m = pe.transpose(pM[0:D, b * P:(b + 1) * P], xs[:, b, :], ident[:, :])
                else:
                    pe.wait_ge(s_qev, g * QP + k)
                    m = pe.matmul(pM[:, :], wqk[:, k - 1, :], xT[:, :], start=True, stop=True)
                m.then_inc(s_q, 1)

            for k in range(QP):
                piece(0, k)

            def body(it, r, has):
                j, g, b4, gp = it * 8 + r, it * 2 + r // GB, r % GB, r // GB
                cols = slice(b4 * P, b4 * P + P)
                for hg in range(HG):
                    if has(0):
                        if b4 == 0 and hg == 0:
                            pe.wait_ge(s_qev, (g + 1) * QP)
                        ge(pe, s_sub, j * HG + (hg - 1))
                        pe.matmul(pS[:, hg, :], qT[gp][:, hg, cols], kT[gp][:, hg, :, cols],
                                  start=True, stop=True).then_inc(s_s, 1)
                    if has(1):
                        pe.wait_ge(s_exp, j * HG + (hg - 1))
                        ge(pe, s_ev, j * HG + (hg - 3))
                        for i in range(HB):
                            m = pe.transpose(pT[:, hg, i * P:(i + 1) * P], ex[1 - r % 2][:, hg, i, :], ident[:, :])
                        m.then_inc(s_t, 1)
                    if hg == 0 and has(3):
                        pe.wait_ge(s_ctx, j - 2)
                        pe.wait_ge(s_qev, before(it, r, 0))
                        for k in range(4):
                            m = pe.transpose(pM[:, k * P:(k + 1) * P], cx[1 - r % 2][:, 2 * k:2 * k + 2, :].rearrange("p a n -> p (a n)"), ident[:, :])
                        m.then_inc(s_ct, 1)
                    if hg == 0 and has(2):
                        pe.wait_ge(s_ev, (j - 1) * HG)
                        ge(pe, s_ctx, j - 2)
                        b = j - 2
                        rhs = xn[:, b, :] if isinstance(b, int) else xn[:, bass.ds(b, 1), :].rearrange("p a n -> p (a n)")
                        for h in range(H1):
                            at = (h % HB) * (D + 1)
                            m = pe.matmul(pO[:, h // HB, at:at + D + 1], exT[r % 2][:, h // HB, h % HB, :], rhs,
                                          start=True, stop=True)
                        m.then_inc(s_pv, 1)
                    if has(0) and piece_at(it, r, hg) is not None:
                        ge(pe, s_cev, j - 2)
                        piece(g + 1, piece_at(it, r, hg))
                    if hg == 1 and has(3):
                        pe.wait_ge(s_cev, j - 2)
                        ge(pe, s_add, j - 3)
                        for k in range(4):
                            m = pe.matmul(pR[:, :], cxT[:, k, :], vo[:, k, :], start=(k == 0), stop=(k == 3))
                        m.then_inc(s_pr, 1)
            steps(pe, B, 3, 8, body)

        @block.scalar
        def _(act):
            def take(g, k, gp):
                act.wait_ge(s_q, g * QP + (k + 1))
                if k == 0:
                    act.activation(xT[:, :], pM[0:D, :], ACT.Copy).then_inc(s_qev, 1)
                elif k <= HG:
                    act.activation(qT[gp][:, k - 1, :], pM[:, :], ACT.Copy).then_inc(s_qev, 1)
                else:
                    for i in range(HB):
                        rows = slice(R1 * i, R1 * i + R1)
                        m = act.activation(kT[gp][rows, k - 1 - HG, i, :], pM[rows, :], ACT.Copy)
                    m.then_inc(s_qev, 1)

            act.wait_ge(s_zero, 2)
            for k in range(QP):
                take(0, k, 0)

            def exp(j, hg, buf):
                act.wait_ge(s_sub, j * HG + (hg + 1))
                e = ex[buf][:, hg, :, :]
                act.activation(e, e, ACT.Exp, scale=SCALE).then_inc(s_exp, 1)

            def body(it, r, has):
                j, g, gp = it * 8 + r, it * 2 + r // GB, r // GB
                for hg in range(HG):
                    if has(1):
                        if hg == 0:
                            exp(j - 1, 1, 1 - r % 2)
                        act.wait_ge(s_t, j * HG + (hg - 1))
                        ge(act, s_pv, j - 2)
                        act.activation(exT[1 - r % 2][:, hg, :, :], pT[:, hg, :].rearrange("p (i t) -> p i t", i=HB),
                                       ACT.Copy).then_inc(s_ev, 1)
                    if hg == 0 and has(3):
                        act.wait_ge(s_ct, j - 2)
                        ge(act, s_pr, j - 3)
                        act.activation(cxT[:, :, :], pM[:, :].rearrange("p (k t) -> p k t", k=4), ACT.Copy).then_inc(s_cev, 1)
                    if has(0) and hg == 1:
                        exp(j, 0, r % 2)
                    if has(0) and piece_at(it, r, hg) is not None:
                        take(g + 1, piece_at(it, r, hg), 1 - gp)
            steps(act, B, 3, 8, body)

        @block.vector
        def _(dve):
            def body(it, r, has):
                j = it * 8 + r
                for hg in range(HG):
                    if has(0):
                        dve.wait_ge(s_s, j * HG + (hg + 1))
                        sc = pS[:, hg, :].rearrange("p (i u) -> p i u", i=HB)
                        m = mx[:, r % 2, HB * hg:HB * (hg + 1)]
                        dve.tensor_reduce(m, sc, AX.X, ALU.max).then_inc(s_max, 1)
                        dve.wait_ge(s_max, j * HG + (hg + 1))
                        ge(dve, s_t, j * HG + (hg - 3))
                        dve.tensor_tensor(ex[r % 2][:, hg, :, :], sc, m.unsqueeze(2).broadcast_to((P, HB, P)),
                                          ALU.subtract).then_inc(s_sub, 1)
                    if hg == 0 and has(2):
                        dve.wait_ge(s_pv, j - 1)
                        o = pO[:, :, 0:HB * (D + 1)].rearrange("p h (i e) -> p h i e", i=HB)
                        q = rs[:, r % 2, :].rearrange("p (h i) -> p h i", h=HG)
                        dve.reciprocal(q, o[:, :, :, D:D + 1].rearrange("p h i e -> p h (i e)")).then_inc(s_rs, 1)
                        dve.wait_ge(s_rs, j - 1)
                        ge(dve, s_ct, j - 3)
                        dve.tensor_tensor(cx[r % 2][:, :, :].rearrange("p (h i) e -> p h i e", h=HG), o[:, :, :, 0:D],
                                          q.unsqueeze(3).broadcast_to((P, HG, HB, D)), ALU.mult).then_inc(s_ctx, 1)
                    if hg == 1 and has(3):
                        dve.wait_ge(s_pr, j - 2)
                        b = j - 3
                        t = tok[:, b, :] if isinstance(b, int) else tok[:, bass.ds(b, 1), :].rearrange("p a n -> p (a n)")
                        dve.tensor_tensor(t, t, pR[:, :], ALU.add).then_inc(s_add, 1)
            steps(dve, B, 3, 8, body)


def mix_phase(nc, sem, d, xn, outs, logits, sxs):
    GB = BANK // P
    NG = B // GB
    QP = 7
    HOLD = 320
    SCALE = float(np.sqrt(DH))
    with ExitStack() as ph:
        def tmp(name, shape, dt=F32):
            return ph.enter_context(nc.sbuf_tensor("mx_" + name, shape, dt))

        def bank(name, shape):
            return ph.enter_context(nc.psum_tensor("mx_" + name, shape, F32))

        ident = tmp("ident", [P, P])
        identb = tmp("identb", [P, P], BF16)
        causal = tmp("causal", [P, P])
        causalb = tmp("causalb", [P, NH, P], BF16)
        hlw, hlbc, hlb = tmp("hlw", [D, D]), tmp("hlbc", [D, 1]), tmp("hlb", [P, D])
        wqk = tmp("wqk", [D, NE + 1, P])
        wv = tmp("wv", [D, D])
        gate, gateb = tmp("gate", [P, 2, NH * NE]), tmp("gateb", [P, NH * NE])
        xs = tmp("xs", [P, GB, D])
        xT = [tmp(f"xT{i}", [D, BANK]) for i in range(2)]
        sxT = [tmp(f"sxT{i}", [D, BANK]) for i in range(2)]
        qT = [tmp(f"qT{i}", [P, NE, BANK]) for i in range(2)]
        kT = [tmp(f"kT{i}", [P, NH, BANK]) for i in range(2)]
        v1 = [tmp(f"v1_{i}", [P, NH, DH + 1]) for i in range(2)]
        msk = [tmp(f"msk{i}", [P, NH, DH]) for i in range(2)]
        mx = tmp("mx", [P, NE, NH])
        ex = [tmp(f"ex{i}", [P, NE, NH, P]) for i in range(2)]
        exT = [tmp(f"exT{i}", [P, NE, NH, P]) for i in range(2)]
        rs = tmp("rs", [P, NH * NE])
        raw = tmp("raw", [P, NH * NE, DH])
        om = [tmp(f"om{i}", [P, NH, NE, DH]) for i in range(2)]
        oT = [tmp(f"oT{i}", [P, 2, P]) for i in range(2)]
        pS = bank("pS", [P, NE, BANK])
        pT = bank("pT", [P, 2, NH, P])
        pO = bank("pO", [P, BANK])
        pM = bank("pM", [P, BANK])
        s_zero = sem("mx_zero")
        s_wts, s_prep, s_xs, s_q, s_qev = (sem("mx_" + n) for n in ("wts", "prep", "xs", "q", "qev"))
        s_s, s_max, s_sub, s_exp, s_t, s_ev = (sem("mx_" + n) for n in ("s", "max", "sub", "exp", "t", "ev"))
        s_sv, s_sx, s_svev, s_pv, s_rs, s_raw, s_om, s_oc = (sem("mx_" + n) for n in ("sv", "sx", "svev", "pv", "rs", "raw", "om", "oc"))
        s_pemark, s_poolmark = sem("mx_pemark"), sem("mx_poolmark")
        s_gt, s_gev, s_gl, s_lg = (sem("mx_" + n) for n in ("gt", "gev", "gl", "lg"))
        PIECES = {(0, 2): 0, (0, 3): 1, (1, 2): 2, (1, 3): 3, (2, 2): 4, (2, 3): 5, (3, 2): 6}
        block = ph.enter_context(nc.Block())

        def before(it, r, slot):
            g = it * 2 + r // GB
            if isinstance(g, int) and g >= NG - 1:
                return QP * NG
            return (g + 1) * QP + sum(1 for at in PIECES if at < (r % GB, slot))

        def piece_at(it, r, slot):
            g = it * 2 + r // GB
            if isinstance(g, int) and g >= NG - 1:
                return None
            return PIECES.get((r % GB, slot))

        def upto(v):
            return min(v, B) if isinstance(v, int) else v

        @block.sync
        def _(sp):
            for t, n in ((ident, "ident"), (causal, "causal"), (hlw, "hlw"), (hlbc, "hlb_col"), (wv, "ffv")):
                sp.dma_start(t[:, :], d[n]).then_inc(s_wts, 16)
            sp.dma_start(wqk[:, :, :], d["ffq"]).then_inc(s_wts, 16)
            sp.dma_start(gate[:, :, :], d["gate"]).then_inc(s_wts, 16)
            sp.dma_start(hlb[:, :], d["hlb"].partition_broadcast(P)).then_inc(s_wts, 16)
            sp.dma_start(gateb[:, :], d["gateb"].partition_broadcast(P)).then_inc(s_wts, 16)

        @block.gpsimd
        def _(pool):
            for i in range(2):
                pool.memset(kT[i][:, :, :], 0.0).then_inc(s_zero, 1)
            pool.tensor_copy(xs[:, :, :], xn[:, 0:GB, 0:D]).then_inc(s_xs, 1)

            def body(it, r, has):
                j, g = it * 8 + r, it * 2 + r // GB
                if has(0) and r % GB == 0 and piece_at(it, r, 2) is not None:
                    pool.wait_ge(s_q, g * QP + 1)
                    mark(pool, s_poolmark)
                    b = (g + 1) * GB
                    src = xn[:, b:b + GB, 0:D] if isinstance(b, int) else xn[:, bass.ds(b, GB), 0:D]
                    pool.tensor_copy(xs[:, :, :], src).then_inc(s_xs, 1)
                if has(2):
                    pool.wait_ge(s_om, j - 1)
                    mark(pool, s_poolmark)
                    b = j - 2
                    dst = outs[:, b:b + 1, :] if isinstance(b, int) else outs[:, bass.ds(b, 1), :]
                    pool.tensor_copy(dst, om[r % 2][:, :, :, :].rearrange("p n e d -> p (n e d)").unsqueeze(1)).then_inc(s_oc, 1)
            steps(pool, B, 4, 8, body)

        @block.tensor
        def _(pe):
            pe.wait_ge(s_wts, 9 * 16)
            pe.wait_ge(s_prep, 1)

            def piece(g, k, gp):
                if k == 0:
                    pe.wait_ge(s_xs, g + 1)
                    ge(pe, s_qev, g * QP)
                    mark(pe, s_pemark)
                    for b in range(GB):
                        m = pe.transpose(pM[0:D, b * P:(b + 1) * P], xs[:, b, :], ident[:, :])
                else:
                    pe.wait_ge(s_qev, g * QP + k)
                    mark(pe, s_pemark)
                    if k == 1:
                        m = pe.matmul(pM[0:D, :], hlw[:, :], xT[gp][:, :], start=True, stop=True)
                    else:
                        m = pe.matmul(pM[:, :], wqk[:, k - 2, :], sxT[gp][:, :], start=True, stop=True)
                m.then_inc(s_q, 1)

            for k in range(QP):
                piece(0, k, 0)

            def body(it, r, has):
                j, g, b4, gp = it * 8 + r, it * 2 + r // GB, r % GB, r // GB
                cols = slice(b4 * P, b4 * P + P)
                for e in range(NE):
                    if has(0):
                        if b4 == 0 and e == 0:
                            pe.wait_ge(s_qev, (g + 1) * QP)
                        ge(pe, s_sub, j * NE + (e - 3))
                        pe.matmul(pS[:, e, :], identb[:, :], causalb[:, :, :].rearrange("p n u -> p (n u)"),
                                  start=True, stop=False)
                        pe.matmul(pS[:, e, :], qT[gp][:, e, cols], kT[gp][:, :, cols],
                                  start=False, stop=True).then_inc(s_s, 1)
                    if has(1):
                        pe.wait_ge(s_exp, j * NE + (e - 3))
                        ge(pe, s_ev, j * NE + (e - 5))
                        for n in range(NH):
                            m = pe.transpose(pT[:, e % 2, n, :], ex[1 - r % 2][:, e, n, :], ident[:, :])
                        m.then_inc(s_t, 1)
                    if e == 0 and has(2):
                        pe.wait_ge(s_ev, (j - 1) * NE)
                        pe.wait_ge(s_svev, j - 1)
                        ge(pe, s_lg, j - 4)
                        ge(pe, s_om, j - 2)
                        for h in range(NH * NE):
                            at = h * (DH + 1)
                            m = pe.matmul(pO[:, at:at + DH + 1], exT[r % 2][:, h % NE, h // NE, :], v1[r % 2][:, h // NE, :],
                                          start=True, stop=True)
                        m.then_inc(s_pv, 1)
                    if e == 0 and has(0):
                        pe.wait_ge(s_qev, before(it, r, 0))
                        ge(pe, s_gev, j - 3)
                        pe.matmul(pM[:, 0:D], xT[gp][:, cols], hlw[:, :], start=True, stop=True)
                        pe.matmul(pM[:, D:2 * D], sxT[gp][:, cols], wv[:, :], start=True, stop=True).then_inc(s_sv, 1)
                    if e == 3 and has(4):
                        pe.wait_ge(s_gev, j - 3)
                        pe.wait_ge(s_om, upto(j - 1))
                        ge(pe, s_lg, j - 4)
                        for k in range(2):
                            m = pe.matmul(pO[:, HOLD:HOLD + NH * NE], oT[r % 2][:, k, :], gate[:, k, :], start=(k == 0), stop=(k == 1))
                        m.then_inc(s_gl, 1)
                    if e == 1 and has(3):
                        pe.wait_ge(s_om, j - 2)
                        ge(pe, s_gev, j - 3)
                        pe.wait_ge(s_svev, upto(j + 1))
                        pe.wait_ge(s_qev, before(it, r, 1))
                        for k in range(2):
                            m = pe.transpose(pM[:, k * P:(k + 1) * P], om[1 - r % 2][:, 2 * k:2 * k + 2, :, :].rearrange("p n e d -> p (n e d)"), ident[:, :])
                        m.then_inc(s_gt, 1)
                    if has(0) and piece_at(it, r, e) is not None:
                        ge(pe, s_gev, j - 2)
                        pe.wait_ge(s_svev, j + 1)
                        piece(g + 1, piece_at(it, r, e), 1 - gp)
            steps(pe, B, 4, 8, body)

        @block.scalar
        def _(act):
            act.wait_ge(s_wts, 9 * 16)

            def take(g, k, gp):
                act.wait_ge(s_q, g * QP + (k + 1))
                if k == 0:
                    act.activation(xT[gp][:, :], pM[0:D, :], ACT.Copy).then_inc(s_qev, 1)
                elif k == 1:
                    act.activation(sxT[gp][:, :], pM[0:D, :], ACT.Identity, bias=hlbc[:, 0:1]).then_inc(s_qev, 1)
                elif k < 2 + NE:
                    act.activation(qT[gp][:, k - 2, :], pM[:, :], ACT.Copy).then_inc(s_qev, 1)
                else:
                    for n in range(NH):
                        rows = slice(32 * n, 32 * n + 32)
                        m = act.activation(kT[gp][rows, n, :], pM[rows, :], ACT.Copy)
                    m.then_inc(s_qev, 1)

            act.wait_ge(s_zero, 2)
            for k in range(QP):
                take(0, k, 0)

            def exp(j, e, buf):
                act.wait_ge(s_sub, j * NE + (e + 1))
                x = ex[buf][:, e, :, :]
                act.activation(x, x, ACT.Exp, scale=SCALE).then_inc(s_exp, 1)

            def body(it, r, has):
                j, g, gp = it * 8 + r, it * 2 + r // GB, r // GB
                for e in range(NE):
                    if e < 2 and has(1):
                        exp(j - 1, e + 2, 1 - r % 2)
                    if has(1):
                        act.wait_ge(s_t, j * NE + (e - 3))
                        ge(act, s_pv, j - 2)
                        act.activation(exT[1 - r % 2][:, e, :, :], pT[:, e % 2, :, :], ACT.Copy).then_inc(s_ev, 1)
                    if e >= 2 and has(0):
                        exp(j, e - 2, r % 2)
                    if e == 1 and has(3):
                        act.wait_ge(s_gt, j - 2)
                        ge(act, s_gl, j - 4)
                        act.activation(oT[1 - r % 2][:, :, :], pM[:, 0:2 * P].rearrange("p (k t) -> p k t", k=2), ACT.Copy).then_inc(s_gev, 1)
                    if has(0) and piece_at(it, r, e) is not None:
                        take(g + 1, piece_at(it, r, e), 1 - gp)
            steps(act, B, 4, 8, body)

        @block.vector
        def _(dve):
            for i in range(2):
                dve.memset(v1[i][:, :, DH:DH + 1], 1.0)
            dve.wait_ge(s_wts, 9 * 16)
            dve.tensor_copy(identb[:, :], ident[:, :])
            dve.tensor_copy(causalb[:, :, :], causal[:, :].unsqueeze(1).broadcast_to((P, NH, P))).then_inc(s_prep, 1)

            def body(it, r, has):
                j = it * 8 + r
                for e in range(NE):
                    if has(0):
                        dve.wait_ge(s_s, j * NE + (e + 1))
                        sc = pS[:, e, :].rearrange("p (n u) -> p n u", n=NH)
                        dve.tensor_reduce(mx[:, e, :], sc, AX.X, ALU.max).then_inc(s_max, 1)
                        dve.wait_ge(s_max, j * NE + (e + 1))
                        ge(dve, s_t, j * NE + (e - 7))
                        dve.tensor_tensor(ex[r % 2][:, e, :, :], sc, mx[:, e, :].unsqueeze(2).broadcast_to((P, NH, P)),
                                          ALU.subtract).then_inc(s_sub, 1)
                    if e == 0 and has(2):
                        dve.wait_ge(s_pv, j - 1)
                        o = pO[:, 0:NH * NE * (DH + 1)].rearrange("p (h e) -> p h e", h=NH * NE)
                        dve.reciprocal(rs[:, :], o[:, :, DH:DH + 1].rearrange("p h e -> p (h e)")).then_inc(s_rs, 1)
                        dve.wait_ge(s_rs, j - 1)
                        dve.tensor_tensor(raw[:, :, :], o[:, :, 0:DH], rs[:, :].unsqueeze(2).broadcast_to((P, NH * NE, DH)), ALU.mult).then_inc(s_raw, 1)
                        dve.wait_ge(s_raw, j - 1)
                        ge(dve, s_gt, j - 3)
                        ge(dve, s_oc, j - 3)
                        dve.tensor_tensor(om[r % 2][:, :, :, :], raw[:, :, :].rearrange("p (n e) d -> p n e d", n=NH),
                                          msk[r % 2][:, :, :].unsqueeze(2).broadcast_to((P, NH, NE, DH)), ALU.mult).then_inc(s_om, 1)
                    if e == 0 and has(0):
                        dve.wait_ge(s_sv, j + 1)
                        sx = sxs[:, j, :] if isinstance(j, int) else sxs[:, bass.ds(j, 1), :].rearrange("p a n -> p (a n)")
                        dve.tensor_tensor(sx, pM[:, 0:D], hlb[:, :], ALU.add).then_inc(s_sx, 1)
                        dve.tensor_copy(v1[r % 2][:, :, 0:DH], pM[:, D:2 * D].rearrange("p (n o) -> p n o", n=NH))
                        dve.wait_ge(s_sx, j + 1)
                        dve.tensor_scalar(msk[r % 2][:, :, :].rearrange("p n o -> p (n o)"), sx, 0.0, None, ALU.not_equal).then_inc(s_svev, 1)
                    if e == 3 and has(4):
                        dve.wait_ge(s_gl, j - 3)
                        b = j - 4
                        lg = logits[:, b, :] if isinstance(b, int) else logits[:, bass.ds(b, 1), :].rearrange("p a n -> p (a n)")
                        dve.tensor_tensor(lg, pO[:, HOLD:HOLD + NH * NE], gateb[:, :], ALU.add).then_inc(s_lg, 1)
            steps(dve, B, 4, 8, body)


def gain_bias(x, g, b):
    shape = (P, B * NH, DH)
    v = x.rearrange("p b (n d) -> p (b n) d", d=DH)
    return (lambda dve: dve.tensor_tensor(v, v, g[:, :].unsqueeze(1).broadcast_to(shape), ALU.mult),
            lambda dve: dve.tensor_tensor(v, v, b[:, :].unsqueeze(1).broadcast_to(shape), ALU.add))


def mixed_phase(nc, sem, d, outs, logits, sxs, fx):
    GR = B * NH
    with ExitStack() as ph:
        def tmp(name, shape):
            return ph.enter_context(nc.sbuf_tensor("mi_" + name, shape, F32))
        lng, lnb = tmp("lng", [P, DH]), tmp("lnb", [P, DH])
        epsc = tmp("eps", [P, 1])
        top, tot = tmp("top", [P, GR]), tmp("tot", [P, GR])
        work = tmp("work", [P, B, D])
        stat = tmp("stat", [P, 2, GR])
        resid = tmp("resid", [P, D])
        s_wts, s_c, s_e, s_v, s_a = (sem("mi_" + n) for n in ("wts", "c", "e", "v", "a"))
        block = ph.enter_context(nc.Block())
        lg = logits[:, :, :].rearrange("p b (n e) -> p (b n) e", n=NH)
        o = outs[:, :, :].rearrange("p b (h d) -> p (b h) d", d=DH)
        fxv = fx[:, :, :].rearrange("p b (n d) -> p (b n) d", d=DH)
        wv = work[:, :, :].rearrange("p b (n d) -> p (b n) d", d=DH)
        nv, na = layernorm(nc.vector, nc.scalar, s_v, s_a, 0, fxv, fxv, wv, stat, GR, DH, epsc[:, 0:1])

        @block.sync
        def _(sp):
            sp.dma_start(lng[:, :], d["lng"].partition_broadcast(P)).then_inc(s_wts, 16)
            sp.dma_start(lnb[:, :], d["lnb"].partition_broadcast(P)).then_inc(s_wts, 16)

        @block.scalar
        def _(act):
            act.wait_ge(s_c, 2)
            act.activation(lg, lg, ACT.Exp).then_inc(s_e, 1)
            na()

        @block.vector
        def _(dve):
            count = [0]

            def link(ins):
                count[0] += 1
                ins.then_inc(s_c, 1)
                dve.wait_ge(s_c, count[0])

            def bc(a, width):
                return a[:, :].unsqueeze(2).broadcast_to((P, GR, width))
            link(dve.tensor_reduce(top[:, :], lg, AX.X, ALU.max))
            link(dve.tensor_tensor(lg, lg, bc(top, NE), ALU.subtract))
            dve.memset(epsc[:, :], 1e-8)
            for n in range(NH):
                dve.tensor_copy(resid[:, n * DH:(n + 1) * DH], sxs[:, n, n * DH:(n + 1) * DH])
            dve.wait_ge(s_e, 1)
            link(dve.tensor_reduce(tot[:, :], lg, AX.X, ALU.add))
            link(dve.reciprocal(tot[:, :], tot[:, :]))
            link(dve.tensor_tensor(lg, lg, bc(tot, NE), ALU.mult))
            w = lg.rearrange("p g e -> p (g e)").unsqueeze(2).broadcast_to((P, GR * NE, DH))
            link(dve.tensor_tensor(o, o, w, ALU.mult))
            link(dve.tensor_reduce(fxv, o.rearrange("p (g e) d -> p g d e", e=NE), AX.X, ALU.add))
            link(dve.tensor_tensor(fx[:, :, :], fx[:, :, :], resid[:, :].unsqueeze(1).broadcast_to((P, B, D)), ALU.add))
            nv().then_inc(s_v, 1)
            dve.wait_ge(s_v, 6)
            dve.wait_ge(s_wts, 32)
            mul, add = gain_bias(fx[:, :, :], lng, lnb)
            link(mul(dve))
            link(add(dve))


def token_phase(nc, sem, name, d, src, out, two):
    GB = BANK // P
    NT = B // GB
    WO = D if two else NH
    with ExitStack() as ph:
        def tmp(n, shape):
            return ph.enter_context(nc.sbuf_tensor(name + n, shape, F32))

        def bank(n, shape):
            return ph.enter_context(nc.psum_tensor(name + n, shape, F32))
        ident = tmp("ident", [P, P])
        wa, ba = tmp("wa", [D, D]), tmp("ba", [D, 1])
        wb, bb = tmp("wb", [D, WO]), tmp("bb", [P, WO])
        xs, fT, msk, hr, hT = ([tmp(f"{n}{i}", [P if n == "xs" else D, GB * D if n == "xs" else BANK]) for i in range(2)]
                               for n in ("xs", "fT", "msk", "hr", "hT"))
        pX, pH, pY = bank("pX", [D, 2, BANK]), bank("pH", [D, 2, BANK]), bank("pY", [P, 2, BANK])
        s_wts, s_xs, s_t, s_fT, s_msk, s_h, s_hr, s_hT, s_y, s_out, s_zero = (
            sem(name + n) for n in ("wts", "xs", "t", "fTs", "msks", "h", "hrs", "hTs", "y", "out", "zero"))
        block = ph.enter_context(nc.Block())
        s_pemark, s_poolmark = sem(name + "pemark"), sem(name + "poolmark")
        rhs_in, s_in = (hT, s_hT) if two else (fT, s_fT)
        LAG = 2 if two else 1

        @block.sync
        def _(sp):
            sp.dma_start(ident[:, :], d["ident"]).then_inc(s_wts, 16)
            sp.dma_start(wb[:, :], d["fc2" if two else "fgate"]).then_inc(s_wts, 16)
            if two:
                sp.dma_start(wa[:, :], d["fc1"]).then_inc(s_wts, 16)
                sp.dma_start(ba[:, :], d["fc1b"]).then_inc(s_wts, 16)
                sp.dma_start(bb[:, :], d["fc2b"].partition_broadcast(P)).then_inc(s_wts, 16)

        @block.gpsimd
        def _(pool):
            def body(it, r, has):
                j = it * 2 + r
                if has(0):
                    ge(pool, s_t, j - 1)
                    mark(pool, s_poolmark)
                    v = j * GB
                    part = src[:, v:v + GB, :] if isinstance(v, int) else src[:, bass.ds(v, GB), :]
                    pool.tensor_copy(xs[r][:, :].rearrange("p (b n) -> p b n", b=GB), part).then_inc(s_xs, 1)
            steps(pool, NT, LAG, 2, body)

        @block.tensor
        def _(pe):
            pe.wait_ge(s_wts, (5 if two else 2) * 16)

            def body(it, r, has):
                j = it * 2 + r
                if has(0):
                    pe.wait_ge(s_xs, j + 1)
                    ge(pe, s_fT, j - 1)
                    mark(pe, s_pemark)
                    for b in range(GB):
                        m = pe.transpose(pX[:, r, b * P:(b + 1) * P], xs[r][:, b * D:(b + 1) * D], ident[:, :])
                    m.then_inc(s_t, 1)
                if two and has(1):
                    pe.wait_ge(s_fT, j)
                    ge(pe, s_hr, j - 2)
                    mark(pe, s_pemark)
                    pe.matmul(pH[:, 1 - r, :], wa[:, :], fT[1 - r][:, :], start=True, stop=True).then_inc(s_h, 1)
                if has(LAG):
                    u = (r - LAG) % 2
                    pe.wait_ge(s_in, j - (LAG - 1))
                    ge(pe, s_out, j - (LAG + 1))
                    for b in range(GB):
                        m = pe.matmul(pY[:, u, b * WO:(b + 1) * WO], rhs_in[u][:, b * P:(b + 1) * P], wb[:, :],
                                      start=True, stop=True)
                    m.then_inc(s_y, 1)
            steps(pe, NT, LAG, 2, body)

        @block.scalar
        def _(act):
            act.wait_ge(s_wts, (5 if two else 2) * 16)

            def body(it, r, has):
                j = it * 2 + r
                if has(0):
                    act.wait_ge(s_t, j + 1)
                    if two:
                        ge(act, s_h, j - 1)
                        ge(act, s_msk, j - 1)
                    else:
                        ge(act, s_y, j - 1)
                    act.activation(fT[r][:, :], pX[:, r, :], ACT.Copy).then_inc(s_fT, 1)
                if two and has(1):
                    act.wait_ge(s_h, j)
                    ge(act, s_hT, j - 2)
                    act.activation(hr[1 - r][:, :], pH[:, 1 - r, :], ACT.Relu, bias=ba[:, 0:1]).then_inc(s_hr, 1)
            steps(act, NT, LAG, 2, body)

        @block.vector
        def _(dve):
            if not two:
                dve.memset(bb[:, :], 0.0).then_inc(s_zero, 1)
                dve.wait_ge(s_zero, 1)
            else:
                dve.wait_ge(s_wts, 5 * 16)

            def body(it, r, has):
                j = it * 2 + r
                if two and has(0):
                    dve.wait_ge(s_fT, j + 1)
                    ge(dve, s_hT, j - 1)
                    dve.tensor_scalar(msk[r][:, :], fT[r][:, :], 0.0, None, ALU.not_equal).then_inc(s_msk, 1)
                if two and has(1):
                    dve.wait_ge(s_hr, j)
                    dve.wait_ge(s_msk, j)
                    ge(dve, s_y, j - 2)
                    dve.tensor_tensor(hT[1 - r][:, :], hr[1 - r][:, :], msk[1 - r][:, :], ALU.mult).then_inc(s_hT, 1)
                if has(LAG):
                    u = (r - LAG) % 2
                    dve.wait_ge(s_y, j - (LAG - 1))
                    v = (j - LAG) * GB
                    dst = out[:, v:v + GB, :] if isinstance(v, int) else out[:, bass.ds(v, GB), :]
                    dve.tensor_tensor(dst, pY[:, u, 0:GB * WO].rearrange("p (b n) -> p b n", b=GB),
                                      bb[:, :].unsqueeze(1).broadcast_to((P, GB, WO)), ALU.add).then_inc(s_out, 1)
            steps(dve, NT, LAG, 2, body)


def hidden_phase(nc, sem, d, fx, hx):
    GR = B * NH
    with ExitStack() as ph:
        def tmp(name, shape):
            return ph.enter_context(nc.sbuf_tensor("hi_" + name, shape, F32))
        g, b = tmp("g", [P, DH]), tmp("b", [P, DH])
        epsc = tmp("eps", [P, 1])
        work = tmp("work", [P, B, D])
        stat = tmp("stat", [P, 2, GR])
        s_wts, s_c, s_v, s_a = (sem("hi_" + n) for n in ("wts", "c", "v", "a"))
        block = ph.enter_context(nc.Block())
        hv = hx[:, :, :].rearrange("p b (n d) -> p (b n) d", d=DH)
        wv = work[:, :, :].rearrange("p b (n d) -> p (b n) d", d=DH)
        nv, na = layernorm(nc.vector, nc.scalar, s_v, s_a, 0, hv, hv, wv, stat, GR, DH, epsc[:, 0:1])

        @block.sync
        def _(sp):
            sp.dma_start(g[:, :], d["fng"].partition_broadcast(P)).then_inc(s_wts, 16)
            sp.dma_start(b[:, :], d["fnb"].partition_broadcast(P)).then_inc(s_wts, 16)

        @block.scalar
        def _(act):
            na()

        @block.vector
        def _(dve):
            dve.memset(epsc[:, :], 1e-8)
            dve.scalar_tensor_tensor(hx[:, :, :], fx[:, :, :], 0.0, hx[:, :, :], ALU.not_equal, ALU.mult).then_inc(s_c, 1)
            dve.wait_ge(s_c, 1)
            dve.tensor_tensor(hx[:, :, :], hx[:, :, :], fx[:, :, :], ALU.add).then_inc(s_c, 1)
            dve.wait_ge(s_c, 2)
            nv().then_inc(s_v, 1)
            dve.wait_ge(s_v, 6)
            dve.wait_ge(s_wts, 32)
            mul, add = gain_bias(hx[:, :, :], g, b)
            mul(dve).then_inc(s_c, 1)
            dve.wait_ge(s_c, 3)
            add(dve).then_inc(s_c, 1)


def gated_phase(nc, sem, hx, lg, tok):
    with ExitStack() as ph:
        top = ph.enter_context(nc.sbuf_tensor("ga_top", [P, B], F32))
        s_c, s_e = sem("ga_c"), sem("ga_e")
        block = ph.enter_context(nc.Block())

        @block.scalar
        def _(act):
            act.wait_ge(s_c, 2)
            act.activation(lg[:, :, :], lg[:, :, :], ACT.Exp).then_inc(s_e, 1)

        @block.vector
        def _(dve):
            count = [0]

            def link(ins):
                count[0] += 1
                ins.then_inc(s_c, 1)
                dve.wait_ge(s_c, count[0])
            bc = top[:, :].unsqueeze(2).broadcast_to((P, B, NH))
            link(dve.tensor_reduce(top[:, :], lg[:, :, :], AX.X, ALU.max))
            link(dve.tensor_tensor(lg[:, :, :], lg[:, :, :], bc, ALU.subtract))
            dve.wait_ge(s_e, 1)
            link(dve.tensor_reduce(top[:, :], lg[:, :, :], AX.X, ALU.add))
            link(dve.reciprocal(top[:, :], top[:, :]))
            link(dve.tensor_tensor(lg[:, :, :], lg[:, :, :], bc, ALU.mult))
            w = lg[:, :, :].rearrange("p b n -> p (b n)").unsqueeze(2).broadcast_to((P, B * NH, DH))
            hv = hx[:, :, :].rearrange("p b (n d) -> p (b n) d", d=DH)
            link(dve.tensor_tensor(hv, hv, w, ALU.mult))
            link(dve.tensor_tensor(tok[:, :, :], tok[:, :, :], hx[:, :, :], ALU.add))


def ffn_all(nc, sem, d, tok):
    with ExitStack() as ph:
        def buf(name, shape):
            return ph.enter_context(nc.sbuf_tensor("f_" + name, shape, F32))
        xn = buf("xn", [P, B, D])
        outs = buf("outs", [P, B, NH * NE * DH])
        logits = buf("logits", [P, B, NH * NE])
        sxs = buf("sxs", [P, B, D])
        lg = buf("lg", [P, B, NH])
        norm_phase(nc, sem, "n2", tok, xn)
        mix_phase(nc, sem, d, xn, outs, logits, sxs)
        mixed_phase(nc, sem, d, outs, logits, sxs, xn)
        token_phase(nc, sem, "fc_", d, xn, sxs, True)
        hidden_phase(nc, sem, d, xn, sxs)
        token_phase(nc, sem, "fg_", d, sxs, lg, False)
        gated_phase(nc, sem, sxs, lg, tok)


def window_layout(x):
    xp = np.pad(x[:, 0, :], ((0, 0), (PAD0, PAD0)), mode="reflect")
    rows = np.zeros((P, NGRP, GX), dtype=x.dtype)
    for q in range(NQ):
        for w in range(2):
            for k in range(K0):
                first = (2 * q + w) * S0 + k
                v = xp[:, first:first + JW * S0 * (CH0 - 1) + 1:JW * S0]
                rows[QUAD * q + WIN * w + k] = v.reshape(NGRP, GX)
            rows[QUAD * q + WIN * w + K0] = 1.0
    return rows


def conv0_layout(w, b):
    out = np.zeros((P, 2, C), dtype=w.dtype)
    for q in range(NQ):
        for i in range(2):
            r = QUAD * q + WIN * i
            out[r:r + K0, i] = w[:, 0, :].T
            out[r + K0, i] = b
    return out


def window_mask():
    m = np.zeros((P, P), dtype=np.float32)
    for q in range(NQ):
        for i in range(2):
            r = QUAD * q + WIN * i
            m[r:r + WIN, r:r + WIN] = 1.0
    return m


def host_inputs(a):
    tok = {k[len("L0_tok_"):]: v for k, v in a.items() if k.startswith("L0_tok_")}
    ffn = {k[len("L0_ffn_"):]: v for k, v in a.items() if k.startswith("L0_ffn_")}
    f32 = np.float32
    out = {
        "x": window_layout(a["x"]),
        "w0": conv0_layout(tok["conv0_w"], tok["conv0_b"]),
        "wmask": window_mask(),
        "ident": np.eye(P, dtype=f32),
        "cols": np.stack([tok[n] for n in ("conv1_b", "conv2_b", "conv3_b", "n0_b", "n1_w", "n1_b", "n2_w", "n2_b",
                                           "n3_w", "n3_b")], axis=1),
        "n0w": tok["n0_w"],
        "w1": tok["conv1_w"].transpose(1, 2, 0),
        "w2": tok["conv2_w"].transpose(1, 2, 0),
        "w3": tok["conv3_w"].transpose(1, 2, 0),
        "mlp_w1": tok["mlp_w1"],
        "mlp_w2": tok["mlp_w2"],
        "mlp_w3": tok["mlp_w3"].reshape(4, P).T,
        "mlp_b12": np.stack([tok["mlp_b1"].reshape(4, P).T, tok["mlp_b2"].reshape(4, P).T], axis=1),
        "mlp_b3": tok["mlp_b3"],
        "upto": np.triu(np.ones((P, P), f32)),
        "before": np.triu(np.ones((P, P), f32), 1),
        "centre": (np.eye(P) - 1.0 / P).astype(f32),
        "iota": np.broadcast_to(np.arange(TN + 1, dtype=f32), (P, TN + 1)),
        "n4": np.stack([tok["n4_w"], tok["n4_b"]], axis=1),
    }
    q, k = (a["L0_attn_" + n].reshape(2, 4 * R1, D).transpose(2, 0, 1) for n in "QK")
    out["wqk"] = np.concatenate([q, k], axis=1)
    out["vo"] = a["L0_attn_VO"].reshape(4, P, D).transpose(1, 0, 2)

    def heads(w):
        n, r, c = w.shape
        m = np.zeros((n * r, n * c), dtype=w.dtype)
        for i in range(n):
            m[i * r:(i + 1) * r, i * c:(i + 1) * c] = w[i]
        return m

    out["causal"] = np.triu(np.full((P, P), -1e30, f32), 1)
    out["hlw"] = ffn["hl_w"].transpose(2, 0, 1).reshape(D, D)
    out["hlb_col"] = ffn["hl_b"].reshape(D, 1)
    out["hlb"] = ffn["hl_b"].reshape(D)
    qk = np.zeros((D, NE + 1, P), dtype=f32)
    for n in range(NH):
        for e in range(NE):
            qk[n * DH:(n + 1) * DH, e, 32 * n:32 * n + DH] = ffn["wq"][n, e].T
        qk[n * DH:(n + 1) * DH, NE, 32 * n:32 * n + DH] = ffn["wk"][n].T
    out["ffq"] = qk
    out["ffv"] = heads(ffn["wv"].transpose(0, 2, 1))
    out["gate"] = heads(ffn["gate_w"].transpose(0, 2, 1)).reshape(2, P, NH * NE).transpose(1, 0, 2)
    out["gateb"] = ffn["gate_b"].reshape(NH * NE)
    out["lng"], out["lnb"], out["fng"], out["fnb"] = (ffn[n] for n in ("ln_g", "ln_b", "fnorm_g", "fnorm_b"))
    for n in ("fc1", "fc2"):
        out[n] = heads(np.broadcast_to(ffn[n + "_w"].T, (NH, DH, DH)))
    out["fc1b"] = np.tile(ffn["fc1_b"], NH).reshape(D, 1)
    out["fc2b"] = np.tile(ffn["fc2_b"], NH)
    out["fgate"] = ffn["fgate_w"].T
    return {k: np.ascontiguousarray(v) for k, v in out.items()}


def audio_tower(nc, d, out):
    with ExitStack() as ctx:
        def sem(name):
            return ctx.enter_context(nc.semaphore(name))

        tok = ctx.enter_context(nc.sbuf_tensor("tok", [P, B, TN], F32))
        with ExitStack() as ph:
            feat = ph.enter_context(nc.sbuf_tensor("feat", [P, B * T], F32))
            imp = ph.enter_context(nc.sbuf_tensor("imp", [P, B], F32))
            conv_phase(nc, sem, d, feat)
            mlp_phase(nc, sem, d, feat, imp)
            pool_phase(nc, sem, d, feat, imp, tok)
        with ExitStack() as ph:
            xn = ph.enter_context(nc.sbuf_tensor("xn", [P, B, TN + 1], F32))
            norm_phase(nc, sem, "n1", tok, xn)
            attn_phase(nc, sem, d, xn, tok)
        ffn_all(nc, sem, d, tok)
        s_out = sem("s_out")
        with nc.Block() as block:
            @block.sync
            def _(sp):
                sp.dma_start(out.rearrange("b c n -> c b n"), tok[:, :, :]).then_inc(s_out, 16)
                sp.wait_ge(s_out, 16)


def kernel(**inputs):
    import numpy as _np
    import concourse.bacc as _bacc
    from concourse import mybir as _mybir
    from concourse.bass_utils import run_bass_kernel_spmd as _run

    nc = _bacc.Bacc("TRN2", target_bir_lowering=False, num_devices=1)
    arrays = host_inputs({k: _np.asarray(v) for k, v in inputs.items()})
    d = {name: nc.dram_tensor(name, a.shape, _mybir.dt.from_np(a.dtype), kind="ExternalInput").ap()
         for name, a in arrays.items()}
    out = nc.dram_tensor("out", (B, C, TN), F32, kind="ExternalOutput").ap()
    audio_tower(nc, d, out)
    r = _run(nc, [arrays], core_ids=[0])
    return r.results[0]["out"]
```

```python
from contextlib import ExitStack

import numpy as np

import concourse.bass as bass
from concourse import mybir

F32 = mybir.dt.float32
BF16 = mybir.dt.bfloat16
F32R = mybir.dt.float32r
ALU = mybir.AluOpType
ACT = mybir.ActivationFunctionType
AX = mybir.AxisListType

P = 128
B = 64
C = 128
BANK = 512
EPS = 1e-5

K0, S0, PAD0, L0 = 10, 5, 3, 2048
K1, S1, PAD1, L1 = 8, 4, 2, 512
K2, S2, PAD2, L2 = 4, 2, 1, 256
K3, S3, PAD3, L3 = 4, 2, 1, 128
T = L3
TN = T // 2
DMLP = 512
G = 4
NGRP = B // G
WIN = K0 + 1
WROWS = 16
JW = P // WROWS
NQ = JW // 2
ONE = P - 1
CH0 = L0 // JW
GX = G * CH0




def ge(eng, sem, value):
    if not isinstance(value, int) or value > 0:
        eng.wait_ge(sem, value)


def mark(eng, sem):
    eng.sem_inc(sem, 1)


def steps(eng, n, lag, per, body):
    rounds = n // per
    head = -(-(lag + 2) // per)
    if rounds - 1 - head < 2:
        head = rounds - 1
    for j in range(head * per):
        body(j // per, j % per, lambda s: j >= s)
    if head < rounds - 1:
        with eng.Fori(head, rounds - 1) as it:
            for r in range(per):
                body(it, r, lambda s: True)
    for j in range(n - per, n + lag):
        body(j // per, j % per, lambda s: 0 <= j - s < n)


MLP_KEPT = (("mlp_w3", P, (4,)), ("mlp_b12", P, (2, 4)), ("mlp_b3", P, (1,)))
MLP_RAW = (("mlp_w1", P, (DMLP,)), ("mlp_w2", P, (4, DMLP)))
LATER = (("ident", P, (P,)), ("upto", P, (P,)), ("before", P, (P,)), ("centre", P, (P,)), ("iota", P, (TN + 1,)),
         ("n4", P, (2,)), ("wqk", TN, (4, P)), ("vo", P, (4, TN)), ("causal", P, (P,)), ("hlw", TN, (TN,)),
         ("hlb_col", TN, (1,)), ("hlb", P, (TN,)), ("ffv", TN, (TN,)), ("ffq", TN, (5, P)), ("gate", P, (2, 16)),
         ("gateb", P, (16,)), ("lorow", P, (1,)), ("fc1", TN, (TN,)), ("fc1b", TN, (1,)), ("fc2", TN, (TN,)), ("fc2b", P, (TN,)),
         ("fgate", TN, (4,)), ("lng", P, (16,)), ("lnb", P, (16,)), ("fng", P, (16,)), ("fnb", P, (16,)))
BROADCAST = ("mlp_b3", "hlb", "gateb", "fc2b", "lng", "lnb", "fng", "fnb")


def size(entries):
    return sum(int(np.prod(shape)) for _, _, shape in entries)


class Weights:

    def __init__(self, area, sem):
        self.place = {}
        for entries, at in ((MLP_KEPT, 0), (MLP_RAW, size(MLP_KEPT)), (LATER, size(MLP_KEPT))):
            for name, parts, shape in entries:
                n = int(np.prod(shape))
                v = area[0:parts, at:at + n]
                self.place[name] = v.rearrange("p (a b) -> p a b", b=shape[1]) if len(shape) == 2 else v
                at += n
        self.s_mlp, self.s_later = sem("w_mlp"), sem("w_later")

    def __getitem__(self, name):
        return self.place[name]

    def load(self, eng, d, entries, signal):
        for name, _, _ in entries:
            src = d[name]
            if name == "mlp_w2":
                src = src.rearrange("(k p) n -> p k n", p=P)
            if name in BROADCAST:
                src = src.partition_broadcast(P)
            eng.dma_start(self.place[name], src).then_inc(signal, 16)

    def wait_mlp(self, eng):
        eng.wait_ge(self.s_mlp, 16 * (len(MLP_KEPT) + len(MLP_RAW)))

    def wait(self, eng):
        eng.wait_ge(self.s_later, 16 * len(LATER))


def conv_phase(nc, sem, d, wts, feat):
    with ExitStack() as ph:
        def tmp(name, shape, dt=F32):
            return ph.enter_context(nc.sbuf_tensor("cv_" + name, shape, dt))

        HI, LO = 0, 1
        PASSES = ((HI, HI), (HI, LO), (LO, HI))
        H0 = L0 + 2 * PAD1
        xw = [tmp(f"xw{i}", [P, GX]) for i in range(2)]
        xs = [tmp(f"xs{i}", [P, 2, GX], F32R) for i in range(2)]
        prod = tmp("prod", [P, GX])
        NX = GX // P
        sdx = tmp("sdx", [P, NX * JW])
        rcx = tmp("rcx", [P, NX * JW])
        rows = tmp("rows", [P, NX * JW, WROWS])
        w0 = tmp("w0", [P, C])
        n0bw = tmp("n0bw", [P, C])
        w0f = tmp("w0f", [P, C])
        w0s = tmp("w0s", [P, 2, JW, C], F32R)
        w0T = tmp("w0T", [C, P])
        n0w = tmp("n0w", [P, C])
        wmask = tmp("wmask", [P, P])
        rowsel = tmp("rowsel", [P, JW])
        gram = tmp("gram", [P, P])
        selv = tmp("selv", [P, JW])
        vcol = tmp("vcol", [P, 1])
        ones = tmp("ones", [P, P])
        onesm = tmp("onesm", [P, P])
        ident = tmp("ident", [P, P])
        epsc = tmp("epsc", [P, 1])
        taps = {"c1": K1, "c2": K2, "c3": K3}
        w = tmp("w", [P, K1 + K2 + K3, C])
        ws = tmp("ws", [P, 2, K1 + K2 + K3, C], F32R)
        first_tap = {"c1": 0, "c2": K1, "c3": K1 + K2}
        wmean = tmp("wmean", [P, 1 + K1 + K2 + K3])
        cols = tmp("cols", [P, 9])
        bc = tmp("bc", [P, 3])
        h0 = [tmp(f"h0_{i}", [P, 2, H0], F32R) for i in range(2)]
        h1 = tmp("h1", [P, 2, G, L1 + 2 * PAD2], F32R)
        h2 = tmp("h2", [P, 2, G, L2 + 2 * PAD3], F32R)
        y = [tmp(f"y{i}", [P, BANK]) for i in range(2)]
        sq = [tmp(f"sq{i}", [P, BANK]) for i in range(2)]
        NT = BANK // P
        sd = tmp("sd", [P, NT])
        rc = tmp("rc", [P, NT])
        diag = tmp("diag", [P, NT, P])
        yn = [tmp(f"yn{i}", [P, BANK]) for i in range(2)]
        act3 = tmp("act3", [P, BANK])
        pa = ph.enter_context(nc.psum_tensor("pa", [P, NQ, BANK], F32))
        pc = ph.enter_context(nc.psum_tensor("pc", [P, 2, BANK], F32))
        pv = ph.enter_context(nc.psum_tensor("pv", [P, NT], F32))
        pr = ph.enter_context(nc.psum_tensor("pr", [P, BANK], F32))

        s_w0, s_wts, s_x = sem("s_w0"), sem("s_wts"), sem("s_x")
        s_prep = sem("s_prep")
        s_w0prep, s_wprep, s_whi = sem("s_w0prep"), sem("s_wprep"), sem("s_whi")
        s_pprep = sem("s_pprep")
        s_a0 = sem("s_a0")
        s_hi0 = sem("s_hi0")
        s_a0free = sem("s_a0free")
        s_halo0 = sem("s_halo0")
        s_z, s_zused = sem("s_z"), sem("s_zused")
        s_v = sem("s_v")
        s_sdx, s_rcx = sem("s_sdx"), sem("s_rcx")
        s_rows, s_tr = sem("s_rows"), sem("s_tr")
        s_xn = sem("s_xn")
        s_split, s_xhi = sem("s_split"), sem("s_xhi")
        s_tile, s_y, s_sq, s_var = sem("s_tile"), sem("s_y"), sem("s_sq"), sem("s_var")
        s_sd, s_rc, s_diag, s_bc, s_yn = sem("s_sd"), sem("s_rc"), sem("s_diag"), sem("s_bc"), sem("s_yn")
        s_relu, s_act, s_lo = sem("s_relu"), sem("s_act"), sem("s_lo")
        s_halo = sem("s_halo")
        s_poolmark, s_pemark, s_spmark = sem("s_poolmark"), sem("s_pemark"), sem("s_spmark")

        TILES = [("c1", 0), ("c2", 1), ("c1", 1), ("c3", 0), ("c1", 2), ("c2", 0), ("c1", 3)]
        SLOTS = len(TILES)
        COL = {"c1": (3, 4), "c2": (5, 6), "c3": (7, 8)}
        BIAS = {"c1": 0, "c2": 1, "c3": 2}

        def slots(i):
            if isinstance(i, int) and i == NGRP:
                return [(0, "c2", 1), (1, "c3", 0)]
            return [(t, k, a) for t, (k, a) in enumerate(TILES)
                    if not (isinstance(i, int) and i == 0 and (k, a) in (("c2", 1), ("c3", 0)))]

        def n_of(i, t):
            if isinstance(i, int) and i == 0:
                return {0: 1, 2: 2, 4: 3, 5: 4, 6: 5}[t]
            if isinstance(i, int) and i == NGRP:
                return SLOTS * NGRP - 1 + t
            return i * SLOTS + (t - 1)

        def n12_of(i, t):
            if isinstance(i, int) and i == 0:
                return n_of(i, t)
            if isinstance(i, int) and i == NGRP:
                return (SLOTS - 1) * NGRP
            return i * (SLOTS - 1) + (t - (1 if t >= 3 else 0))

        def bank_of(i, u, t):
            if isinstance(i, int):
                return (n_of(i, t) - 1) % 2
            return (u + t) % 2

        def prev(i, t):
            at = [x[0] for x in slots(i)].index(t)
            if at > 0:
                return (i,) + slots(i)[at - 1]
            if isinstance(i, int) and i == 0:
                return None
            return (i - 1, SLOTS - 1) + TILES[-1]

        def set_at(i, t):
            if TILES[t][0] != "c1":
                return None
            s = TILES[t][1] + 1
            if s == G and isinstance(i, int) and i == NGRP - 1:
                return None
            return i * G + s, s % 2, s == G

        def first_after(i, t, at):
            return t == min(x[0] for x in slots(i) if x[0] >= at)

        def ahead(i):
            return not isinstance(i, int) or i + 2 < NGRP

        def iterations(eng, body):
            body(0, 0)
            body(1, 1)
            with eng.Fori(1, NGRP // 2 - 1) as pair:
                for u in range(2):
                    body(pair * 2 + u, u)
            body(NGRP - 2, 0)
            body(NGRP - 1, 1)

        def part_of(kind, part, which):
            if kind == "c1":
                return h1[:, which, part, PAD2:PAD2 + L1]
            return h2[:, which, 2 * part:2 * part + 2, PAD3:PAD3 + L2]

        def shaped(kind, ap):
            return ap if kind != "c2" else ap.rearrange("p (b n) -> p b n", b=2)

        block = ph.enter_context(nc.Block())

        @block.sync
        def _(sp):
            sp.dma_start(xw[0][:, :], d["x"][:, 0, :]).then_inc(s_x, 16)
            for t, n in ((w0, "w0"), (wmask, "wmask"), (ident, "ident"), (cols, "cols"), (n0bw, "n0bw"),
                         (rowsel, "rowsel")):
                sp.dma_start(t[:, :], d[n]).then_inc(s_w0, 16)
            sp.dma_start(n0w[:, :], d["n0w"].partition_broadcast(P)).then_inc(s_w0, 16)
            sp.dma_start(xw[1][:, :], d["x"][:, 1, :]).then_inc(s_x, 16)
            sp.dma_start(w[:, 0:K1, :], d["w1"]).then_inc(s_wts, 16)
            sp.dma_start(w[:, K1:K1 + K2, :], d["w2"]).then_inc(s_wts, 16)
            sp.dma_start(w[:, K1 + K2:, :], d["w3"]).then_inc(s_wts, 16)
            wts.load(sp, d, MLP_KEPT + MLP_RAW, wts.s_mlp)
            with sp.Fori(0, NGRP // 2 - 1) as pair:
                for u in range(2):
                    sp.wait_ge(s_split, pair * 2 + (u + 1))
                    mark(sp, s_spmark)
                    sp.wait_ge(s_z, pair * 2 + (u + 2))
                    sp.dma_start(xw[u][:, :], d["x"][:, bass.ds(pair * 2 + (u + 2), 1), :].rearrange("p a n -> p (a n)")).then_inc(s_x, 16)

        @block.gpsimd
        def _(pool):
            def edges0(m, buf):
                pool.wait_ge(s_a0free, (m + 1) * NQ)
                mark(pool, s_poolmark)
                h = h0[buf]
                for to, at in ((0, 4), (1, 3), (H0 - 2, H0 - 4), (H0 - 1, H0 - 5)):
                    pool.tensor_copy(h[:, :, to:to + 1], h[:, :, at:at + 1]).then_inc(s_halo0, 1)

            def edges(i, t, kind, part):
                pool.wait_ge(s_lo, n12_of(i, t))
                mark(pool, s_poolmark)
                if kind == "c1":
                    v, e = h1[:, :, part, :], L1 + 2 * PAD2
                    pool.tensor_copy(v[:, :, 0:1], v[:, :, 2:3])
                    pool.tensor_copy(v[:, :, e - 1:e], v[:, :, e - 3:e - 2]).then_inc(s_halo, 1)
                else:
                    v, e = h2[:, :, 2 * part:2 * part + 2, :], L2 + 2 * PAD3
                    pool.tensor_copy(v[:, :, :, 0:1], v[:, :, :, 2:3])
                    pool.tensor_copy(v[:, :, :, e - 1:e], v[:, :, :, e - 3:e - 2]).then_inc(s_halo, 1)

            def spread(g):
                pool.wait_ge(s_rcx, g + 1)
                if not isinstance(g, int) or g > 0:
                    pool.wait_ge(s_tr, g)
                mark(pool, s_poolmark)
                pool.tensor_copy(rows[:, :, 0:WROWS - 1], rcx[:, :].unsqueeze(2).broadcast_to((P, NX * JW, WROWS - 1))).then_inc(s_rows, 1)

            def split(g, u):
                pool.wait_ge(s_xn, g + 1)
                if not isinstance(g, int) or g >= 2:
                    pool.wait_ge(s_a0, (g - 1) * (G * NQ))
                mark(pool, s_poolmark)
                pool.tensor_copy(xs[u][:, HI, :], xw[u][:, :]).then_inc(s_xhi, 1)
                pool.wait_ge(s_xhi, g + 1)
                mark(pool, s_poolmark)
                pool.tensor_tensor(xs[u][:, LO, :], xw[u][:, :], xs[u][:, HI, :].bitcast(F32), ALU.subtract).then_inc(s_split, 1)

            def body(i, u):
                for t, kind, part in slots(i):
                    if set_at(i, t):
                        edges0(set_at(i, t)[0], set_at(i, t)[1])
                    before = prev(i, t)
                    if before and before[2] != "c3":
                        edges(*before)
                    if ahead(i) and first_after(i, t, 3):
                        spread(i + 2)
                if ahead(i):
                    split(i + 2, u)
            pool.memset(rows[:, :, WROWS - 1:WROWS], 1.0)
            for g in range(2):
                spread(g)
                split(g, g)
            edges0(0, 0)
            iterations(pool, body)
            edges(*prev(NGRP, 0))
            edges(*prev(NGRP, 1))

        @block.tensor
        def _(pe):
            pe.wait_ge(s_prep, 3)
            pe.transpose(pa[:, 0, 0:P], w0[:, :], ident[:, :]).then_inc(s_pprep, 1)
            pe.wait_ge(s_prep, 4)
            pe.matmul(pa[:, 1, 0:P], w0T[:, :], w0T[:, :], start=True, stop=True).then_inc(s_pprep, 1)
            pe.matmul(pa[:, 2, 0:3], onesm[:, :], cols[:, 0:3], start=True, stop=True).then_inc(s_pprep, 1)

            def stat_z(g, u, sets):
                pe.wait_ge(s_x, (g + 1) * 16)
                if sets is not None:
                    pe.wait_ge(s_a0free, sets)
                for hf in range(2):
                    m = pe.matmul(pa[:, hf, :], gram[:, :], xw[u][:, hf * BANK:(hf + 1) * BANK], start=True, stop=True)
                m.then_inc(s_z, 1)

            def stat_v(g, sets):
                pe.wait_ge(s_zused, g + 1)
                if sets is not None:
                    pe.wait_ge(s_a0free, sets)
                for x in range(NX):
                    m = pe.matmul(pa[:, 0, x * JW:(x + 1) * JW], prod[:, x * P:(x + 1) * P], selv[:, :], start=True, stop=True)
                m.then_inc(s_v, 1)

            def stat_t(g, sets):
                pe.wait_ge(s_rows, g + 1)
                if sets is not None:
                    pe.wait_ge(s_a0free, sets)
                mark(pe, s_pemark)
                for x in range(NX):
                    m = pe.transpose(pa[:, x // NT, (x % NT) * P:(x % NT + 1) * P],
                                     rows[:, x * JW:(x + 1) * JW, :].rearrange("p j r -> p (j r)"), ident[:, :])
                m.then_inc(s_tr, 1)

            def conv0(m, gp, s):
                x = xs[gp][:, :, s * CH0:(s + 1) * CH0]
                for q in range(NQ):
                    if not isinstance(m, int) or m > 0:
                        pe.wait_ge(s_a0free, m * NQ + (q + 1 - NQ))
                    for j in range(2):
                        for k, (a, b) in enumerate(PASSES):
                            mm = pe.matmul(pa[:, q, j * CH0:(j + 1) * CH0], w0s[:, a, 2 * q + j, :], x[:, b, :],
                                           start=(k == 0), stop=(k == 2))
                    mm.then_inc(s_a0, 1)

            def var(n, b):
                pe.wait_ge(s_sq, n)
                if not isinstance(n, int) or n > 1:
                    pe.wait_ge(s_sd, n - 1)
                for x in range(NT):
                    m = pe.matmul(pv[:, x:x + 1], sq[b][:, x * P:(x + 1) * P], vcol[:, :], start=True, stop=True)
                m.then_inc(s_var, 1)

            def spread(n):
                pe.wait_ge(s_diag, n)
                if not isinstance(n, int) or n > 1:
                    pe.wait_ge(s_yn, n - 1)
                pe.matmul(pr[:, :], ones[:, :], diag[:, :, :].rearrange("p x c -> p (x c)"), start=True, stop=True).then_inc(s_bc, 1)

            def tile(i, u, t, kind, part, var_at=None, spread_at=None):
                n, b = n_of(i, t), bank_of(i, u, t)
                if not isinstance(n, int) or n > 2:
                    pe.wait_ge(s_y, n - 2)
                if kind == "c1":
                    pe.wait_ge(s_halo0, (i * G + (part + 1)) * 4)
                    src = [h0[part % 2][:, :, k:k + S1 * (L1 - 1) + 1:S1] for k in range(K1)]
                elif kind == "c2":
                    pe.wait_ge(s_halo, n12_of(i, 2) if part == 0 else n12_of(i - 1, 6))
                    src = [h1[:, :, 2 * part:2 * part + 2, k:k + S2 * (L2 - 1) + 1:S2] for k in range(K2)]
                else:
                    pe.wait_ge(s_halo, (SLOTS - 1) * NGRP if isinstance(i, int) and i == NGRP else n12_of(i, 1))
                    src = [h2[:, :, :, k:k + S3 * (L3 - 1) + 1:S3] for k in range(K3)]
                total = len(PASSES) * taps[kind]
                for at in range(total):
                    if at == var_at and prev(i, t):
                        var(n - 1, 1 - b)
                    if at == spread_at and prev(i, t):
                        spread(n - 1)
                    (a, c), k = PASSES[at // taps[kind]], at % taps[kind]
                    m = pe.matmul(pc[:, b, :], ws[:, a, first_tap[kind] + k, :], src[k][:, c], start=(at == 0), stop=(at == total - 1))
                m.then_inc(s_tile, 1)
                if spread_at == total:
                    spread(n - 1)

            def body(i, u):
                for t, kind, part in slots(i):
                    s = set_at(i, t)
                    if s:
                        m, _, nxt = s
                        if nxt:
                            pe.wait_ge(s_split, i + 2)
                        if ahead(i) and part == 1:
                            pe.wait_ge(s_zused, i + 3)
                        if ahead(i) and part == 2:
                            pe.wait_ge(s_sdx, i + 3)
                        if ahead(i) and part == 3:
                            pe.wait_ge(s_xn, i + 3)
                        conv0(m, 1 - u if nxt else u, 0 if nxt else part + 1)
                    total = len(PASSES) * taps[kind]
                    var_at, spread_at = (0, 13) if s else (5, 12)
                    tile(i, u, t, kind, part, var_at, spread_at)
                    if ahead(i) and (kind, part) == ("c1", 0):
                        stat_z(i + 2, u, (i * G + 2) * NQ)
                    if ahead(i) and (kind, part) == ("c1", 1):
                        stat_v(i + 2, (i * G + 3) * NQ)
                    if ahead(i) and (kind, part) == ("c1", 2):
                        stat_t(i + 2, (i * G + 4) * NQ)

            pe.wait_ge(s_prep, 5)
            for g in range(2):
                stat_z(g, g, None)
                stat_v(g, None)
                pe.wait_ge(s_sdx, g + 1)
                stat_t(g, None)
                pe.wait_ge(s_xn, g + 1)
            pe.wait_ge(s_w0prep, 3 * JW)
            pe.wait_ge(s_split, 1)
            conv0(0, 0, 0)
            pe.wait_ge(s_wprep, 4)
            iterations(pe, body)
            n = n_of(NGRP, 0)
            var(n - 1, n % 2)
            spread(n - 1)
            tile(NGRP, 0, 0, "c2", 1)
            var(n, (n - 1) % 2)
            spread(n)
            tile(NGRP, 0, 1, "c3", 0)
            var(n + 1, n % 2)
            spread(n + 1)

        @block.scalar
        def _(act):
            def deviation_x(g):
                act.wait_ge(s_v, g + 1)
                if not isinstance(g, int) or g > 0:
                    act.wait_ge(s_rcx, g)
                act.activation(sdx[:, :], pa[:, 0, 0:NX * JW], ACT.Sqrt, bias=epsc[:, 0:1]).then_inc(s_sdx, 1)

            def take0(m, buf):
                for q in range(NQ):
                    act.wait_ge(s_a0, m * NQ + (q + 1))
                    j = 2 * q + PAD1
                    dst = h0[buf][:, HI, PAD1:PAD1 + L0].rearrange("p (n j) -> p j n", j=JW)[:, 2 * q:2 * q + 2, :]
                    act.activation(dst, pa[:, q, :].rearrange("p (j n) -> p j n", j=2), ACT.Relu).then_inc(s_hi0, 1)

            def square(n, b, kind):
                act.wait_ge(s_tile, n)
                if not isinstance(n, int) or n > 2:
                    act.wait_ge(s_var, n - 2)
                act.activation(sq[b][:, :], pc[:, b, :], ACT.Square, bias=bc[:, BIAS[kind]:BIAS[kind] + 1]).then_inc(s_sq, 1)

            def deviation(n):
                act.wait_ge(s_var, n)
                if not isinstance(n, int) or n > 1:
                    act.wait_ge(s_rc, n - 1)
                act.activation(sd[:, :], pv[:, :], ACT.Sqrt, bias=epsc[:, 0:1]).then_inc(s_sd, 1)

            def relu(i, t, kind, part, n, b):
                if kind == "c3":
                    return
                act.wait_ge(s_yn, n)
                act.activation(part_of(kind, part, HI), shaped(kind, yn[b][:, :]), ACT.Relu,
                               bias=cols[:, COL[kind][1]:COL[kind][1] + 1]).then_inc(s_relu, 1)

            def body(i, u):
                for t, kind, part in slots(i):
                    n, b = n_of(i, t), bank_of(i, u, t)
                    before = prev(i, t)
                    if ahead(i) and first_after(i, t, 3):
                        deviation_x(i + 2)
                    if set_at(i, t):
                        take0(set_at(i, t)[0], set_at(i, t)[1])
                    if before:
                        deviation(n - 1)
                    if before and kind == "c1":
                        relu(*before, n - 1, 1 - b)
                    square(n, b, kind)
                    if before and kind != "c1":
                        relu(*before, n - 1, 1 - b)

            act.wait_ge(s_w0, 7 * 16)
            act.wait_ge(s_prep, 1)
            deviation_x(0)
            deviation_x(1)
            take0(0, 0)
            iterations(act, body)
            for t, kind, part in slots(NGRP):
                n, b = n_of(NGRP, t), bank_of(NGRP, 0, t)
                deviation(n - 1)
                relu(*prev(NGRP, t), n - 1, 1 - b)
                square(n, b, kind)
            deviation(n)

        @block.vector
        def _(dve):
            done = {}

            def prep(ins, sem=s_prep):
                ins.then_inc(sem, 1)
                done[sem.name] = done.get(sem.name, 0) + 1
                dve.wait_ge(sem, done[sem.name])

            dve.memset(ones[:, :], 1.0)
            dve.memset(vcol[:, :], 1.0 / (C - 1))
            dve.memset(onesm[:, :], 1.0 / C)
            dve.memset(epsc[:, :], EPS)
            dve.wait_ge(s_w0, 7 * 16)
            prep(dve.tensor_reduce(wmean[:, 0:1], w0[:, :], AX.X, ALU.add))
            prep(dve.tensor_scalar(wmean[:, 0:1], wmean[:, 0:1], 1.0 / C, None, ALU.mult))
            prep(dve.tensor_scalar(w0[:, :], w0[:, :], wmean[:, 0:1], None, ALU.subtract))
            dve.wait_ge(s_pprep, 1)
            prep(dve.tensor_copy(w0T[:, :], pa[:, 0, 0:P]))
            dve.wait_ge(s_pprep, 3)
            dve.tensor_tensor(gram[:, :], pa[:, 1, 0:P], wmask[:, :], ALU.mult)
            dve.tensor_scalar(selv[:, :], rowsel[:, :], 1.0 / (C - 1), None, ALU.mult)
            dve.tensor_tensor(bc[:, :], cols[:, 0:3], pa[:, 2, 0:3], ALU.subtract)
            prep(dve.tensor_tensor(w0[:, :], w0[:, :], n0w[:, :], ALU.mult))

            def products(g, u):
                dve.wait_ge(s_z, g + 1)
                if not isinstance(g, int) or g > 0:
                    dve.wait_ge(s_v, g)
                dve.tensor_tensor(prod[:, :].rearrange("p (a n) -> p a n", a=2), pa[:, 0:2, :],
                                  xw[u][:, :].rearrange("p (a n) -> p a n", a=2), ALU.mult).then_inc(s_zused, 1)

            def inverse_x(g):
                dve.wait_ge(s_sdx, g + 1)
                if not isinstance(g, int) or g > 0:
                    dve.wait_ge(s_rows, g)
                dve.reciprocal(rcx[:, :], sdx[:, :]).then_inc(s_rcx, 1)

            def normalise_x(g, u):
                dve.wait_ge(s_tr, g + 1)
                x = xw[u][:, :].rearrange("p (a n) -> p a n", a=2)
                dve.tensor_tensor(x, pa[:, 0:2, :], x, ALU.mult).then_inc(s_xn, 1)

            def take0(m, buf):
                for q in range(NQ):
                    dve.wait_ge(s_hi0, m * NQ + (q + 1))
                    hi, lo = (h0[buf][:, a, PAD1:PAD1 + L0].rearrange("p (n j) -> p j n", j=JW)[:, 2 * q:2 * q + 2, :]
                              for a in (HI, LO))
                    dve.scalar_tensor_tensor(lo, pa[:, q, :].rearrange("p (j n) -> p j n", j=2), 0.0, hi.bitcast(F32),
                                             ALU.max, ALU.subtract).then_inc(s_a0free, 1)

            def inverse(n):
                dve.wait_ge(s_sd, n)
                dve.reciprocal(rc[:, :], sd[:, :]).then_inc(s_rc, 1)
                dve.wait_ge(s_rc, n)
                blocks = (P, NT, P)
                dve.tensor_tensor(diag[:, :, :], ident[:, :].unsqueeze(1).broadcast_to(blocks),
                                  rc[:, :].unsqueeze(2).broadcast_to(blocks), ALU.mult).then_inc(s_diag, 1)

            def centre(n, b, kind):
                dve.wait_ge(s_sq, n)
                dve.tensor_scalar(y[b][:, :], pc[:, b, :], bc[:, BIAS[kind]:BIAS[kind] + 1], None, ALU.add).then_inc(s_y, 1)

            def normalise(i, t, kind, part, n, b):
                dve.wait_ge(s_bc, n)
                two = prev(i, t) and prev(*prev(i, t)[:2])
                if two:
                    dve.wait_ge(s_relu, n12_of(two[0], two[1]))
                g = COL[kind][0]
                dve.scalar_tensor_tensor(yn[b][:, :], y[b][:, :], cols[:, g:g + 1], pr[:, :], ALU.mult,
                                         ALU.mult).then_inc(s_yn, 1)

            def finish(i, t, kind, part, n, b):
                dve.wait_ge(s_yn, n)
                bias = cols[:, COL[kind][1]:COL[kind][1] + 1]
                if kind == "c3":
                    dst = feat[:, (i - 1) * G * T:i * G * T] if isinstance(i, int) else feat[:, bass.ds((i - 1) * (G * T), G * T)]
                    dve.tensor_scalar(dst, yn[b][:, :], bias, 0.0, ALU.add, ALU.max)
                    return
                ge(dve, s_lo, n12_of(i, t) - 1)
                dve.tensor_scalar(act3[:, :], yn[b][:, :], bias, 0.0, ALU.add, ALU.max).then_inc(s_act, 1)
                dve.wait_ge(s_act, n12_of(i, t))
                dve.wait_ge(s_relu, n12_of(i, t))
                dve.tensor_tensor(part_of(kind, part, LO), shaped(kind, act3[:, :]), part_of(kind, part, HI).bitcast(F32),
                                  ALU.subtract).then_inc(s_lo, 1)

            def windows(i, u, t):
                if ahead(i) and first_after(i, t, 1):
                    products(i + 2, u)
                if ahead(i) and first_after(i, t, 3):
                    inverse_x(i + 2)
                if ahead(i) and t == 5:
                    normalise_x(i + 2, u)

            def body(i, u):
                for t, kind, part in slots(i):
                    n, b = n_of(i, t), bank_of(i, u, t)
                    before = prev(i, t)
                    windows(i, u, t)
                    if set_at(i, t):
                        take0(set_at(i, t)[0], set_at(i, t)[1])
                    if before:
                        inverse(n - 1)
                    if kind != "c1":
                        centre(n, b, kind)
                    if before:
                        normalise(*before, n - 1, 1 - b)
                        finish(*before, n - 1, 1 - b)
                    if kind == "c1":
                        centre(n, b, kind)

            products(0, 0)
            inverse_x(0)
            for j in range(JW):
                prep(dve.scalar_tensor_tensor(w0f[:, :], w0[:, :], rowsel[:, j:j + 1], n0bw[:, :], ALU.mult, ALU.add), s_w0prep)
                prep(dve.tensor_copy(w0s[:, HI, j, :], w0f[:, :]), s_w0prep)
                prep(dve.tensor_tensor(w0s[:, LO, j, :], w0f[:, :], w0s[:, HI, j, :].bitcast(F32), ALU.subtract), s_w0prep)
            normalise_x(0, 0)
            products(1, 1)
            inverse_x(1)
            normalise_x(1, 1)
            dve.wait_ge(s_wts, 3 * 16)
            m = wmean[:, 1:]
            prep(dve.tensor_reduce(m, w[:, :, :], AX.X, ALU.add), s_wprep)
            prep(dve.tensor_scalar(m, m, 1.0 / C, None, ALU.mult), s_wprep)
            prep(dve.tensor_tensor(w[:, :, :], w[:, :, :], m.unsqueeze(2).broadcast_to((P, K1 + K2 + K3, C)), ALU.subtract), s_wprep)
            dve.tensor_copy(ws[:, HI, :, :], w[:, :, :]).then_inc(s_whi, 1)
            dve.wait_ge(s_whi, 1)
            prep(dve.tensor_tensor(ws[:, LO, :, :], w[:, :, :], ws[:, HI, :, :].bitcast(F32), ALU.subtract), s_wprep)
            take0(0, 0)
            iterations(dve, body)
            for t, kind, part in slots(NGRP):
                n, b = n_of(NGRP, t), bank_of(NGRP, 0, t)
                inverse(n - 1)
                normalise(*prev(NGRP, t), n - 1, 1 - b)
                finish(*prev(NGRP, t), n - 1, 1 - b)
                centre(n, b, kind)
            inverse(n)
            normalise(NGRP, t, kind, part, n, b)
            finish(NGRP, t, kind, part, n, b)


def mlp_phase(nc, sem, d, wts, feat, imp):
    HI, LO = 0, 1
    PASSES = ((HI, HI), (HI, LO), (LO, HI))
    DM = DMLP
    KT = DM // P
    NT = B * T // BANK
    BT = BANK // T
    with ExitStack() as ph:
        def tmp(name, shape, dt=F32):
            return ph.enter_context(nc.sbuf_tensor("ml_" + name, shape, dt))

        w1, w2, w3, b12, b3 = (wts["mlp_" + n] for n in ("w1", "w2", "w3", "b12", "b3"))
        w1s = tmp("w1s", [P, 2, DM], F32R)
        w2s = tmp("w2s", [P, 2, KT, DM], F32R)
        fs = [tmp(f"fs{i}", [P, 2, BANK], F32R) for i in range(2)]
        z1 = tmp("z1", [P, KT, BANK])
        z1s = [tmp(f"z1s{i}", [P, 2, KT, BANK], F32R) for i in range(2)]
        z2 = [tmp(f"z2_{i}", [P, KT, BANK]) for i in range(2)]
        acc = [tmp(f"acc{i}", [P, BANK]) for i in range(2)]
        ones = tmp("ones", [P, 1])
        p1 = ph.enter_context(nc.psum_tensor("ml_p1", [P, 2, BANK], F32))
        p2 = ph.enter_context(nc.psum_tensor("ml_p2", [P, KT, BANK], F32))
        p3 = ph.enter_context(nc.psum_tensor("ml_p3", [P, B], F32))
        s_m1, s_g1 = sem("ml_m1"), sem("ml_g1")
        s_m2, s_g2 = sem("ml_m2"), sem("ml_g2")
        s_acc = sem("ml_acc")
        s_m3, s_sig = sem("ml_m3"), sem("ml_sig")
        s_whi, s_ws = sem("ml_whi"), sem("ml_ws")
        s_fhi, s_fs = sem("ml_fhi"), sem("ml_fs")
        s_zhi, s_zs = sem("ml_zhi"), sem("ml_zs")
        block = ph.enter_context(nc.Block())

        @block.sync
        def _(sp):
            sp.wait_ge(s_ws, 2)
            wts.load(sp, d, LATER, wts.s_later)

        @block.tensor
        def _(pe):
            wts.wait_mlp(pe)
            pe.wait_ge(s_ws, 2)

            def body(it, r, has):
                c = it * 2 + r
                if has(0):
                    for m in range(KT):
                        ge(pe, s_g1, c * KT + (m - 1))
                        if m == 0:
                            pe.wait_ge(s_fs, c + 1)
                        for i, (a, b) in enumerate(PASSES):
                            m1 = pe.matmul(p1[:, m % 2, :], w1s[:, a, m * P:(m + 1) * P], fs[r % 2][:, b, :], start=(i == 0), stop=(i == 2))
                        m1.then_inc(s_m1, 1)
                if has(2):
                    pe.wait_ge(s_acc, (c - 1) * KT)
                    for q in range(BT):
                        col = (c - 2) * BT + q
                        out = p3[:, col:col + 1] if isinstance(col, int) else p3[:, bass.ds(col, 1)]
                        m3 = pe.matmul(out, acc[r % 2][:, q * T:(q + 1) * T], ones[:, :], start=True, stop=True)
                    m3.then_inc(s_m3, 1)
                if has(1):
                    ge(pe, s_zs, c * KT)
                    for m in range(KT):
                        ge(pe, s_g2, (c - 2) * KT + (m + 1))
                        for i, (a, b) in enumerate(PASSES):
                            for k in range(KT):
                                m2 = pe.matmul(p2[:, m, :], w2s[:, a, k, m * P:(m + 1) * P], z1s[1 - r % 2][:, b, k, :],
                                               start=(i == 0 and k == 0), stop=(i == 2 and k == KT - 1))
                        m2.then_inc(s_m2, 1)
            steps(pe, NT, 2, 2, body)

        @block.scalar
        def _(act):
            wts.wait_mlp(act)

            def body(it, r, has):
                c = it * 2 + r
                for m in range(KT):
                    if has(0):
                        act.wait_ge(s_m1, c * KT + (m + 1))
                        ge(act, s_zs, (c - 1) * KT + (m + 1))
                        act.activation(z1[:, m, :], p1[:, m % 2, :], ACT.Gelu, bias=b12[:, 0, m:m + 1]).then_inc(s_g1, 1)
                for m in range(KT):
                    if has(1):
                        act.wait_ge(s_m2, (c - 1) * KT + (m + 1))
                        if m == 0:
                            ge(act, s_acc, (c - 2) * KT)
                        act.activation(z2[1 - r % 2][:, m, :], p2[:, m, :], ACT.Gelu, bias=b12[:, 1, m:m + 1]).then_inc(s_g2, 1)
            steps(act, NT, 2, 2, body)
            act.wait_ge(s_m3, NT)
            act.activation(imp[:, :], p3[:, :], ACT.Sigmoid, bias=b3[:, 0:1]).then_inc(s_sig, 1)

        @block.vector
        def _(dve):
            wts.wait_mlp(dve)
            dve.memset(ones[:, :], 1.0)
            dve.tensor_copy(w1s[:, HI, :], w1[:, :]).then_inc(s_whi, 1)
            dve.tensor_copy(w2s[:, HI, :, :], w2[:, :, :]).then_inc(s_whi, 1)
            dve.wait_ge(s_whi, 2)
            dve.tensor_tensor(w1s[:, LO, :], w1[:, :], w1s[:, HI, :].bitcast(F32), ALU.subtract).then_inc(s_ws, 1)
            dve.tensor_tensor(w2s[:, LO, :, :], w2[:, :, :], w2s[:, HI, :, :].bitcast(F32), ALU.subtract).then_inc(s_ws, 1)

            def body(it, r, has):
                c = it * 2 + r
                if has(0):
                    ge(dve, s_m1, (c - 1) * KT)
                    f = feat[:, c * BANK:(c + 1) * BANK] if isinstance(c, int) else feat[:, bass.ds(c * BANK, BANK)]
                    dve.tensor_copy(fs[r % 2][:, HI, :], f).then_inc(s_fhi, 1)
                    dve.wait_ge(s_fhi, c + 1)
                    dve.tensor_tensor(fs[r % 2][:, LO, :], f, fs[r % 2][:, HI, :].bitcast(F32), ALU.subtract).then_inc(s_fs, 1)
                for m in range(KT):
                    if has(2):
                        dve.wait_ge(s_g2, (c - 2) * KT + (m + 1))
                        if m == 0:
                            ge(dve, s_m3, c - 3)
                            dve.tensor_scalar(acc[r % 2][:, :], z2[r % 2][:, m, :], w3[:, m:m + 1], None, ALU.mult).then_inc(s_acc, 1)
                        else:
                            dve.wait_ge(s_acc, (c - 2) * KT + m)
                            dve.scalar_tensor_tensor(acc[r % 2][:, :], z2[r % 2][:, m, :], w3[:, m:m + 1], acc[r % 2][:, :],
                                                     ALU.mult, ALU.add).then_inc(s_acc, 1)
                    if has(1):
                        dve.wait_ge(s_g1, (c - 1) * KT + (m + 1))
                        if m == 0:
                            ge(dve, s_m2, (c - 2) * KT)
                        z = z1s[1 - r % 2]
                        dve.tensor_copy(z[:, HI, m, :], z1[:, m, :]).then_inc(s_zhi, 1)
                        dve.wait_ge(s_zhi, (c - 1) * KT + (m + 1))
                        dve.tensor_tensor(z[:, LO, m, :], z1[:, m, :], z[:, HI, m, :].bitcast(F32), ALU.subtract).then_inc(s_zs, 1)
            steps(dve, NT, 2, 2, body)


def pool_phase(nc, sem, wts, feat, imp, tok):
    NB = BANK // TN
    NT = B // NB
    with ExitStack() as ph:
        def tmp(name, shape, dt=F32):
            return ph.enter_context(nc.sbuf_tensor("po_" + name, shape, dt))

        ident, upto, before, centre, iota, gb = (wts[n] for n in ("ident", "upto", "before", "centre", "iota", "n4"))
        one = tmp("one", [P, P])
        epsc = tmp("epsc", [P, 1])
        rsum = tmp("rsum", [P, B])
        cs = tmp("cs", [P, 2, B])
        share = [tmp(f"share{i}", [P, NB, TN]) for i in range(2)]
        wm = [tmp(f"wm{i}", [P, NB, TN]) for i in range(2)]
        XB = BANK // P
        vcol = tmp("vcol", [P, 1])
        sd, rc = tmp("sd", [P, XB]), tmp("rc", [P, XB])
        diag = tmp("diag", [P, XB, P])
        fin = [tmp(f"fin{i}", [P, NB * T]) for i in range(2)]
        fT = [tmp(f"fT{i}", [P, NB * T]) for i in range(2)]
        pooled, cen, sq, yn = ([tmp(f"{n}{i}", [P, BANK]) for i in range(2)] for n in ("pooled", "cen", "sq", "yn"))
        pt = ph.enter_context(nc.psum_tensor("po_pt", [P, NB * T], F32))
        pp = ph.enter_context(nc.psum_tensor("po_pp", [P, BANK], F32))
        py = ph.enter_context(nc.psum_tensor("po_py", [P, 2, BANK], F32))
        pv = ph.enter_context(nc.psum_tensor("po_pv", [P, XB], F32))
        pr = ph.enter_context(nc.psum_tensor("po_pr", [P, BANK], F32))
        s_imp, s_sum = sem("po_imp"), sem("po_sum")
        s_fin, s_t, s_fT = sem("po_fin"), sem("po_t"), sem("po_fT")
        s_pool, s_pooled, s_cen, s_sq = sem("po_pool"), sem("po_pooled"), sem("po_cen"), sem("po_sq")
        s_var, s_dev, s_rec, s_norm, s_relu = (sem("po_" + n) for n in ("var", "dev", "rec", "norm", "relu"))
        s_cev = sem("po_cev")
        s_x, s_share, s_wm, s_diag, s_sp = (sem("po_" + n) for n in ("x", "share", "wm", "diag", "sp"))
        block = ph.enter_context(nc.Block())

        @block.gpsimd
        def _(pool):
            wts.wait(pool)
            pool.wait_ge(s_rec, 1)
            for j in range(NT):
                if j >= 2:
                    pool.wait_ge(s_pool, j - 1)
                for a in range(2):
                    ge(pool, s_wm, j)
                    pool.tensor_tensor(share[a][:, :, :], cs[:, a, j * NB:(j + 1) * NB].unsqueeze(2).broadcast_to((P, NB, TN)),
                                       iota[:, 0:TN].unsqueeze(1).broadcast_to((P, NB, TN)), ALU.subtract).then_inc(s_x, 1)
                    pool.wait_ge(s_x, 2 * j + a + 1)
                    inner = share[a][:, :, 0:TN - 1]
                    pool.tensor_scalar(inner, inner, 0.0, 1.0, ALU.max, ALU.min).then_inc(s_share, 1)
                    outer = share[a][:, :, TN - 1:TN]
                    pool.tensor_scalar(outer, outer, 0.0, None, ALU.max).then_inc(s_share, 1)
                pool.wait_ge(s_share, 4 * (j + 1))
                pool.tensor_tensor(wm[j % 2][:, :, :], share[0][:, :, :], share[1][:, :, :], ALU.subtract).then_inc(s_wm, 1)

        @block.tensor
        def _(pe):
            wts.wait(pe)
            pe.wait_ge(s_imp, 1)
            pe.matmul(pr[:, 0:B], one[:, :], imp[:, :], start=True, stop=True).then_inc(s_sum, 1)
            pe.wait_ge(s_imp, 3)
            pe.matmul(pp[:, 0:B], upto[:, :], imp[:, :], start=True, stop=True)
            pe.matmul(pp[:, B:2 * B], before[:, :], imp[:, :], start=True, stop=True).then_inc(s_sum, 1)

            def body(it, r, has):
                j = it * 2 + r
                if has(4):
                    pe.wait_ge(s_diag, j - 3)
                    ge(pe, s_norm, j - 4)
                    pe.matmul(pr[:, :], one[:, :], diag[:, :, :].rearrange("p x c -> p (x c)"), start=True, stop=True).then_inc(s_sp, 1)
                if has(3):
                    ge(pe, s_sq, j - 2)
                    ge(pe, s_dev, j - 3)
                    for x in range(XB):
                        m = pe.matmul(pv[:, x:x + 1], sq[1 - r][:, x * P:(x + 1) * P], vcol[:, :], start=True, stop=True)
                    m.then_inc(s_var, 1)
                if has(0):
                    pe.wait_ge(s_fin, j + 1)
                    ge(pe, s_fT, j)
                    for q in range(NB):
                        m = pe.transpose(pt[:, q * T:(q + 1) * T], fin[r][:, q * T:(q + 1) * T], ident[:, :])
                    m.then_inc(s_t, 1)
                if has(1):
                    ge(pe, s_fT, j)
                    pe.wait_ge(s_wm, j)
                    ge(pe, s_pooled, j - 1)
                    for q in range(NB):
                        m = pe.matmul(pp[:, q * TN:(q + 1) * TN], fT[1 - r][:, q * T:(q + 1) * T], wm[1 - r][:, q, :],
                                      start=True, stop=True)
                    m.then_inc(s_pool, 1)
                if has(2):
                    ge(pe, s_pooled, j - 1)
                    ge(pe, s_cev, j - 3)
                    pe.matmul(py[:, r, :], centre[:, :], pooled[r][:, :], start=True, stop=True).then_inc(s_cen, 1)
            steps(pe, NT, 4, 2, body)

        @block.scalar
        def _(act):
            wts.wait(act)

            def body(it, r, has):
                j = it * 2 + r
                if has(0):
                    ge(act, s_t, j - 1)
                    v = j * NB * T
                    src = feat[:, v:v + NB * T] if isinstance(v, int) else feat[:, bass.ds(v, NB * T)]
                    act.activation(fin[r][:, :], src, ACT.Copy).then_inc(s_fin, 1)
                if has(3):
                    act.wait_ge(s_var, j - 2)
                    ge(act, s_diag, j - 3)
                    act.activation(sd[:, :], pv[:, :], ACT.Sqrt, bias=epsc[:, 0:1]).then_inc(s_dev, 1)
                if has(4):
                    act.wait_ge(s_norm, j - 3)
                    v = (j - 4) * NB
                    dst = tok[:, v:v + NB, :] if isinstance(v, int) else tok[:, bass.ds(v, NB), :]
                    act.activation(dst, yn[r][:, :].rearrange("p (b n) -> p b n", n=TN), ACT.Relu, bias=gb[:, 1:2],
                                   scale=gb[:, 0:1]).then_inc(s_relu, 1)
                if has(2):
                    act.wait_ge(s_cen, j - 1)
                    ge(act, s_var, j - 3)
                    act.activation(sq[r][:, :], py[:, r, :], ACT.Square).then_inc(s_sq, 1)
            act.wait_ge(s_imp, 1)
            steps(act, NT, 4, 2, body)

        @block.vector
        def _(dve):
            dve.memset(vcol[:, :], 1.0 / (C - 1))
            dve.memset(one[:, :], 1.0)
            dve.memset(epsc[:, :], EPS)
            dve.tensor_scalar(imp[:, :], imp[:, :], 1e-5, None, ALU.add).then_inc(s_imp, 1)
            dve.wait_ge(s_sum, 1)
            dve.reciprocal(rsum[:, :], pr[:, 0:B]).then_inc(s_imp, 1)
            dve.wait_ge(s_imp, 2)
            dve.scalar_tensor_tensor(imp[:, :], imp[:, :], float(TN), rsum[:, :], ALU.mult, ALU.mult).then_inc(s_imp, 1)
            dve.wait_ge(s_sum, 2)
            wts.wait(dve)
            dve.tensor_copy(cs[:, :, :], pp[:, 0:2 * B].rearrange("p (a b) -> p a b", a=2)).then_inc(s_rec, 1)
            dve.wait_ge(s_rec, 1)
            def body(it, r, has):
                j = it * 2 + r
                if has(3):
                    dve.wait_ge(s_sq, j - 2)
                    ge(dve, s_norm, j - 4)
                    dve.tensor_copy(cen[1 - r][:, :], py[:, 1 - r, :]).then_inc(s_cev, 1)
                if has(4):
                    dve.wait_ge(s_cev, j - 3)
                    dve.wait_ge(s_sp, j - 3)
                    ge(dve, s_relu, j - 5)
                    dve.tensor_tensor(yn[r][:, :], cen[r][:, :], pr[:, :], ALU.mult).then_inc(s_norm, 1)
                if has(3):
                    dve.wait_ge(s_dev, j - 2)
                    dve.reciprocal(rc[:, :], sd[:, :]).then_inc(s_rec, 1)
                    dve.wait_ge(s_rec, j - 1)
                    ge(dve, s_sp, j - 3)
                    dve.tensor_tensor(diag[:, :, :], ident.unsqueeze(1).broadcast_to((P, XB, P)),
                                      rc[:, :].unsqueeze(2).broadcast_to((P, XB, P)), ALU.mult).then_inc(s_diag, 1)
                if has(0):
                    dve.wait_ge(s_t, j + 1)
                    ge(dve, s_pool, j - 1)
                    dve.tensor_copy(fT[r][:, :], pt[:, :]).then_inc(s_fT, 1)
                if has(1):
                    dve.wait_ge(s_pool, j)
                    ge(dve, s_cen, j - 2)
                    dve.tensor_copy(pooled[1 - r][:, :], pp[:, :]).then_inc(s_pooled, 1)
            steps(dve, NT, 4, 2, body)


def layernorm(dve, act, s_v, s_a, count, x, out, work, stat, groups, width, eps):
    xv, ov, wv = x, out, work

    def bc(a):
        return a.unsqueeze(2).broadcast_to((P, groups, width))

    def vector():
        dve.tensor_reduce(stat[:, 0, 0:groups], xv, AX.X, ALU.add).then_inc(s_v, 1)
        dve.wait_ge(s_v, count + 1)
        dve.tensor_scalar(stat[:, 0, 0:groups], stat[:, 0, 0:groups], 1.0 / width, None, ALU.mult).then_inc(s_v, 1)
        dve.wait_ge(s_v, count + 2)
        dve.tensor_tensor(ov, xv, bc(stat[:, 0, 0:groups]), ALU.subtract).then_inc(s_v, 1)
        dve.wait_ge(s_a, count // 5 * 2 + 1)
        dve.tensor_reduce(stat[:, 1, 0:groups], wv, AX.X, ALU.add).then_inc(s_v, 1)
        dve.wait_ge(s_a, count // 5 * 2 + 2)
        dve.reciprocal(stat[:, 1, 0:groups], stat[:, 1, 0:groups]).then_inc(s_v, 1)
        dve.wait_ge(s_v, count + 5)
        return dve.tensor_tensor(ov, ov, bc(stat[:, 1, 0:groups]), ALU.mult)

    def scalar():
        act.wait_ge(s_v, count + 3)
        act.activation(wv, ov, ACT.Square).then_inc(s_a, 1)
        act.wait_ge(s_v, count + 4)
        act.activation(stat[:, 1, 0:groups], stat[:, 1, 0:groups], ACT.Sqrt, bias=eps, scale=1.0 / width).then_inc(s_a, 1)
    return vector, scalar


D = TN
H1, R1 = 8, 32
NH, NE, DH = 4, 4, 16


def norm_phase(nc, sem, name, tok, xn):
    with ExitStack() as ph:
        work = ph.enter_context(nc.sbuf_tensor(name + "_work", [P, B, D], F32))
        stat = ph.enter_context(nc.sbuf_tensor(name + "_stat", [P, 2, B], F32))
        epsc = ph.enter_context(nc.sbuf_tensor(name + "_eps", [P, 1], F32))
        s_v, s_a = sem(name + "_v"), sem(name + "_a")
        block = ph.enter_context(nc.Block())
        v, a = layernorm(nc.vector, nc.scalar, s_v, s_a, 0, tok[:, :, :], xn[:, :, 0:D], work[:, :, :], stat, B, D, epsc[:, 0:1])

        @block.vector
        def _(dve):
            dve.memset(epsc[:, :], EPS)
            if xn.shape[2] > D:
                dve.memset(xn[:, :, D:D + 1], 1.0)
            v().then_inc(s_v, 1)

        @block.scalar
        def _(act):
            a()


def attn_phase(nc, sem, wts, xn, tok):
    GB = BANK // P
    NG = B // GB
    HB = P // R1
    HG = H1 // HB
    QP = 1 + 2 * HG
    SCALE = 1.0 / float(np.sqrt(D))
    with ExitStack() as ph:
        def tmp(name, shape, dt=F32):
            return ph.enter_context(nc.sbuf_tensor("at_" + name, shape, dt))

        def bank(name, shape):
            return ph.enter_context(nc.psum_tensor("at_" + name, shape, F32))

        ident, wqk, vo = wts["ident"], wts["wqk"], wts["vo"]
        xs = tmp("xs", [P, GB, D])
        xT = tmp("xT", [D, BANK])
        qT = [tmp(f"qT{i}", [P, HG, BANK]) for i in range(2)]
        kT = [tmp(f"kT{i}", [P, HG, HB, BANK]) for i in range(2)]
        mx = tmp("mx", [P, 2, H1])
        ex = [tmp(f"ex{i}", [P, HG, HB, P]) for i in range(2)]
        exT = [tmp(f"exT{i}", [P, HG, HB, P]) for i in range(2)]
        rs = tmp("rs", [P, 2, H1])
        cx = [tmp(f"cx{i}", [P, H1, D]) for i in range(2)]
        cxT = tmp("cxT", [P, 4, P])
        pS = bank("pS", [P, HG, BANK])
        pT = bank("pT", [P, HG, BANK])
        pO = bank("pO", [P, HG, BANK])
        pM = bank("pM", [P, BANK])
        pR = bank("pR", [P, D])
        s_zero, s_xs, s_q, s_qev = (sem("at_" + n) for n in ("zero", "xs", "q", "qev"))
        s_pemark, s_poolmark = sem("at_pemark"), sem("at_poolmark")
        s_s, s_max, s_sub, s_exp, s_t, s_ev = (sem("at_" + n) for n in ("s", "max", "sub", "exp", "t", "ev"))
        s_pv, s_rs, s_ctx, s_ct, s_cev, s_pr, s_add = (sem("at_" + n) for n in ("pv", "rs", "ctx", "ct", "cev", "pr", "add"))
        PIECES = {(0, 1): 0, (1, 0): 1, (1, 1): 2, (2, 1): 3, (3, 0): 4}
        block = ph.enter_context(nc.Block())

        def before(it, r, slot):
            g = it * 2 + r // GB
            if isinstance(g, int) and g >= NG - 1:
                return QP * NG
            return (g + 1) * QP + sum(1 for at in PIECES if at < (r % GB, slot))

        def piece_at(it, r, slot):
            g = it * 2 + r // GB
            if isinstance(g, int) and g >= NG - 1:
                return None
            return PIECES.get((r % GB, slot))

        @block.gpsimd
        def _(pool):
            pool.tensor_copy(xs[:, :, :], xn[:, 0:GB, 0:D]).then_inc(s_xs, 1)
            with pool.Fori(1, NG) as g:
                pool.wait_ge(s_q, g * QP - (QP - 1))
                mark(pool, s_poolmark)
                pool.tensor_copy(xs[:, :, :], xn[:, bass.ds(g * GB, GB), 0:D]).then_inc(s_xs, 1)

        @block.tensor
        def _(pe):
            wts.wait(pe)

            def piece(g, k):
                if k == 0:
                    pe.wait_ge(s_xs, g + 1)
                    ge(pe, s_qev, g * QP)
                    mark(pe, s_pemark)
                    for b in range(GB):
                        m = pe.transpose(pM[0:D, b * P:(b + 1) * P], xs[:, b, :], ident[:, :])
                else:
                    pe.wait_ge(s_qev, g * QP + k)
                    m = pe.matmul(pM[:, :], wqk[:, k - 1, :], xT[:, :], start=True, stop=True)
                m.then_inc(s_q, 1)

            for k in range(QP):
                piece(0, k)

            def body(it, r, has):
                j, g, b4, gp = it * 8 + r, it * 2 + r // GB, r % GB, r // GB
                cols = slice(b4 * P, b4 * P + P)
                for hg in range(HG):
                    if has(0):
                        if b4 == 0 and hg == 0:
                            pe.wait_ge(s_qev, (g + 1) * QP)
                        ge(pe, s_sub, j * HG + (hg - 1))
                        pe.matmul(pS[:, hg, :], qT[gp][:, hg, cols], kT[gp][:, hg, :, cols],
                                  start=True, stop=True).then_inc(s_s, 1)
                    if has(1):
                        pe.wait_ge(s_exp, j * HG + (hg - 1))
                        ge(pe, s_ev, j * HG + (hg - 3))
                        for i in range(HB):
                            m = pe.transpose(pT[:, hg, i * P:(i + 1) * P], ex[1 - r % 2][:, hg, i, :], ident[:, :])
                        m.then_inc(s_t, 1)
                    if hg == 0 and has(3):
                        pe.wait_ge(s_ctx, j - 2)
                        pe.wait_ge(s_qev, before(it, r, 0))
                        for k in range(4):
                            m = pe.transpose(pM[:, k * P:(k + 1) * P], cx[1 - r % 2][:, 2 * k:2 * k + 2, :].rearrange("p a n -> p (a n)"), ident[:, :])
                        m.then_inc(s_ct, 1)
                    if hg == 0 and has(2):
                        pe.wait_ge(s_ev, (j - 1) * HG)
                        ge(pe, s_ctx, j - 2)
                        b = j - 2
                        rhs = xn[:, b, :] if isinstance(b, int) else xn[:, bass.ds(b, 1), :].rearrange("p a n -> p (a n)")
                        for h in range(H1):
                            at = (h % HB) * (D + 1)
                            m = pe.matmul(pO[:, h // HB, at:at + D + 1], exT[r % 2][:, h // HB, h % HB, :], rhs,
                                          start=True, stop=True)
                        m.then_inc(s_pv, 1)
                    if has(0) and piece_at(it, r, hg) is not None:
                        ge(pe, s_cev, j - 2)
                        piece(g + 1, piece_at(it, r, hg))
                    if hg == 1 and has(3):
                        pe.wait_ge(s_cev, j - 2)
                        ge(pe, s_add, j - 3)
                        for k in range(4):
                            m = pe.matmul(pR[:, :], cxT[:, k, :], vo[:, k, :], start=(k == 0), stop=(k == 3))
                        m.then_inc(s_pr, 1)
            steps(pe, B, 3, 8, body)

        @block.scalar
        def _(act):
            def take(g, k, gp):
                act.wait_ge(s_q, g * QP + (k + 1))
                if k == 0:
                    act.activation(xT[:, :], pM[0:D, :], ACT.Copy).then_inc(s_qev, 1)
                elif k <= HG:
                    act.activation(qT[gp][:, k - 1, :], pM[:, :], ACT.Copy).then_inc(s_qev, 1)
                else:
                    if isinstance(g, int) and g == 0:
                        act.wait_ge(s_zero, 1)
                    for i in range(HB):
                        rows = slice(R1 * i, R1 * i + R1)
                        m = act.activation(kT[gp][rows, k - 1 - HG, i, :], pM[rows, :], ACT.Copy)
                    m.then_inc(s_qev, 1)

            for k in range(QP):
                take(0, k, 0)
            act.wait_ge(s_zero, 2)

            def exp(j, hg, buf):
                act.wait_ge(s_sub, j * HG + (hg + 1))
                e = ex[buf][:, hg, :, :]
                act.activation(e, e, ACT.Exp, scale=SCALE).then_inc(s_exp, 1)

            def body(it, r, has):
                j, g, gp = it * 8 + r, it * 2 + r // GB, r // GB
                for hg in range(HG):
                    if has(1):
                        if hg == 0:
                            exp(j - 1, 1, 1 - r % 2)
                        act.wait_ge(s_t, j * HG + (hg - 1))
                        ge(act, s_pv, j - 2)
                        act.activation(exT[1 - r % 2][:, hg, :, :], pT[:, hg, :].rearrange("p (i t) -> p i t", i=HB),
                                       ACT.Copy).then_inc(s_ev, 1)
                    if hg == 0 and has(3):
                        act.wait_ge(s_ct, j - 2)
                        ge(act, s_pr, j - 3)
                        act.activation(cxT[:, :, :], pM[:, :].rearrange("p (k t) -> p k t", k=4), ACT.Copy).then_inc(s_cev, 1)
                    if has(0) and hg == 1:
                        exp(j, 0, r % 2)
                    if has(0) and piece_at(it, r, hg) is not None:
                        take(g + 1, piece_at(it, r, hg), 1 - gp)
            steps(act, B, 3, 8, body)

        @block.vector
        def _(dve):
            for i in range(2):
                dve.memset(kT[i][:, :, :, :], 0.0).then_inc(s_zero, 1)

            def body(it, r, has):
                j = it * 8 + r
                for hg in range(HG):
                    if has(0):
                        dve.wait_ge(s_s, j * HG + (hg + 1))
                        sc = pS[:, hg, :].rearrange("p (i u) -> p i u", i=HB)
                        m = mx[:, r % 2, HB * hg:HB * (hg + 1)]
                        dve.tensor_reduce(m, sc, AX.X, ALU.max).then_inc(s_max, 1)
                        dve.wait_ge(s_max, j * HG + (hg + 1))
                        ge(dve, s_t, j * HG + (hg - 3))
                        dve.tensor_tensor(ex[r % 2][:, hg, :, :], sc, m.unsqueeze(2).broadcast_to((P, HB, P)),
                                          ALU.subtract).then_inc(s_sub, 1)
                    if hg == 0 and has(2):
                        dve.wait_ge(s_pv, j - 1)
                        o = pO[:, :, 0:HB * (D + 1)].rearrange("p h (i e) -> p h i e", i=HB)
                        q = rs[:, r % 2, :].rearrange("p (h i) -> p h i", h=HG)
                        dve.reciprocal(q, o[:, :, :, D:D + 1].rearrange("p h i e -> p h (i e)")).then_inc(s_rs, 1)
                        dve.wait_ge(s_rs, j - 1)
                        ge(dve, s_ct, j - 3)
                        dve.tensor_tensor(cx[r % 2][:, :, :].rearrange("p (h i) e -> p h i e", h=HG), o[:, :, :, 0:D],
                                          q.unsqueeze(3).broadcast_to((P, HG, HB, D)), ALU.mult).then_inc(s_ctx, 1)
                    if hg == 1 and has(3):
                        dve.wait_ge(s_pr, j - 2)
                        b = j - 3
                        t = tok[:, b, :] if isinstance(b, int) else tok[:, bass.ds(b, 1), :].rearrange("p a n -> p (a n)")
                        dve.tensor_tensor(t, t, pR[:, :], ALU.add).then_inc(s_add, 1)
            steps(dve, B, 3, 8, body)


def mix_phase(nc, sem, wts, xn, sxs, fx):
    GB = BANK // P
    NG = B // GB
    QP = 7
    KP = 3
    WHICH = {2: 0, KP: NE, 4: 1, 5: 2, 6: 3}
    LAG = 2 * GB + 3
    HOLD = 320
    SCALE = float(np.sqrt(DH))
    with ExitStack() as ph:
        def tmp(name, shape, dt=F32):
            return ph.enter_context(nc.sbuf_tensor("mx_" + name, shape, dt))

        def bank(name, shape):
            return ph.enter_context(nc.psum_tensor("mx_" + name, shape, F32))

        ident, causal, hlw, hlbc, hlb = (wts[n] for n in ("ident", "causal", "hlw", "hlb_col", "hlb"))
        wqk, wv, gate, gateb = (wts[n] for n in ("ffq", "ffv", "gate", "gateb"))
        identb = tmp("identb", [P, P], BF16)
        causalb = tmp("causalb", [P, NH, P], BF16)
        xs = tmp("xs", [P, GB, D])
        xT = [tmp(f"xT{i}", [D, BANK]) for i in range(2)]
        sxT = [tmp(f"sxT{i}", [D, BANK]) for i in range(2)]
        lorow = wts["lorow"]
        lng, lnb = wts["lng"], wts["lnb"]
        qhi = tmp("qhi", [P, BANK], F32R)
        qT = [tmp(f"qT{i}", [P, NE, BANK], F32R) for i in range(2)]
        kT = [[tmp(f"k{part}{i}", [P, NH, BANK], F32R) for part in ("hi", "lo")] for i in range(2)]
        v1 = [tmp(f"v1_{i}", [P, NH, DH + 1]) for i in range(2)]
        msk = [tmp(f"msk{i}", [P, NH, DH]) for i in range(2)]
        mx = tmp("mx", [P, NE, NH])
        ex = [tmp(f"ex{i}", [P, NE, NH, P]) for i in range(2)]
        exT = [tmp(f"exT{i}", [P, NE, NH, P]) for i in range(2)]
        rs = tmp("rs", [P, NH * NE])
        raw = tmp("raw", [P, NH * NE, DH])
        om = [tmp(f"om{i}", [P, GB, NH * NE * DH]) for i in range(2)]
        lg = [tmp(f"lg{i}", [P, GB, NH * NE]) for i in range(2)]
        GR = GB * NH
        top, tot = tmp("top", [P, GR]), tmp("tot", [P, GR])
        fg, sqs = tmp("fg", [P, GB, D]), tmp("sqs", [P, GB, D])
        mean, istd = tmp("mean", [P, GR]), tmp("istd", [P, GR])
        resid, epsc, zero = tmp("resid", [P, D]), tmp("epsc", [P, 1]), tmp("zero", [P, 1])
        oT = [tmp(f"oT{i}", [P, 2, P]) for i in range(2)]
        pS = bank("pS", [P, NE, BANK])
        pT = bank("pT", [P, 2, NH, P])
        pO = bank("pO", [P, BANK])
        pM = bank("pM", [P, BANK])
        s_zero = sem("mx_zero")
        s_prep, s_xs, s_q, s_qev = (sem("mx_" + n) for n in ("prep", "xs", "q", "qev"))
        s_s, s_max, s_sub, s_exp, s_t, s_ev = (sem("mx_" + n) for n in ("s", "max", "sub", "exp", "t", "ev"))
        s_sv, s_sx, s_svev, s_pv, s_rs, s_raw, s_om = (sem("mx_" + n) for n in ("sv", "sx", "svev", "pv", "rs", "raw", "om"))
        s_pemark, s_poolmark = sem("mx_pemark"), sem("mx_poolmark")
        s_c = sem("mx_c")
        s_qhi = sem("mx_qhi")
        s_e, s_sqs, s_std = sem("mx_e"), sem("mx_sqs"), sem("mx_std")
        LINKS = 16
        s_gt, s_gev, s_gl, s_lg = (sem("mx_" + n) for n in ("gt", "gev", "gl", "lg"))
        PIECES = {(0, 2): 0, (0, 3): 1, (1, 2): 2, (1, 3): 3, (2, 2): 4, (2, 3): 5, (3, 2): 6}
        block = ph.enter_context(nc.Block())

        def before(it, r, slot):
            g = it * 2 + r // GB
            if isinstance(g, int) and g >= NG - 1:
                return QP * NG
            return (g + 1) * QP + sum(1 for at in PIECES if at < (r % GB, slot))

        def piece_at(it, r, slot):
            g = it * 2 + r // GB
            if isinstance(g, int) and g >= NG - 1:
                return None
            return PIECES.get((r % GB, slot))

        def upto(v):
            return min(v, B) if isinstance(v, int) else v

        @block.gpsimd
        def _(pool):
            pool.tensor_copy(xs[:, :, :], xn[:, 0:GB, 0:D]).then_inc(s_xs, 1)

            def body(it, r, has):
                g = it * 2 + r // GB
                if has(0) and r % GB == 0 and piece_at(it, r, 2) is not None:
                    pool.wait_ge(s_q, g * QP + 1)
                    mark(pool, s_poolmark)
                    b = (g + 1) * GB
                    src = xn[:, b:b + GB, 0:D] if isinstance(b, int) else xn[:, bass.ds(b, GB), 0:D]
                    pool.tensor_copy(xs[:, :, :], src).then_inc(s_xs, 1)
            steps(pool, B, LAG, 8, body)

        @block.tensor
        def _(pe):
            wts.wait(pe)
            pe.wait_ge(s_prep, 1)

            def piece(g, k, gp):
                if k == 0:
                    pe.wait_ge(s_xs, g + 1)
                    ge(pe, s_qev, g * QP)
                    mark(pe, s_pemark)
                    for b in range(GB):
                        m = pe.transpose(pM[0:D, b * P:(b + 1) * P], xs[:, b, :], ident[:, :])
                else:
                    pe.wait_ge(s_qev, g * QP + k)
                    mark(pe, s_pemark)
                    if k == 1:
                        m = pe.matmul(pM[0:D, :], hlw[:, :], xT[gp][:, :], start=True, stop=True)
                    else:
                        m = pe.matmul(pM[:, :], wqk[:, WHICH[k], :], sxT[gp][:, :], start=True, stop=True)
                m.then_inc(s_q, 1)

            for k in range(QP):
                piece(0, k, 0)

            def body(it, r, has):
                j, g, b4, gp = it * 8 + r, it * 2 + r // GB, r % GB, r // GB
                cols = slice(b4 * P, b4 * P + P)
                for e in range(NE):
                    if has(0):
                        if b4 == 0 and e == 0:
                            pe.wait_ge(s_qev, (g + 1) * QP)
                        ge(pe, s_sub, j * NE + (e - 3))
                        pe.matmul(pS[:, e, :], identb[:, :], causalb[:, :, :].rearrange("p n u -> p (n u)"),
                                  start=True, stop=False)
                        pe.matmul(pS[:, e, :], qT[gp][:, e, cols], kT[gp][0][:, :, cols], start=False, stop=False)
                        pe.matmul(pS[:, e, :], qT[gp][:, e, cols], kT[gp][1][:, :, cols],
                                  start=False, stop=True).then_inc(s_s, 1)
                    if has(1):
                        pe.wait_ge(s_exp, j * NE + (e - 3))
                        ge(pe, s_ev, j * NE + (e - 5))
                        for n in range(NH):
                            m = pe.transpose(pT[:, e % 2, n, :], ex[1 - r % 2][:, e, n, :], ident[:, :])
                        m.then_inc(s_t, 1)
                    if e == 0 and has(2):
                        pe.wait_ge(s_ev, (j - 1) * NE)
                        pe.wait_ge(s_svev, j - 1)
                        ge(pe, s_lg, j - 4)
                        ge(pe, s_om, j - 2)
                        for h in range(NH * NE):
                            at = h * (DH + 1)
                            m = pe.matmul(pO[:, at:at + DH + 1], exT[r % 2][:, h % NE, h // NE, :], v1[r % 2][:, h // NE, :],
                                          start=True, stop=True)
                        m.then_inc(s_pv, 1)
                    if e == 0 and has(0):
                        pe.wait_ge(s_qev, before(it, r, 0))
                        ge(pe, s_gev, j - 3)
                        pe.matmul(pM[:, 0:D], xT[gp][:, cols], hlw[:, :], start=True, stop=True)
                        pe.matmul(pM[:, D:2 * D], sxT[gp][:, cols], wv[:, :], start=True, stop=True).then_inc(s_sv, 1)
                    if e == 3 and has(4):
                        pe.wait_ge(s_gev, j - 3)
                        pe.wait_ge(s_om, upto(j - 1))
                        ge(pe, s_lg, j - 4)
                        for k in range(2):
                            m = pe.matmul(pO[:, HOLD:HOLD + NH * NE], oT[r % 2][:, k, :], gate[:, k, :], start=(k == 0), stop=(k == 1))
                        m.then_inc(s_gl, 1)
                    if e == 1 and has(3):
                        pe.wait_ge(s_om, j - 2)
                        ge(pe, s_gev, j - 3)
                        pe.wait_ge(s_svev, upto(j + 1))
                        pe.wait_ge(s_qev, before(it, r, 1))
                        for k in range(2):
                            m = pe.transpose(pM[:, k * P:(k + 1) * P], om[(r - 3) // GB % 2][:, (r - 3) % GB, k * P:(k + 1) * P], ident[:, :])
                        m.then_inc(s_gt, 1)
                    if has(0) and piece_at(it, r, e) is not None:
                        ge(pe, s_gev, j - 2)
                        pe.wait_ge(s_svev, j + 1)
                        piece(g + 1, piece_at(it, r, e), 1 - gp)
            steps(pe, B, LAG, 8, body)

        @block.scalar
        def _(act):
            wts.wait(act)

            def take(g, k, gp):
                act.wait_ge(s_q, g * QP + (k + 1))
                if k == 0:
                    act.activation(xT[gp][:, :], pM[0:D, :], ACT.Copy).then_inc(s_qev, 1)
                elif k == 1:
                    act.activation(sxT[gp][:, :], pM[0:D, :], ACT.Identity, bias=hlbc[:, 0:1]).then_inc(s_qev, 1)
                elif k != KP:
                    act.activation(qhi[:, :], pM[:, :], ACT.Copy).then_inc(s_qhi, 1)
                else:
                    if isinstance(g, int) and g == 0:
                        act.wait_ge(s_zero, 2)
                    for n in range(NH):
                        rows = slice(32 * n, 32 * n + 32)
                        m = act.activation(kT[gp][0][rows, n, :], pM[rows, :], ACT.Copy)
                    m.then_inc(s_qhi, 1)

            for k in range(QP):
                take(0, k, 0)
            act.wait_ge(s_zero, 4)

            def exp(j, e, buf):
                act.wait_ge(s_sub, j * NE + (e + 1))
                x = ex[buf][:, e, :, :]
                act.activation(x, x, ACT.Exp, scale=SCALE).then_inc(s_exp, 1)

            def mixture(it, r, has, e):
                if not has(2 * GB + r % GB):
                    return
                at, g, gp = (r % GB, e), it * 2 + r // GB - 2, r // GB
                if at == (0, 3):
                    act.wait_ge(s_c, g * LINKS + 2)
                    act.activation(lg[gp][:, :, :], lg[gp][:, :, :], ACT.Exp).then_inc(s_e, 1)
                if at == (2, 2):
                    act.wait_ge(s_c, g * LINKS + 11)
                    act.activation(sqs[:, :, :], fg[:, :, :], ACT.Square).then_inc(s_sqs, 1)
                if at == (3, 0):
                    act.wait_ge(s_c, g * LINKS + 12)
                    act.activation(istd[:, :], istd[:, :], ACT.Sqrt, bias=epsc[:, 0:1], scale=1.0 / DH).then_inc(s_std, 1)

            def body(it, r, has):
                j, g, gp = it * 8 + r, it * 2 + r // GB, r // GB
                for e in range(NE):
                    if e < 2 and has(1):
                        exp(j - 1, e + 2, 1 - r % 2)
                    if has(1):
                        act.wait_ge(s_t, j * NE + (e - 3))
                        ge(act, s_pv, j - 2)
                        act.activation(exT[1 - r % 2][:, e, :, :], pT[:, e % 2, :, :], ACT.Copy).then_inc(s_ev, 1)
                    if has(0) and piece_at(it, r, e) is not None:
                        take(g + 1, piece_at(it, r, e), 1 - gp)
                    if e >= 2 and has(0):
                        exp(j, e - 2, r % 2)
                    if e == 1 and has(3):
                        act.wait_ge(s_gt, j - 2)
                        ge(act, s_gl, j - 4)
                        act.activation(oT[1 - r % 2][:, :, :], pM[:, 0:2 * P].rearrange("p (k t) -> p k t", k=2), ACT.Copy).then_inc(s_gev, 1)
                    mixture(it, r, has, e)
            steps(act, B, LAG, 8, body)

        @block.vector
        def _(dve):
            for i in range(2):
                dve.memset(v1[i][:, :, DH:DH + 1], 1.0)
            wts.wait(dve)
            dve.tensor_copy(identb[:, :], ident[:, :])
            dve.tensor_copy(causalb[:, :, :], causal[:, :].unsqueeze(1).broadcast_to((P, NH, P))).then_inc(s_prep, 1)
            dve.memset(zero[:, :], 0.0).then_inc(s_prep, 1)
            dve.wait_ge(s_prep, 2)
            for i in range(2):
                for part in range(2):
                    dve.tensor_copy(kT[i][part][:, :, :].rearrange("p n t -> p (n t)"), zero[:, 0:1].broadcast_to((P, NH * BANK))).then_inc(s_zero, 1)
            dve.memset(epsc[:, :], 1e-8)

            def take(g, k, gp):
                if k < 2:
                    return
                dve.wait_ge(s_qhi, g * (QP - 2) + (k - 1))
                if k != KP:
                    dve.scalar_tensor_tensor(qT[gp][:, WHICH[k], :], qhi[:, :].bitcast(F32), lorow[:, 0:1], pM[:, :],
                                             ALU.mult, ALU.add).then_inc(s_qev, 1)
                else:
                    for n in range(NH):
                        rows = slice(32 * n, 32 * n + 32)
                        m = dve.tensor_tensor(kT[gp][1][rows, n, :], pM[rows, :], kT[gp][0][rows, n, :].bitcast(F32), ALU.subtract)
                    m.then_inc(s_qev, 1)

            dve.wait_ge(s_zero, 4)
            for k in range(QP):
                take(0, k, 0)

            def mixture(it, r, has, e):
                if not has(2 * GB + r % GB):
                    return
                at, g, gp = (r % GB, e), it * 2 + r // GB - 2, r // GB
                rows3 = (P, GR, DH)
                lv = lg[gp][:, :, :].rearrange("p b (n e) -> p (b n) e", n=NH)
                ov = om[gp][:, :, :].rearrange("p b (h d) -> p (b h) d", d=DH)
                fv = fg[:, :, :].rearrange("p b (n d) -> p (b n) d", d=DH)
                sv = sqs[:, :, :].rearrange("p b (n d) -> p (b n) d", d=DH)

                def link(k, ins):
                    ins.then_inc(s_c, 1)
                    dve.wait_ge(s_c, g * LINKS + k)

                def over(a, width):
                    return a[:, :].unsqueeze(2).broadcast_to((P, GR, width))

                if at == (0, 1):
                    dve.wait_ge(s_lg, (g + 1) * GB)
                    link(1, dve.tensor_reduce(top[:, :], lv, AX.X, ALU.max))
                    link(2, dve.tensor_tensor(lv, lv, over(top, NE), ALU.subtract))
                if at == (1, 1):
                    dve.wait_ge(s_e, g + 1)
                    link(3, dve.tensor_reduce(tot[:, :], lv, AX.X, ALU.add))
                    link(4, dve.reciprocal(tot[:, :], tot[:, :]))
                    link(5, dve.tensor_tensor(lv, lv, over(tot, NE), ALU.mult))
                if at == (1, 2):
                    dve.wait_ge(s_om, (g + 1) * GB)
                    w = lv.rearrange("p g e -> p (g e)").unsqueeze(2).broadcast_to((P, GR * NE, DH))
                    link(6, dve.tensor_tensor(ov, ov, w, ALU.mult))
                if at == (1, 3):
                    link(7, dve.tensor_reduce(fv, ov.rearrange("p (g e) d -> p g d e", e=NE), AX.X, ALU.add))
                if at == (2, 1):
                    link(8, dve.tensor_tensor(fg[:, :, :], fg[:, :, :], resid[:, :].unsqueeze(1).broadcast_to((P, GB, D)), ALU.add))
                    link(9, dve.tensor_reduce(mean[:, :], fv, AX.X, ALU.add))
                    link(10, dve.tensor_scalar(mean[:, :], mean[:, :], 1.0 / DH, None, ALU.mult))
                    link(11, dve.tensor_tensor(fv, fv, over(mean, DH), ALU.subtract))
                if at == (2, 3):
                    dve.wait_ge(s_sqs, g + 1)
                    link(12, dve.tensor_reduce(istd[:, :], sv, AX.X, ALU.add))
                if at == (3, 1):
                    dve.wait_ge(s_std, g + 1)
                    link(13, dve.reciprocal(istd[:, :], istd[:, :]))
                    link(14, dve.tensor_tensor(fv, fv, over(istd, DH), ALU.mult))
                    link(15, dve.tensor_tensor(fv, fv, lng.unsqueeze(1).broadcast_to(rows3), ALU.mult))
                    b = g * GB
                    dst = fx[:, b:b + GB, 0:D] if isinstance(b, int) else fx[:, bass.ds(b, GB), 0:D]
                    dst = dst.rearrange("p b (n d) -> p b n d", d=DH)
                    link(16, dve.tensor_tensor(dst, fg[:, :, :].rearrange("p b (n d) -> p b n d", d=DH),
                                               lnb.unsqueeze(1).unsqueeze(1).broadcast_to((P, GB, NH, DH)), ALU.add))

            def body(it, r, has):
                j = it * 8 + r
                for e in range(NE):
                    if has(0):
                        dve.wait_ge(s_s, j * NE + (e + 1))
                        sc = pS[:, e, :].rearrange("p (n u) -> p n u", n=NH)
                        dve.tensor_reduce(mx[:, e, :], sc, AX.X, ALU.max).then_inc(s_max, 1)
                        dve.wait_ge(s_max, j * NE + (e + 1))
                        ge(dve, s_t, j * NE + (e - 7))
                        dve.tensor_tensor(ex[r % 2][:, e, :, :], sc, mx[:, e, :].unsqueeze(2).broadcast_to((P, NH, P)),
                                          ALU.subtract).then_inc(s_sub, 1)
                    if e == 0 and has(2):
                        dve.wait_ge(s_pv, j - 1)
                        o = pO[:, 0:NH * NE * (DH + 1)].rearrange("p (h e) -> p h e", h=NH * NE)
                        dve.reciprocal(rs[:, :], o[:, :, DH:DH + 1].rearrange("p h e -> p (h e)")).then_inc(s_rs, 1)
                        dve.wait_ge(s_rs, j - 1)
                        dve.tensor_tensor(raw[:, :, :], o[:, :, 0:DH], rs[:, :].unsqueeze(2).broadcast_to((P, NH * NE, DH)), ALU.mult).then_inc(s_raw, 1)
                        dve.wait_ge(s_raw, j - 1)
                        ge(dve, s_gt, j - 9)
                        dve.tensor_tensor(om[(r - 2) // GB % 2][:, (r - 2) % GB, :].rearrange("p (n e d) -> p n e d", n=NH, e=NE), raw[:, :, :].rearrange("p (n e) d -> p n e d", n=NH),
                                          msk[r % 2][:, :, :].unsqueeze(2).broadcast_to((P, NH, NE, DH)), ALU.mult).then_inc(s_om, 1)
                    if e == 0 and has(0):
                        dve.wait_ge(s_sv, j + 1)
                        sx = sxs[:, j, :] if isinstance(j, int) else sxs[:, bass.ds(j, 1), :].rearrange("p a n -> p (a n)")
                        dve.tensor_tensor(sx, pM[:, 0:D], hlb[:, :], ALU.add).then_inc(s_sx, 1)
                        dve.tensor_copy(v1[r % 2][:, :, 0:DH], pM[:, D:2 * D].rearrange("p (n o) -> p n o", n=NH))
                        dve.wait_ge(s_sx, j + 1)
                        dve.tensor_scalar(msk[r % 2][:, :, :].rearrange("p n o -> p (n o)"), sx, 0.0, None, ALU.not_equal).then_inc(s_svev, 1)
                    if e == 3 and has(4):
                        dve.wait_ge(s_gl, j - 3)
                        dve.tensor_tensor(lg[(r - 4) // GB % 2][:, (r - 4) % GB, :], pO[:, HOLD:HOLD + NH * NE], gateb[:, :], ALU.add).then_inc(s_lg, 1)
                    if has(0) and piece_at(it, r, e) is not None:
                        take(it * 2 + r // GB + 1, piece_at(it, r, e), 1 - r // GB)
                    if isinstance(j, int) and (j, e) == (GB, 0):
                        dve.wait_ge(s_sx, GB)
                        for n in range(NH):
                            dve.tensor_copy(resid[:, n * DH:(n + 1) * DH], sxs[:, n, n * DH:(n + 1) * DH])
                    mixture(it, r, has, e)
            steps(dve, B, LAG, 8, body)


def gain_bias(x, g, b):
    shape = (P, B * NH, DH)
    v = x.rearrange("p b (n d) -> p (b n) d", d=DH)
    return (lambda dve: dve.tensor_tensor(v, v, g[:, :].unsqueeze(1).broadcast_to(shape), ALU.mult),
            lambda dve: dve.tensor_tensor(v, v, b[:, :].unsqueeze(1).broadcast_to(shape), ALU.add))


def token_phase(nc, sem, name, wts, src, out, two, dram=None):
    GB = BANK // P
    NT = B // GB
    WO = D if two else NH
    with ExitStack() as ph:
        def tmp(n, shape):
            return ph.enter_context(nc.sbuf_tensor(name + n, shape, F32))

        def bank(n, shape):
            return ph.enter_context(nc.psum_tensor(name + n, shape, F32))
        ident, wa, ba, wb = wts["ident"], wts["fc1"], wts["fc1b"], wts["fc2" if two else "fgate"]
        bb = wts["fc2b"]
        GR = GB * NH
        mean = tmp("mean", [P, GR])
        hid = tmp("hid", [P, GB, D])
        lg = [tmp(f"lg{i}", [P, GB, NH]) for i in range(2)]
        top, tot = tmp("top", [P, GB]), tmp("tot", [P, GB])
        xs, fT, msk, hr, hT = ([tmp(f"{n}{i}", [P if n == "xs" else D, GB * D if n == "xs" else BANK]) for i in range(2)]
                               for n in ("xs", "fT", "msk", "hr", "hT"))
        pX, pH, pY = bank("pX", [D, 2, BANK]), bank("pH", [D, 2, BANK]), bank("pY", [P, 2, BANK])
        s_xs, s_t, s_fT, s_msk, s_h, s_hr, s_hT, s_y, s_out = (
            sem(name + n) for n in ("xs", "t", "fTs", "msks", "h", "hrs", "hTs", "y", "out"))
        block = ph.enter_context(nc.Block())
        s_pemark, s_poolmark = sem(name + "pemark"), sem(name + "poolmark")
        rhs_in, s_in = (hT, s_hT) if two else (fT, s_fT)
        s_c = sem(name + "c")
        s_top, s_e, s_tok, s_dma = sem(name + "top"), sem(name + "e"), sem(name + "tok"), sem(name + "dma")
        DEEP = 2
        LAG = 2 if two else 1

        if not two:
            @block.sync
            def _(sp):
                rows = dram.rearrange("b c n -> c b n")
                for j in range(NT):
                    sp.wait_ge(s_tok, j + 1)
                    sp.dma_start(rows[:, j * GB:(j + 1) * GB, :], out[:, j * GB:(j + 1) * GB, :]).then_inc(s_dma, 16)
                sp.wait_ge(s_dma, 16 * NT)

        @block.gpsimd
        def _(pool):
            def body(it, r, has):
                j = it * 2 + r
                if has(0):
                    ge(pool, s_t, j - 1)
                    mark(pool, s_poolmark)
                    v = j * GB
                    part = src[:, v:v + GB, :] if isinstance(v, int) else src[:, bass.ds(v, GB), :]
                    pool.tensor_copy(xs[r][:, :].rearrange("p (b n) -> p b n", b=GB), part).then_inc(s_xs, 1)
            steps(pool, NT, DEEP, 2, body)

        @block.tensor
        def _(pe):
            wts.wait(pe)

            def body(it, r, has):
                j = it * 2 + r
                if has(0):
                    pe.wait_ge(s_xs, j + 1)
                    ge(pe, s_fT, j - 1)
                    mark(pe, s_pemark)
                    for b in range(GB):
                        m = pe.transpose(pX[:, r, b * P:(b + 1) * P], xs[r][:, b * D:(b + 1) * D], ident[:, :])
                    m.then_inc(s_t, 1)
                if two and has(1):
                    pe.wait_ge(s_fT, j)
                    ge(pe, s_hr, j - 2)
                    mark(pe, s_pemark)
                    pe.matmul(pH[:, 1 - r, :], wa[:, :], fT[1 - r][:, :], start=True, stop=True).then_inc(s_h, 1)
                if has(LAG):
                    u = (r - LAG) % 2
                    pe.wait_ge(s_in, j - (LAG - 1))
                    ge(pe, s_out, j - (LAG + 1))
                    for b in range(GB):
                        m = pe.matmul(pY[:, u, b * WO:(b + 1) * WO], rhs_in[u][:, b * P:(b + 1) * P], wb[:, :],
                                      start=True, stop=True)
                    m.then_inc(s_y, 1)
            steps(pe, NT, DEEP, 2, body)

        @block.scalar
        def _(act):
            wts.wait(act)

            def body(it, r, has):
                j = it * 2 + r
                if has(0):
                    act.wait_ge(s_t, j + 1)
                    if two:
                        ge(act, s_h, j - 1)
                        ge(act, s_msk, j - 1)
                    else:
                        ge(act, s_y, j - 1)
                    act.activation(fT[r][:, :], pX[:, r, :], ACT.Copy).then_inc(s_fT, 1)
                if two and has(1):
                    act.wait_ge(s_h, j)
                    ge(act, s_hT, j - 2)
                    act.activation(hr[1 - r][:, :], pH[:, 1 - r, :], ACT.Relu, bias=ba[:, 0:1]).then_inc(s_hr, 1)
                if not two and has(1):
                    act.wait_ge(s_out, j)
                    act.activation(lg[1 - r][:, :, :], lg[1 - r][:, :, :], ACT.Exp).then_inc(s_e, 1)
            steps(act, NT, DEEP, 2, body)

        @block.vector
        def _(dve):
            wts.wait(dve)

            def body(it, r, has):
                j = it * 2 + r
                if two and has(0):
                    dve.wait_ge(s_fT, j + 1)
                    ge(dve, s_hT, j - 1)
                    dve.tensor_scalar(msk[r][:, :], fT[r][:, :], 0.0, None, ALU.not_equal).then_inc(s_msk, 1)
                if two and has(1):
                    dve.wait_ge(s_hr, j)
                    dve.wait_ge(s_msk, j)
                    ge(dve, s_y, j - 2)
                    dve.tensor_tensor(hT[1 - r][:, :], hr[1 - r][:, :], msk[1 - r][:, :], ALU.mult).then_inc(s_hT, 1)
                def at(t, lag):
                    v = (j - lag) * GB
                    return t[:, v:v + GB, :] if isinstance(v, int) else t[:, bass.ds(v, GB), :]

                def link(ins, count):
                    ins.then_inc(s_c, 1)
                    dve.wait_ge(s_c, count)

                if two and has(2):
                    dve.wait_ge(s_y, j - 1)
                    h, x, done = hid[:, :, :], at(src, 2), (j - 2) * 5
                    hv = h.rearrange("p b (n d) -> p b n d", d=DH)
                    ov = at(out, 2).rearrange("p b (n d) -> p b n d", d=DH)
                    dve.tensor_tensor(h, pY[:, r, 0:GB * WO].rearrange("p (b n) -> p b n", b=GB),
                                      bb.unsqueeze(1).broadcast_to((P, GB, WO)), ALU.add).then_inc(s_out, 1)
                    dve.wait_ge(s_out, j - 1)
                    link(dve.scalar_tensor_tensor(h, x, 0.0, h, ALU.not_equal, ALU.mult), done + 1)
                    link(dve.tensor_tensor(h, h, x, ALU.add), done + 2)
                    link(dve.tensor_reduce(mean[:, :].rearrange("p (b n) -> p b n", n=NH), hv, AX.X, ALU.add), done + 3)
                    link(dve.tensor_scalar(mean[:, :], mean[:, :], 1.0 / DH, None, ALU.mult), done + 4)
                    link(dve.tensor_tensor(ov, hv, mean[:, :].rearrange("p (b n) -> p b n", n=NH).unsqueeze(3).broadcast_to((P, GB, NH, DH)),
                                           ALU.subtract), done + 5)
                if not two and has(1):
                    dve.wait_ge(s_y, j)
                    y = pY[:, 1 - r, 0:GB * NH].rearrange("p (b n) -> p b n", b=GB)
                    ge(dve, s_out, j - 1)
                    dve.tensor_reduce(top[:, :], y, AX.X, ALU.max).then_inc(s_top, 1)
                    dve.wait_ge(s_top, j)
                    dve.tensor_tensor(lg[1 - r][:, :, :], y, top[:, :].unsqueeze(2).broadcast_to((P, GB, NH)), ALU.subtract).then_inc(s_out, 1)
                if not two and has(2):
                    dve.wait_ge(s_e, j - 1)
                    e, done = lg[r][:, :, :], (j - 2) * 4
                    x, t = at(src, 2), at(out, 2)
                    xv = x.rearrange("p b (n d) -> p b n d", d=DH)
                    link(dve.tensor_reduce(tot[:, :], e, AX.X, ALU.add), done + 1)
                    link(dve.reciprocal(tot[:, :], tot[:, :]), done + 2)
                    link(dve.tensor_tensor(e, e, tot[:, :].unsqueeze(2).broadcast_to((P, GB, NH)), ALU.mult), done + 3)
                    link(dve.tensor_tensor(xv, xv, e.unsqueeze(3).broadcast_to((P, GB, NH, DH)), ALU.mult), done + 4)
                    dve.tensor_tensor(t, t, x, ALU.add).then_inc(s_tok, 1)
            steps(dve, NT, DEEP, 2, body)


def hidden_phase(nc, sem, wts, hx):
    GR = B * NH
    with ExitStack() as ph:
        def tmp(name, shape):
            return ph.enter_context(nc.sbuf_tensor("hi_" + name, shape, F32))
        epsc = tmp("eps", [P, 1])
        work = tmp("work", [P, B, D])
        istd = tmp("istd", [P, GR])
        s_c, s_a = sem("hi_c"), sem("hi_a")
        block = ph.enter_context(nc.Block())
        hv = hx[:, :, :].rearrange("p b (n d) -> p (b n) d", d=DH)
        wv = work[:, :, :].rearrange("p b (n d) -> p (b n) d", d=DH)
        HALF = GR // 2

        @block.scalar
        def _(act):
            for i in range(2):
                rows = slice(i * HALF, (i + 1) * HALF)
                act.activation(wv[:, rows, :], hv[:, rows, :], ACT.Square).then_inc(s_a, 1)
            act.wait_ge(s_c, 3)
            act.activation(istd[:, :], istd[:, :], ACT.Sqrt, bias=epsc[:, 0:1], scale=1.0 / DH).then_inc(s_a, 1)

        @block.vector
        def _(dve):
            wts.wait(dve)
            dve.memset(epsc[:, :], 1e-8).then_inc(s_c, 1)
            for i in range(2):
                rows = slice(i * HALF, (i + 1) * HALF)
                dve.wait_ge(s_a, i + 1)
                dve.tensor_reduce(istd[:, rows], wv[:, rows, :], AX.X, ALU.add).then_inc(s_c, 1)
            dve.wait_ge(s_a, 3)
            dve.reciprocal(istd[:, :], istd[:, :]).then_inc(s_c, 1)
            dve.wait_ge(s_c, 4)
            dve.tensor_tensor(hv, hv, istd[:, :].unsqueeze(2).broadcast_to((P, GR, DH)), ALU.mult).then_inc(s_c, 1)
            mul, add = gain_bias(hx[:, :, :], wts["fng"], wts["fnb"])
            dve.wait_ge(s_c, 5)
            mul(dve).then_inc(s_c, 1)
            dve.wait_ge(s_c, 6)
            add(dve).then_inc(s_c, 1)


def ffn_all(nc, sem, wts, tok, out):
    with ExitStack() as ph:
        def buf(name, shape):
            return ph.enter_context(nc.sbuf_tensor("f_" + name, shape, F32))
        xn = buf("xn", [P, B, D])
        sxs = buf("sxs", [P, B, D])
        norm_phase(nc, sem, "n2", tok, xn)
        mix_phase(nc, sem, wts, xn, sxs, xn)
        token_phase(nc, sem, "fc_", wts, xn, sxs, True)
        hidden_phase(nc, sem, wts, sxs)
        token_phase(nc, sem, "fg_", wts, sxs, tok, False, out)


def window_layout(x):
    xp = np.pad(x[:, 0, :], ((0, 0), (PAD0, PAD0)), mode="reflect")
    rows = np.zeros((P, NGRP, GX), dtype=x.dtype)
    for j in range(JW):
        for k in range(K0):
            first = j * S0 + k
            v = xp[:, first:first + JW * S0 * (CH0 - 1) + 1:JW * S0]
            rows[WROWS * j + k] = v.reshape(NGRP, GX)
        rows[WROWS * j + K0] = 1.0
    rows[ONE] = 1.0
    return rows


def conv0_layout(w, b):
    out = np.zeros((P, C), dtype=w.dtype)
    for j in range(JW):
        out[WROWS * j:WROWS * j + K0] = w[:, 0, :].T
        out[WROWS * j + K0] = b
    return out


def window_masks():
    m = np.zeros((P, P), dtype=np.float32)
    sel = np.zeros((P, JW), dtype=np.float32)
    for j in range(JW):
        r = slice(WROWS * j, WROWS * j + WIN)
        m[r, r] = 1.0
        sel[r, j] = 1.0
    return m, sel


def host_inputs(a):
    tok = {k[len("L0_tok_"):]: v for k, v in a.items() if k.startswith("L0_tok_")}
    ffn = {k[len("L0_ffn_"):]: v for k, v in a.items() if k.startswith("L0_ffn_")}
    f32 = np.float32
    out = {
        "x": window_layout(a["x"]),
        "w0": conv0_layout(tok["conv0_w"], tok["conv0_b"]),
        "wmask": window_masks()[0],
        "rowsel": window_masks()[1],
        "n0bw": np.where(np.arange(P)[:, None] == ONE, tok["n0_b"][None, :], np.float32(0)),
        "ident": np.eye(P, dtype=f32),
        "cols": np.stack([tok[n] for n in ("conv1_b", "conv2_b", "conv3_b", "n1_w", "n1_b", "n2_w", "n2_b",
                                           "n3_w", "n3_b")], axis=1),
        "n0w": tok["n0_w"],
        "w1": tok["conv1_w"].transpose(1, 2, 0),
        "w2": tok["conv2_w"].transpose(1, 2, 0),
        "w3": tok["conv3_w"].transpose(1, 2, 0),
        "mlp_w1": tok["mlp_w1"],
        "mlp_w2": tok["mlp_w2"],
        "mlp_w3": tok["mlp_w3"].reshape(4, P).T,
        "mlp_b12": np.stack([tok["mlp_b1"].reshape(4, P).T, tok["mlp_b2"].reshape(4, P).T], axis=1),
        "mlp_b3": tok["mlp_b3"],
        "upto": np.triu(np.ones((P, P), f32)),
        "before": np.triu(np.ones((P, P), f32), 1),
        "centre": (np.eye(P) - 1.0 / P).astype(f32),
        "iota": np.broadcast_to(np.arange(TN + 1, dtype=f32), (P, TN + 1)),
        "n4": np.stack([tok["n4_w"], tok["n4_b"]], axis=1),
    }
    q, k = (a["L0_attn_" + n].reshape(2, 4 * R1, D).transpose(2, 0, 1) for n in "QK")
    out["wqk"] = np.concatenate([q, k], axis=1)
    out["vo"] = a["L0_attn_VO"].reshape(4, P, D).transpose(1, 0, 2)

    def heads(w):
        n, r, c = w.shape
        m = np.zeros((n * r, n * c), dtype=w.dtype)
        for i in range(n):
            m[i * r:(i + 1) * r, i * c:(i + 1) * c] = w[i]
        return m

    out["causal"] = np.triu(np.full((P, P), -1e30, f32), 1)
    out["hlw"] = ffn["hl_w"].transpose(2, 0, 1).reshape(D, D)
    out["hlb_col"] = ffn["hl_b"].reshape(D, 1)
    out["hlb"] = ffn["hl_b"].reshape(D)
    qk = np.zeros((D, NE + 1, P), dtype=f32)
    for n in range(NH):
        for row in (32 * n, 32 * n + DH):
            for e in range(NE):
                qk[n * DH:(n + 1) * DH, e, row:row + DH] = ffn["wq"][n, e].T
            qk[n * DH:(n + 1) * DH, NE, row:row + DH] = ffn["wk"][n].T
    out["lorow"] = np.where(np.arange(P) % 32 < DH, 0.0, -1.0).astype(f32).reshape(P, 1)
    out["ffq"] = qk
    out["ffv"] = heads(ffn["wv"].transpose(0, 2, 1))
    out["gate"] = heads(ffn["gate_w"].transpose(0, 2, 1)).reshape(2, P, NH * NE).transpose(1, 0, 2)
    out["gateb"] = ffn["gate_b"].reshape(NH * NE)
    out["lng"], out["lnb"], out["fng"], out["fnb"] = (ffn[n] for n in ("ln_g", "ln_b", "fnorm_g", "fnorm_b"))
    for n in ("fc1", "fc2"):
        out[n] = heads(np.broadcast_to(ffn[n + "_w"].T, (NH, DH, DH)))
    out["fc1b"] = np.tile(ffn["fc1_b"], NH).reshape(D, 1)
    out["fc2b"] = np.tile(ffn["fc2_b"], NH)
    out["fgate"] = ffn["fgate_w"].T
    return {k: np.ascontiguousarray(v) for k, v in out.items()}


def audio_tower(nc, d, out):
    with ExitStack() as ctx:
        marks = {}

        def sem(name):
            for engine in ("pemark", "poolmark", "spmark"):
                if name.endswith(engine):
                    if engine not in marks:
                        marks[engine] = ctx.enter_context(nc.semaphore(engine))
                    return marks[engine]
            return ctx.enter_context(nc.semaphore(name))

        tok = ctx.enter_context(nc.sbuf_tensor("tok", [P, B, TN], F32))
        area = ctx.enter_context(nc.sbuf_tensor("weights", [P, size(MLP_KEPT) + max(size(MLP_RAW), size(LATER))], F32))
        wts = Weights(area, sem)
        with ExitStack() as ph:
            feat = ph.enter_context(nc.sbuf_tensor("feat", [P, B * T], F32))
            imp = ph.enter_context(nc.sbuf_tensor("imp", [P, B], F32))
            conv_phase(nc, sem, d, wts, feat)
            mlp_phase(nc, sem, d, wts, feat, imp)
            pool_phase(nc, sem, wts, feat, imp, tok)
        with ExitStack() as ph:
            xn = ph.enter_context(nc.sbuf_tensor("xn", [P, B, TN + 1], F32))
            norm_phase(nc, sem, "n1", tok, xn)
            attn_phase(nc, sem, wts, xn, tok)
        ffn_all(nc, sem, wts, tok, out)


def kernel(**inputs):
    import numpy as _np
    import concourse.bacc as _bacc
    from concourse import mybir as _mybir
    from concourse.bass_utils import run_bass_kernel_spmd as _run

    nc = _bacc.Bacc("TRN2", target_bir_lowering=False, num_devices=1)
    arrays = host_inputs({k: _np.asarray(v) for k, v in inputs.items()})
    d = {name: nc.dram_tensor(name, a.shape, _mybir.dt.from_np(a.dtype), kind="ExternalInput").ap()
         for name, a in arrays.items()}
    out = nc.dram_tensor("out", (B, C, TN), F32, kind="ExternalOutput").ap()
    audio_tower(nc, d, out)
    r = _run(nc, [arrays], core_ids=[0])
    return r.results[0]["out"]
```
